# Optimizing a Trainium2 kernel written in Bass

```python
import numpy as np
import jax
import jax.numpy as jnp

def _softmax(x, axis=-1):
    return jax.nn.softmax(x, axis=axis)

def _gelu(x):
    return jax.nn.gelu(x, approximate=True)

def _silu(x):
    return jax.nn.silu(x)

def _sigmoid(x):
    return jax.nn.sigmoid(x)

def _layernorm(x, axis=-1, eps=1e-05):
    m = jnp.mean(x, axis=axis, keepdims=True)
    v = jnp.var(x, axis=axis, keepdims=True)
    return (x - m) / jnp.sqrt(v + eps)

def _scatter_add(tgt, idx, src, axis=0):
    return tgt.at[idx].add(src)

def _segment_sum(src, seg, n):
    return jax.ops.segment_sum(src, seg, n)
kernel_name = 'mk_cond_seq_d2_seqx_r2_fd05ed'

def setup_inputs(seed: int=0):
    np.random.seed(seed)
    _w = jnp.asarray

    def _rec_inputs():
        import jax
        import jax.numpy as jnp
        _rk = jax.random.key(seed)
        x = -0.0003929 + 0.9999 * jax.random.normal(jax.random.fold_in(_rk, 1), (2, 2048, 512), jnp.float32)
        _lenS = 2048 - jax.random.randint(jax.random.fold_in(_rk, 7), (2,), 0, max(1, 2048 // 4) + 1, jnp.int32)
        _lenS2 = 2048 - jax.random.randint(jax.random.fold_in(_rk, 8), (2,), 0, max(1, 2048 // 4) + 1, jnp.int32)
        cond_1024 = 0.00782532 + 1.00527 * jax.random.normal(jax.random.fold_in(_rk, 11), (2, 512), jnp.float32)
        return (x, cond_1024)
    x, cond_1024 = _rec_inputs()

    def _L0_cond_setup():
        import jax, jax.numpy as jnp
        import numpy as np
        B, L, D, P = (8, 1024, 512, 128)

        def _ln(x):
            m = x.mean(-1, keepdims=True)
            v = x.var(-1, keepdims=True)
            return (x - m) * jax.lax.rsqrt(v + 1e-05)

        def _s5(u, Lam_re, Lam_im, B_re, B_im, C_re, C_im, D_diag, log_step):
            Lam = Lam_re + 1j * Lam_im
            dt = jnp.exp(log_step)
            Lam_bar = jnp.exp(Lam * dt)
            Bc = B_re + 1j * B_im
            B_bar = ((Lam_bar - 1.0) / Lam)[:, None] * Bc
            Bu = jnp.einsum('bld,pd->blp', u.astype(B_bar.dtype), B_bar)
            A = jnp.broadcast_to(Lam_bar, Bu.shape)

            def binop(e1, e2):
                a1, b1 = e1
                a2, b2 = e2
                return (a1 * a2, a2 * b1 + b2)
            _, xs = jax.lax.associative_scan(binop, (A, Bu), axis=1)
            Cc = C_re + 1j * C_im
            return 2.0 * jnp.einsum('blp,dp->bld', xs, Cc).real + D_diag * u
        key = jax.random.key(seed)
        ks = jax.random.split(key, 16)
        inp = {'y': jax.random.normal(ks[0], (B, L, D), jnp.float32), 't': jax.random.normal(ks[1], (B, D), jnp.float32), 'Wm': jax.random.normal(ks[2], (D, 6 * D), jnp.float32) * 0.02, 'bm': jax.random.normal(ks[3], (6 * D,), jnp.float32) * 0.02, 'Lam_re': -0.5 * jnp.ones((P,), jnp.float32), 'Lam_im': jnp.pi * jnp.arange(P, dtype=jnp.float32), 'B_re': jax.random.normal(ks[4], (P, D), jnp.float32) / np.sqrt(D), 'B_im': jax.random.normal(ks[5], (P, D), jnp.float32) / np.sqrt(D), 'C_re': jax.random.normal(ks[6], (D, P), jnp.float32) / np.sqrt(P), 'C_im': jax.random.normal(ks[7], (D, P), jnp.float32) / np.sqrt(P), 'D_diag': jax.random.normal(ks[8], (D,), jnp.float32), 'log_step': jax.random.uniform(ks[9], (P,), jnp.float32, np.log(0.001), np.log(0.1)), 'Wc': jax.random.normal(ks[10], (D, 2 * D), jnp.float32) * 0.02, 'bc': jax.random.normal(ks[11], (2 * D,), jnp.float32) * 0.02, 'W1': jax.random.normal(ks[12], (D, 4 * D), jnp.float32) / np.sqrt(D), 'b1': jnp.zeros((4 * D,), jnp.float32), 'W2': jax.random.normal(ks[13], (4 * D, D), jnp.float32) / np.sqrt(4 * D) * 0.1, 'b2': jnp.zeros((D,), jnp.float32)}
        return inp
    _L0_cond_all = _L0_cond_setup()
    _L0_cond_in = {k: v for k, v in _L0_cond_all.items() if k in ('Wm', 'bm', 'Lam_re', 'Lam_im', 'B_re', 'B_im', 'C_re', 'C_im', 'D_diag', 'log_step', 'Wc', 'bc', 'W1', 'b1', 'W2', 'b2')}
    del _L0_cond_all

    def _L1_cond_setup():
        import jax, jax.numpy as jnp
        import numpy as np
        EPS = 1e-05

        def _sln(h, w, ln_g, ln_b, Wg, bg, Wb, bb):
            mu = jnp.mean(h, axis=-1, keepdims=True)
            var = jnp.mean((h - mu) ** 2, axis=-1, keepdims=True)
            ln = (h - mu) / jnp.sqrt(var + EPS) * ln_g + ln_b
            gamma = (w @ Wg.T + bg)[:, None, :]
            beta = (w @ Wb.T + bb)[:, None, :]
            return gamma * ln + beta
        key = jax.random.key(seed)
        ks = jax.random.split(key, 20)
        B, N, D = (4, 512, 512)
        F = 4 * D
        s = lambda fan: 1.0 / np.sqrt(fan)
        inp = {'hidden': jax.random.normal(ks[0], (B, N, D), jnp.float32), 'w': jax.random.normal(ks[1], (B, D), jnp.float32), 'ln_g': jnp.ones((D,), jnp.float32), 'ln_b': jnp.zeros((D,), jnp.float32), 'Wg': jax.random.normal(ks[2], (D, D), jnp.float32) * s(D), 'bg': jnp.zeros((D,), jnp.float32), 'Wb': jax.random.normal(ks[3], (D, D), jnp.float32) * s(D), 'bb': jnp.zeros((D,), jnp.float32), 'Wqkv': jax.random.normal(ks[4], (3 * D, D), jnp.float32) * s(D), 'bqkv': jnp.zeros((3 * D,), jnp.float32), 'Wp': jax.random.normal(ks[5], (D, D), jnp.float32) * s(D), 'bp': jnp.zeros((D,), jnp.float32), 'W1': jax.random.normal(ks[6], (F, D), jnp.float32) * s(D), 'b1': jnp.zeros((F,), jnp.float32), 'W2': jax.random.normal(ks[7], (D, F), jnp.float32) * s(F), 'b2': jnp.zeros((D,), jnp.float32), 'num_heads': 16}
        return inp
    _L1_cond_all = _L1_cond_setup()
    _L1_cond_in = {k: v for k, v in _L1_cond_all.items() if k in ('ln_g', 'ln_b', 'Wg', 'bg', 'Wb', 'bb', 'Wqkv', 'bqkv', 'Wp', 'bp', 'W1', 'b1', 'W2', 'b2')}
    del _L1_cond_all
    return {'x': x, 'cond_1024': cond_1024, 'L0_cond_Wm': _L0_cond_in['Wm'], 'L0_cond_bm': _L0_cond_in['bm'], 'L0_cond_Lam_re': _L0_cond_in['Lam_re'], 'L0_cond_Lam_im': _L0_cond_in['Lam_im'], 'L0_cond_B_re': _L0_cond_in['B_re'], 'L0_cond_B_im': _L0_cond_in['B_im'], 'L0_cond_C_re': _L0_cond_in['C_re'], 'L0_cond_C_im': _L0_cond_in['C_im'], 'L0_cond_D_diag': _L0_cond_in['D_diag'], 'L0_cond_log_step': _L0_cond_in['log_step'], 'L0_cond_Wc': _L0_cond_in['Wc'], 'L0_cond_bc': _L0_cond_in['bc'], 'L0_cond_W1': _L0_cond_in['W1'], 'L0_cond_b1': _L0_cond_in['b1'], 'L0_cond_W2': _L0_cond_in['W2'], 'L0_cond_b2': _L0_cond_in['b2'], 'L1_cond_ln_g': _L1_cond_in['ln_g'], 'L1_cond_ln_b': _L1_cond_in['ln_b'], 'L1_cond_Wg': _L1_cond_in['Wg'], 'L1_cond_bg': _L1_cond_in['bg'], 'L1_cond_Wb': _L1_cond_in['Wb'], 'L1_cond_bb': _L1_cond_in['bb'], 'L1_cond_Wqkv': _L1_cond_in['Wqkv'], 'L1_cond_bqkv': _L1_cond_in['bqkv'], 'L1_cond_Wp': _L1_cond_in['Wp'], 'L1_cond_bp': _L1_cond_in['bp'], 'L1_cond_W1': _L1_cond_in['W1'], 'L1_cond_b1': _L1_cond_in['b1'], 'L1_cond_W2': _L1_cond_in['W2'], 'L1_cond_b2': _L1_cond_in['b2']}

def reference(x, cond_1024, L0_cond_Wm, L0_cond_bm, L0_cond_Lam_re, L0_cond_Lam_im, L0_cond_B_re, L0_cond_B_im, L0_cond_C_re, L0_cond_C_im, L0_cond_D_diag, L0_cond_log_step, L0_cond_Wc, L0_cond_bc, L0_cond_W1, L0_cond_b1, L0_cond_W2, L0_cond_b2, L1_cond_ln_g, L1_cond_ln_b, L1_cond_Wg, L1_cond_bg, L1_cond_Wb, L1_cond_bb, L1_cond_Wqkv, L1_cond_bqkv, L1_cond_Wp, L1_cond_bp, L1_cond_W1, L1_cond_b1, L1_cond_W2, L1_cond_b2):
    import jax
    import jax.numpy as jnp

    def _L0_cond_ref(y, t, Wm, bm, Lam_re, Lam_im, B_re, B_im, C_re, C_im, D_diag, log_step, Wc, bc, W1, b1, W2, b2):
        import jax, jax.numpy as jnp
        import numpy as np
        B, L, D, P = (8, 1024, 512, 128)

        def _ln(x):
            m = x.mean(-1, keepdims=True)
            v = x.var(-1, keepdims=True)
            return (x - m) * jax.lax.rsqrt(v + 1e-05)

        def _s5(u, Lam_re, Lam_im, B_re, B_im, C_re, C_im, D_diag, log_step):
            Lam = Lam_re + 1j * Lam_im
            dt = jnp.exp(log_step)
            Lam_bar = jnp.exp(Lam * dt)
            Bc = B_re + 1j * B_im
            B_bar = ((Lam_bar - 1.0) / Lam)[:, None] * Bc
            Bu = jnp.einsum('bld,pd->blp', u.astype(B_bar.dtype), B_bar)
            A = jnp.broadcast_to(Lam_bar, Bu.shape)

            def binop(e1, e2):
                a1, b1 = e1
                a2, b2 = e2
                return (a1 * a2, a2 * b1 + b2)
            _, xs = jax.lax.associative_scan(binop, (A, Bu), axis=1)
            Cc = C_re + 1j * C_im
            return 2.0 * jnp.einsum('blp,dp->bld', xs, Cc).real + D_diag * u
        mod = t @ Wm + bm
        shift_a, scale_a, gate_a, shift_ff, scale_ff, gate_ff = jnp.split(mod, 6, axis=-1)
        y_mod = _ln(y) * (1 + scale_a[:, None]) + shift_a[:, None]
        a_y = _s5(y_mod, Lam_re, Lam_im, B_re, B_im, C_re, C_im, D_diag, log_step)
        y = y + gate_a[:, None] * a_y
        cond = t @ Wc + bc
        scale_c, shift_c = jnp.split(cond, 2, axis=-1)
        y_norm = _ln(y) * (1 + scale_c[:, None]) + shift_c[:, None]
        y_mod = y_norm * (1 + scale_ff[:, None]) + shift_ff[:, None]
        h = jax.nn.gelu(y_mod @ W1 + b1)
        ff_y = h @ W2 + b2
        return y + gate_ff[:, None] * ff_y

    def _L1_cond_ref(hidden, w, ln_g, ln_b, Wg, bg, Wb, bb, Wqkv, bqkv, Wp, bp, W1, b1, W2, b2, num_heads):
        import jax, jax.numpy as jnp
        import numpy as np
        EPS = 1e-05

        def _sln(h, w, ln_g, ln_b, Wg, bg, Wb, bb):
            mu = jnp.mean(h, axis=-1, keepdims=True)
            var = jnp.mean((h - mu) ** 2, axis=-1, keepdims=True)
            ln = (h - mu) / jnp.sqrt(var + EPS) * ln_g + ln_b
            gamma = (w @ Wg.T + bg)[:, None, :]
            beta = (w @ Wb.T + bb)[:, None, :]
            return gamma * ln + beta
        B, N, D = hidden.shape
        hd = D // num_heads
        h = _sln(hidden, w, ln_g, ln_b, Wg, bg, Wb, bb)
        qkv = (h @ Wqkv.T + bqkv).reshape(B, N, num_heads, hd, 3)
        q = jnp.moveaxis(qkv[..., 0], 2, 1)
        k = jnp.moveaxis(qkv[..., 1], 2, 1)
        v = jnp.moveaxis(qkv[..., 2], 2, 1)
        energy = jnp.einsum('bhqd,bhkd->bhqk', q, k)
        att = jax.nn.softmax(energy, axis=-1) / D ** 0.5
        out = jnp.einsum('bhqk,bhkd->bhqd', att, v)
        out = jnp.moveaxis(out, 1, 2).reshape(B, N, D)
        out = out @ Wp.T + bp
        h1 = out + hidden
        h2 = _sln(h1, w, ln_g, ln_b, Wg, bg, Wb, bb)
        return h2 + h1
    x = _L0_cond_ref(x, cond_1024, L0_cond_Wm, L0_cond_bm, L0_cond_Lam_re, L0_cond_Lam_im, L0_cond_B_re, L0_cond_B_im, L0_cond_C_re, L0_cond_C_im, L0_cond_D_diag, L0_cond_log_step, L0_cond_Wc, L0_cond_bc, L0_cond_W1, L0_cond_b1, L0_cond_W2, L0_cond_b2)
    x = _L1_cond_ref(x, cond_1024, L1_cond_ln_g, L1_cond_ln_b, L1_cond_Wg, L1_cond_bg, L1_cond_Wb, L1_cond_bb, L1_cond_Wqkv, L1_cond_bqkv, L1_cond_Wp, L1_cond_bp, L1_cond_W1, L1_cond_b1, L1_cond_W2, L1_cond_b2, 16)
    return x

_drawn_inputs = setup_inputs


def setup_inputs(seed=0):
    import zlib

    import numpy as np

    out = dict(_drawn_inputs(seed))
    spreads = {'L0_cond_Lam_re': (-0.5, 0.6),
     'L0_cond_b1': (0.0, 2.0),
     'L0_cond_b2': (0.0, 0.1),
     'L1_cond_ln_g': (1.0, 0.2),
     'L1_cond_ln_b': (0.0, 0.1),
     'L1_cond_bg': (0.0, 0.1),
     'L1_cond_bb': (0.0, 0.1),
     'L1_cond_bqkv': (0.0, 0.8),
     'L1_cond_bp': (0.0, 0.1),
     'L1_cond_b1': (0.0, 0.1),
     'L1_cond_b2': (0.0, 0.1)}
    factors = {'L0_cond_Wc': 3.527, 'L0_cond_bc': 64.0}
    for name, (base, spread) in spreads.items():
        noise = np.random.default_rng([zlib.crc32(name.encode()), seed]).standard_normal(out[name].shape)
        drawn = base * np.exp(spread * noise) if base else spread * noise
        out[name] = jnp.asarray(drawn.astype(out[name].dtype))
    for name, factor in factors.items():
        out[name] = (out[name] * factor).astype(out[name].dtype)
    return out
```

```python
import concourse.bass as bass
from concourse import mybir
from contextlib import ExitStack

B, L, D = 2, 2048, 512
P = 128
KT = D // P
FF = 2048
FT = FF // P
HEADS, HD = 16, 32
HG = P // HD
NG = HEADS // HG
CH = 512
NCH = L // CH
TT = CH // P
EPS = 1e-5

F32 = mybir.dt.float32
F32R = mybir.dt.float32r
I32 = mybir.dt.int32
ALU = mybir.AluOpType
ACT = mybir.ActivationFunctionType
AX = mybir.AxisListType

V_GAIN_A, V_SHIFT_A, V_GAIN_F, V_SHIFT_F, V_GAIN_1, V_SHIFT_1, V_GATE_A, V_GATE_F = range(8)
NV, NVC = 8, 6



def split_matmuls(nc, out, w_hi, w_lo, x_hi, x_lo, first, last):
    nc.tensor.matmul(out, w_hi, x_hi, start=first, stop=False)
    nc.tensor.matmul(out, w_lo, x_hi, start=False, stop=False)
    return nc.tensor.matmul(out, w_hi, x_lo, start=False, stop=last)


MOMENT_STEPS, INVERSE_STEPS = TT + 6, 6


def ln_moments(dve, x, stats, mean2, var, diff, stat, at):
    for t in range(TT):
        dve.bn_stats(stats[:, t, :], x[:, t, :]).then_inc(stat, 1)
    dve.wait_ge(stat, at + TT)
    dve.tensor_tensor(mean2[:, :], stats[:, :, 1], stats[:, :, 4], ALU.add).then_inc(stat, 1)
    dve.tensor_tensor(diff[:, :], stats[:, :, 1], stats[:, :, 4], ALU.subtract).then_inc(stat, 1)
    dve.tensor_tensor(var[:, :], stats[:, :, 2], stats[:, :, 5], ALU.add).then_inc(stat, 1)
    dve.wait_ge(stat, at + TT + 2)
    dve.scalar_tensor_tensor(out=diff[:, :], in0=diff[:, :], scalar=0.25, in1=diff[:, :], op0=ALU.mult, op1=ALU.mult).then_inc(stat, 1)
    dve.wait_ge(stat, at + TT + 3)
    dve.tensor_scalar(var[:, :], var[:, :], 1.0 / D, EPS, ALU.mult, ALU.add).then_inc(stat, 1)
    dve.wait_ge(stat, at + TT + 5)
    dve.tensor_tensor(var[:, :], var[:, :], diff[:, :], ALU.add).then_inc(stat, 1)


def ln_inverse(dve, root, mean2, var, inv, off, chain, at):
    dve.reciprocal(inv[:, :], root[:, :]).then_inc(chain, 1)
    dve.wait_ge(chain, at + 1)
    dve.tensor_tensor(off[:, :], inv[:, :], inv[:, :], ALU.mult).then_inc(chain, 1)
    dve.wait_ge(chain, at + 2)
    dve.tensor_tensor(off[:, :], off[:, :], var[:, :], ALU.mult).then_inc(chain, 1)
    dve.wait_ge(chain, at + 3)
    dve.tensor_scalar(off[:, :], off[:, :], -0.5, 1.5, ALU.mult, ALU.add).then_inc(chain, 1)
    dve.wait_ge(chain, at + 4)
    dve.tensor_tensor(inv[:, :], inv[:, :], off[:, :], ALU.mult).then_inc(chain, 1)
    dve.wait_ge(chain, at + 5)
    dve.scalar_tensor_tensor(out=off[:, :], in0=mean2[:, :], scalar=-0.5, in1=inv[:, :], op0=ALU.mult, op1=ALU.mult).then_inc(chain, 1)


def prep_stage(nc, sb, sem, psum, a, ident, columns, s5, vec_dram):
    wm = sb("wm", [P, KT, 6 * D])
    wc = sb("wc", [P, KT, 2 * D])
    wgb = sb("wgb", [P, 2, KT, D])
    wgb_t = sb("wgb_t", [P, 2, KT, D])
    cond = sb("cond", [B, D])
    cond_t = sb("cond_t", [P, KT, B])
    bias = sb("bias", [B, 10, D])
    ln_gb = sb("ln_gb", [B, 2, D])
    mod = sb("mod", [B, 10, D])
    vec = sb("vec", [B, NV, D])
    d_rows = sb("d_rows", [KT, P])
    d_col = sb("d_col", [P, KT])
    lam = sb("lam", [P, 3])
    b_in = sb("b_in", [P, 2, D])
    c_in = sb("c_in", [P, 2, KT, P])
    b_bar = sb("b_bar", [P, 2, D])
    tmp = sb("prep_tmp", [P, D])
    scr = sb("prep_scr", [P, 64])
    pow2 = sb("prep_pow2", [P, 1], I32)

    ld_ssm, ld_row, ld_wm, ld_wc, ld_wgb = (sem(f"prep_ld_{n}") for n in ("ssm", "row", "wm", "wc", "wgb"))
    ident_zero, ident_ready = sem("ident_zero"), sem("ident_ready")
    cond_tp, cond_ready = sem("cond_tp"), sem("cond_ready")
    sec_ready, sec_read = sem("sec_ready"), sem("sec_read")
    gb_tp, gb_ready = sem("gb_tp"), sem("gb_ready")
    d_tp, d_ready = sem("d_tp"), sem("d_ready")
    chain = sem("prep_chain")
    bbar_ready, bc_tp, bc_hi, bc_lo = sem("bbar_ready"), sem("bc_tp"), sem("bc_hi"), sem("bc_lo")
    vec_ready, col_tp, col_ready = sem("vec_ready"), sem("col_tp"), sem("col_ready")
    vec_stored = sem("vec_stored")

    def rows(v, n):
        return v.rearrange("(o n d) -> o n d", o=1, n=n)

    with nc.Block() as block:
        @block.sync
        def _(sp):
            for n, name in enumerate(("Lam_re", "Lam_im", "log_step")):
                sp.dma_start(lam[:, n:n + 1], a["L0_cond_" + name].rearrange("(p o) -> p o", o=1)).then_inc(ld_ssm, 16)
            for n, name in enumerate(("B_re", "B_im")):
                sp.dma_start(b_in[:, n, :], a["L0_cond_" + name]).then_inc(ld_ssm, 16)
            for n, name in enumerate(("C_re", "C_im")):
                sp.dma_start(c_in[:, n], a["L0_cond_" + name].rearrange("(k d) p -> d k p", d=P)).then_inc(ld_ssm, 16)
            sp.dma_start(d_rows[:, :], a["L0_cond_D_diag"].rearrange("(k p) -> k p", p=P)).then_inc(ld_ssm, 16)
            sp.dma_start(cond[:, :], a["cond_1024"]).then_inc(ld_row, 16)
            for b in range(B):
                for at, n, name in ((0, 6, "L0_cond_bm"), (6, 2, "L0_cond_bc"), (8, 1, "L1_cond_bg"), (9, 1, "L1_cond_bb")):
                    sp.dma_start(bias[b:b + 1, at:at + n, :], rows(a[name], n)).then_inc(ld_row, 16)
                for at, name in enumerate(("L1_cond_ln_g", "L1_cond_ln_b")):
                    sp.dma_start(ln_gb[b:b + 1, at:at + 1, :], rows(a[name], 1)).then_inc(ld_row, 16)
            sp.dma_start(wm[:, :, :], a["L0_cond_Wm"].rearrange("(k p) n -> p k n", p=P)).then_inc(ld_wm, 16)
            sp.dma_start(wc[:, :, :], a["L0_cond_Wc"].rearrange("(k p) n -> p k n", p=P)).then_inc(ld_wc, 16)
            for n, name in enumerate(("Wg", "Wb")):
                sp.dma_start(wgb[:, n], a["L1_cond_" + name].rearrange("(m p) k -> p m k", p=P)).then_inc(ld_wgb, 16)
            sp.wait_ge(vec_ready, 1)
            sp.dma_start(vec_dram.rearrange("v b d -> b v d"), vec[:, :, :]).then_inc(vec_stored, 16)
            sp.wait_ge(vec_stored, 16)

        @block.gpsimd
        def _(pool):
            pool.memset(ident[:, :], 0.0).then_inc(ident_zero, 1)
            pool.wait_ge(ident_zero, 1)
            pool.affine_select(out=ident[:, :], in_=ident[:, :], compare_op=ALU.not_equal, fill=1.0, base=0,
                               pattern=[[-1, P]], channel_multiplier=1).then_inc(ident_ready, 1)

        @block.tensor
        def _(pe):
            pe.wait_ge(ident_ready, 1)
            pe.wait_ge(ld_ssm, 16 * 8)
            pe.transpose(psum[:, 7, 0:KT], d_rows[:, :], ident[0:KT, 0:KT]).then_inc(d_tp, 1)
            for n in range(2):
                for k in range(KT):
                    mm = pe.transpose(psum[:, n, k * P:(k + 1) * P], c_in[:, n, k, :], ident[:, :])
                mm.then_inc(bc_tp, 1)
            pe.wait_ge(ld_row, 16 * (1 + 6 * B))
            for k in range(KT):
                mm = pe.transpose(psum[:, 6, k * B:(k + 1) * B], cond[:, k * P:(k + 1) * P], ident[0:B, 0:B])
            mm.then_inc(cond_tp, 1)
            pe.wait_ge(bbar_ready, 1)
            for n in range(2):
                for k in range(KT):
                    mm = pe.transpose(psum[:, 2 + n, k * P:(k + 1) * P], b_bar[:, n, k * P:(k + 1) * P], ident[:, :])
                mm.then_inc(bc_tp, 1)
            pe.wait_ge(cond_ready, 1)
            for n in range(10):
                if n == 0:
                    pe.wait_ge(ld_wm, 16)
                if n == 6:
                    pe.wait_ge(ld_wc, 16)
                if n == 8:
                    pe.wait_ge(ld_wgb, 32)
                    pe.wait_ge(bc_hi, 4)
                    pe.wait_ge(bc_lo, 4)
                    for j in range(2 * KT):
                        if j >= 4:
                            pe.wait_ge(gb_ready, j - 3)
                        for m in range(KT):
                            mm = pe.transpose(psum[:, j % 4, m * P:(m + 1) * P],
                                              wgb[:, j // KT, m, (j % KT) * P:(j % KT + 1) * P], ident[:, :])
                        mm.then_inc(gb_tp, 1)
                    pe.wait_ge(gb_ready, 2 * KT)
                if n >= 2:
                    pe.wait_ge(sec_read, n - 1)
                for k in range(KT):
                    w = wm[:, k, n * D:(n + 1) * D] if n < 6 else (
                        wc[:, k, (n - 6) * D:(n - 5) * D] if n < 8 else wgb_t[:, n - 8, k, :])
                    mm = pe.matmul(psum[0:B, 4 + n % 2, :], cond_t[:, k, :], w, start=(k == 0), stop=(k == KT - 1))
                mm.then_inc(sec_ready, 1)
            pe.wait_ge(vec_ready, 1)
            for v in range(NVC):
                for k in range(KT):
                    at = (v * KT + k) * B
                    mm = pe.transpose(psum[:, 6, at:at + B], vec[:, v, k * P:(k + 1) * P], ident[0:B, 0:B])
            mm.then_inc(col_tp, 1)

        @block.scalar
        def _(act):
            for n, times in enumerate((2.0, -2.0)):
                act.wait_ge(bc_tp, n + 1)
                act.activation(s5["c_hi"][:, n, :], psum[:, n, :], ACT.Copy, scale=times).then_inc(bc_hi, 1)
            act.wait_ge(cond_tp, 1)
            act.activation(cond_t[:, :, :], psum[:, 6, 0:KT * B].rearrange("p (k b) -> p k b", b=B), ACT.Copy).then_inc(cond_ready, 1)
            for n in range(2):
                act.wait_ge(bc_tp, 3 + n)
                act.activation(s5["b_hi"][:, :, n * P:(n + 1) * P], psum[:, 2 + n, :].rearrange("p (k s) -> p k s", s=P),
                               ACT.Copy).then_inc(bc_hi, 1)
            for j in range(2 * KT):
                act.wait_ge(gb_tp, j + 1)
                act.activation(wgb_t[:, j // KT, j % KT, :], psum[:, j % 4, :], ACT.Copy).then_inc(gb_ready, 1)
            act.wait_ge(col_tp, 1)
            act.activation(columns[:, :, :, :], psum[:, 6, 0:NVC * KT * B].rearrange("p (v k b) -> p v k b", k=KT, b=B),
                           ACT.Copy).then_inc(col_ready, 1)

        @block.vector
        def _(dve):
            done = [0]

            def link(instruction):
                done[0] += 1
                instruction.then_inc(chain, 1)
                dve.wait_ge(chain, done[0])

            used = [0]

            def col():
                used[0] += 1
                return scr[:, used[0] - 1:used[0]]

            def polynomial(out, y, coefficients):
                top, following, *rest = coefficients[::-1]
                link(dve.tensor_scalar(out, y, top, following, ALU.mult, ALU.add))
                for c in rest:
                    link(dve.tensor_scalar(out, out, y, c, ALU.mult, ALU.add))

            MAGIC = 1.5 * 2 ** 23

            def exponential(out, x):
                n, f, p = col(), col(), col()
                link(dve.tensor_scalar(f, x, 88.0, -87.0, ALU.min, ALU.max))
                link(dve.tensor_scalar(n, f, 1.4426950408889634, MAGIC, ALU.mult, ALU.add))
                link(dve.tensor_scalar(n, n, MAGIC, None, ALU.subtract))
                for part in (0.693359375, -2.12194440e-4):
                    link(dve.scalar_tensor_tensor(out=f, in0=n, scalar=-part, in1=f, op0=ALU.mult, op1=ALU.add))
                polynomial(p, f, [1.0, 1.0, 1 / 2, 1 / 6, 1 / 24, 1 / 120, 1 / 720, 1 / 5040, 1 / 40320])
                link(dve.tensor_scalar(pow2[:, :], n, 127.0, float(2 ** 23), ALU.add, ALU.mult))
                link(dve.tensor_tensor(out, p, pow2[:, :].bitcast(F32), ALU.mult))

            def sine_cosine(sine, cosine, x):
                n, f, y, s, c, j, q, t = (col() for _ in range(8))
                link(dve.tensor_scalar(n, x, 0.6366197723675814, MAGIC, ALU.mult, ALU.add))
                link(dve.tensor_scalar(n, n, MAGIC, None, ALU.subtract))
                link(dve.scalar_tensor_tensor(out=f, in0=n, scalar=-1.5703125, in1=x, op0=ALU.mult, op1=ALU.add))
                for part in (4.837512969970703125e-4, 7.54978995489188216e-8):
                    link(dve.scalar_tensor_tensor(out=f, in0=n, scalar=-part, in1=f, op0=ALU.mult, op1=ALU.add))
                link(dve.tensor_tensor(y, f, f, ALU.mult))
                polynomial(s, y, [1.0, -1 / 6, 1 / 120, -1 / 5040, 1 / 362880])
                link(dve.tensor_tensor(s, s, f, ALU.mult))
                polynomial(c, y, [1.0, -1 / 2, 1 / 24, -1 / 720, 1 / 40320, -1 / 3628800])
                link(dve.tensor_scalar(j, n, 0.25, MAGIC, ALU.mult, ALU.add))
                link(dve.tensor_scalar(j, j, MAGIC, None, ALU.subtract))
                link(dve.scalar_tensor_tensor(out=j, in0=j, scalar=-4.0, in1=n, op0=ALU.mult, op1=ALU.add))
                link(dve.scalar_tensor_tensor(out=t, in0=j, scalar=-1.0, in1=j, op0=ALU.mult, op1=ALU.max))
                link(dve.tensor_scalar(t, t, -1.0, 2.0, ALU.mult, ALU.add))
                link(dve.tensor_tensor(t, t, j, ALU.mult))
                link(dve.tensor_tensor(q, j, j, ALU.mult))
                link(dve.tensor_scalar(q, q, -1.0, 1.0, ALU.mult, ALU.add))
                link(dve.tensor_scalar(q, q, -1.0, None, ALU.max))
                link(dve.tensor_tensor(sine, c, t, ALU.mult))
                link(dve.scalar_tensor_tensor(out=sine, in0=s, scalar=q, in1=sine, op0=ALU.mult, op1=ALU.add))
                link(dve.tensor_tensor(cosine, s, t, ALU.mult))
                link(dve.scalar_tensor_tensor(out=cosine, in0=c, scalar=q, in1=cosine, op0=ALU.mult, op1=ALU.subtract))

            cos, sin, decay = s5["cos"], s5["sin"], s5["decay"]
            dve.wait_ge(ld_ssm, 16 * 8)
            dt, x, r, l_re, l_im, c_re, c_im, mag, u, w = (col() for _ in range(10))
            lr, li = lam[:, 0:1], lam[:, 1:2]
            exponential(dt, lam[:, 2:3])
            link(dve.tensor_tensor(x, lr, dt, ALU.mult))
            exponential(r, x)
            link(dve.tensor_tensor(x, li, dt, ALU.mult))
            sine_cosine(sin[:, 0:1], cos[:, 0:1], x)
            link(dve.tensor_tensor(l_re, r, cos[:, 0:1], ALU.mult))
            link(dve.tensor_tensor(l_im, r, sin[:, 0:1], ALU.mult))
            link(dve.tensor_scalar(l_re, l_re, 1.0, None, ALU.subtract))
            link(dve.tensor_tensor(mag, lr, lr, ALU.mult))
            link(dve.scalar_tensor_tensor(out=mag, in0=li, scalar=li, in1=mag, op0=ALU.mult, op1=ALU.add))
            link(dve.reciprocal(mag, mag))
            link(dve.tensor_tensor(u, l_im, li, ALU.mult))
            link(dve.scalar_tensor_tensor(out=u, in0=l_re, scalar=lr, in1=u, op0=ALU.mult, op1=ALU.add))
            link(dve.tensor_tensor(c_re, u, mag, ALU.mult))
            link(dve.tensor_tensor(w, l_re, li, ALU.mult))
            link(dve.scalar_tensor_tensor(out=w, in0=l_im, scalar=lr, in1=w, op0=ALU.mult, op1=ALU.subtract))
            link(dve.tensor_tensor(c_im, w, mag, ALU.mult))
            link(dve.tensor_scalar(tmp[:, :], b_in[:, 1, :], c_im, None, ALU.mult))
            link(dve.scalar_tensor_tensor(out=b_bar[:, 0, :], in0=b_in[:, 0, :], scalar=c_re, in1=tmp[:, :], op0=ALU.mult, op1=ALU.subtract))
            link(dve.tensor_scalar(tmp[:, :], b_in[:, 0, :], c_im, None, ALU.mult))
            dve.scalar_tensor_tensor(out=b_bar[:, 1, :], in0=b_in[:, 1, :], scalar=c_re, in1=tmp[:, :], op0=ALU.mult, op1=ALU.add).then_inc(bbar_ready, 1)
            dve.wait_ge(d_tp, 1)
            link(dve.tensor_copy(d_col[:, :], psum[:, 7, 0:KT]))
            dve.wait_ge(ident_ready, 1)
            for k in range(KT):
                link(dve.tensor_scalar(s5["d_hi"][:, k, :], ident[:, :], d_col[:, k:k + 1], None, ALU.mult))
                dve.scalar_tensor_tensor(out=s5["d_lo"][:, k, :], in0=ident[:, :], scalar=d_col[:, k:k + 1],
                                         in1=s5["d_hi"][:, k, :].bitcast(F32), op0=ALU.mult, op1=ALU.subtract).then_inc(d_ready, 1)
            for n, times in enumerate((2.0, -2.0)):
                dve.wait_ge(bc_hi, n + 1)
                dve.scalar_tensor_tensor(out=s5["c_lo"][:, n, :], in0=psum[:, n, :], scalar=times, in1=s5["c_hi"][:, n, :].bitcast(F32),
                                         op0=ALU.mult, op1=ALU.subtract).then_inc(bc_lo, 1)
            for n in range(2):
                dve.wait_ge(bc_hi, 3 + n)
                dve.tensor_tensor(s5["b_lo"][:, :, n * P:(n + 1) * P], psum[:, 2 + n, :].rearrange("p (k s) -> p k s", s=P),
                                  s5["b_hi"][:, :, n * P:(n + 1) * P].bitcast(F32), ALU.subtract).then_inc(bc_lo, 1)
            dve.memset(decay[:, :], 1.0).then_inc(chain, 1)
            done[0] += 1
            dve.wait_ge(chain, done[0])
            link(dve.tensor_scalar(decay[:, :], decay[:, :], r, None, ALU.mult))
            s = 1
            while s < CH:
                w_re, w_im = cos[:, s - 1:s], sin[:, s - 1:s]
                link(dve.tensor_scalar(tmp[:, 0:s], sin[:, 0:s], w_im, None, ALU.mult))
                link(dve.scalar_tensor_tensor(out=cos[:, s:2 * s], in0=cos[:, 0:s], scalar=w_re, in1=tmp[:, 0:s], op0=ALU.mult, op1=ALU.subtract))
                link(dve.tensor_scalar(tmp[:, 0:s], sin[:, 0:s], w_re, None, ALU.mult))
                link(dve.scalar_tensor_tensor(out=sin[:, s:2 * s], in0=cos[:, 0:s], scalar=w_im, in1=tmp[:, 0:s], op0=ALU.mult, op1=ALU.add))
                s *= 2
            dve.wait_ge(ld_row, 16 * (1 + 6 * B))
            for n in range(10):
                dve.wait_ge(sec_ready, n + 1)
                dve.tensor_tensor(mod[:, n, :], psum[0:B, 4 + n % 2, :], bias[:, n, :], ALU.add).then_inc(sec_read, 1)
            dve.wait_ge(sec_read, 10)
            shift_a, scale_a, gate_a, shift_f, scale_f, gate_f, scale_c, shift_c, gamma, beta = (mod[:, n, :] for n in range(10))
            link(dve.tensor_scalar(vec[:, V_GAIN_A, :], scale_a, 1.0, None, ALU.add))
            link(dve.tensor_copy(vec[:, V_SHIFT_A, :], shift_a))
            link(dve.tensor_scalar(scale_f, scale_f, 1.0, None, ALU.add))
            link(dve.scalar_tensor_tensor(out=vec[:, V_GAIN_F, :], in0=scale_c, scalar=1.0, in1=scale_f, op0=ALU.add, op1=ALU.mult))
            link(dve.tensor_tensor(shift_c, shift_c, scale_f, ALU.mult))
            link(dve.tensor_tensor(vec[:, V_SHIFT_F, :], shift_c, shift_f, ALU.add))
            link(dve.tensor_tensor(vec[:, V_GAIN_1, :], gamma, ln_gb[:, 0, :], ALU.mult))
            link(dve.tensor_tensor(gamma, gamma, ln_gb[:, 1, :], ALU.mult))
            link(dve.tensor_tensor(vec[:, V_SHIFT_1, :], gamma, beta, ALU.add))
            link(dve.tensor_copy(vec[:, V_GATE_A, :], gate_a))
            dve.tensor_copy(vec[:, V_GATE_F, :], gate_f).then_inc(vec_ready, 1)


def s5_stage(nc, sb, sem, psum, a, ident, columns, s5, vec_dram, y_dram):
    x = [sb(f"x{b}", [P, TT, D]) for b in range(B)]
    y = [sb(f"y{b}", [P, TT, D]) for b in range(B)]
    norm = sb("norm", [P, TT, D])
    gate = [sb(f"gate{b}", [P, D]) for b in range(B)]
    stats = sb("stats", [P, TT, 6])
    root, inv, off, mean2, var, diff = (sb(f"ln_{n}", [P, TT]) for n in ("root", "inv", "off", "mean2", "var", "diff"))
    u = [sb(f"u{n}", [P, CH]) for n in range(2)]
    u_hi = [sb(f"u_hi{b}", [P, KT, CH], F32R) for b in range(B)]
    u_lo = [sb(f"u_lo{b}", [P, KT, CH], F32R) for b in range(B)]
    prod = sb("prod", [P, 4, CH])
    turned = sb("turned", [P, 2, CH])
    scan = sb("scan", [P, 2, CH])
    state = [sb(f"state{b}", [P, 2, CH]) for b in range(B)]
    s_hi = sb("s_hi", [P, 2, CH], F32R)
    s_lo = sb("s_lo", [P, 2, CH], F32R)
    gated = [sb(f"gated{n}", [P, D]) for n in range(2)]

    x_ld = [sem(f"s5_x_ld{b}") for b in range(B)]
    y_st = [sem(f"s5_y_st{b}") for b in range(B)]
    gate_ld, start = sem("s5_gate_ld"), sem("s5_start")
    stat, root_ready, ln_chain, norm_ready = sem("s5_stat"), sem("s5_root"), sem("s5_ln_chain"), sem("s5_norm")
    tr_ready, uhi_ready, u_ready, ulo_ready = sem("s5_tr"), sem("s5_uhi"), sem("s5_u"), sem("s5_ulo")
    bu_ready, prod_ready, turned_ready, scan_ready = sem("s5_bu"), sem("s5_prod"), sem("s5_turned"), sem("s5_scan")
    back_ready, state_ready, shi_ready, slo_ready = sem("s5_back"), sem("s5_state"), sem("s5_shi"), sem("s5_slo")
    cy_ready, gated_ready, y_ready = sem("s5_cy"), sem("s5_gated"), sem("s5_y")

    cos, sin, decay = s5["cos"], s5["sin"], s5["decay"]
    TR, BU, CY = 0, 2, 6

    def chunk(dram, i, b):
        return dram[b].rearrange("(i t p) d -> i p t d", p=P, t=TT)[bass.ds(i, 1)].rearrange("o p t d -> (o p) t d")

    def steps(engine, body):
        front, back = body
        front(0, 0)
        with engine.Fori(0, NCH - 1) as i:
            front(i, 1)
            back(i, 0)
            front(i + 1, 0)
            back(i, 1)
        front(NCH - 1, 1)
        back(NCH - 1, 0)
        back(NCH - 1, 1)

    with nc.Block() as block:
        @block.sync
        def _(sp):
            for b in range(B):
                sp.dma_start(x[b][:, :, :], chunk(a["x"], 0, b)).then_inc(x_ld[b], 16)
            for b in range(B):
                sp.dma_start(gate[b][:, :], vec_dram[V_GATE_A, b:b + 1, :].broadcast_to((P, D))).then_inc(gate_ld, 16)

            def store(i, b):
                sp.wait_ge(y_ready, TT * (2 * i + b + 1))
                sp.dma_start(chunk(y_dram, i, b), y[b][:, :, :]).then_inc(y_st[b], 16)

            with sp.Fori(0, NCH - 1) as i:
                for b in range(B):
                    store(i, b)
                    sp.dma_start(x[b][:, :, :], chunk(a["x"], i + 1, b)).then_inc(x_ld[b], 16)
            for b in range(B):
                store(NCH - 1, b)
            for b in range(B):
                sp.wait_ge(y_st[b], 16 * NCH)

        @block.tensor
        def _(pe):
            def front(i, b):
                c = 2 * i + b
                pe.wait_ge(norm_ready, c + 1)
                for k in range(KT):
                    pe.wait_ge(u_ready, KT * c + k + 1)
                    for t in range(TT):
                        mm = pe.transpose(psum[:, TR + k % 2, t * P:(t + 1) * P], norm[:, t, k * P:(k + 1) * P], ident[:, :])
                    mm.then_inc(tr_ready, 1)
                pe.wait_ge(uhi_ready, KT * (c + 1))
                pe.wait_ge(ulo_ready, KT * (c + 1) + 2)
                pe.wait_ge(prod_ready, 4 * (c + 1))
                for n in range(2):
                    for k in range(KT):
                        mm = split_matmuls(nc, psum[:, BU + 2 * b + n, :], s5["b_hi"][:, k, n * P:(n + 1) * P],
                                           s5["b_lo"][:, k, n * P:(n + 1) * P], u_hi[b][:, k, :], u_lo[b][:, k, :], k == 0, k == KT - 1)
                mm.then_inc(bu_ready, 1)

            def back(i, b):
                c = 2 * i + b
                pe.wait_ge(shi_ready, c + 1)
                pe.wait_ge(slo_ready, c + 1)
                for t in range(TT):
                    pe.wait_ge(gated_ready, TT * c + t + 1)
                    tok = slice(t * P, (t + 1) * P)
                    out = psum[:, CY + t % 2, :]
                    for n in range(2):
                        split_matmuls(nc, out, s_hi[:, n, tok], s_lo[:, n, tok], s5["c_hi"][:, n, :], s5["c_lo"][:, n, :], n == 0, False)
                    for k in range(KT):
                        mm = split_matmuls(nc, out[:, k * P:(k + 1) * P], u_hi[b][:, k, tok], u_lo[b][:, k, tok],
                                           s5["d_hi"][:, k, :], s5["d_lo"][:, k, :], False, k == KT - 1)
                    mm.then_inc(cy_ready, 1)

            steps(pe, (front, back))

        @block.scalar
        def _(act):
            act.sem_inc(u_ready, 2)

            def front(i, b):
                c = 2 * i + b
                act.wait_ge(stat, MOMENT_STEPS * (c + 1))
                act.activation(root[:, :], var[:, :], ACT.Sqrt).then_inc(root_ready, 1)
                for k in range(KT):
                    act.wait_ge(tr_ready, KT * c + k + 1)
                    act.wait_ge(ulo_ready, KT * c + k + 1)
                    act.activation(u[k % 2][:, :], psum[:, TR + k % 2, :], ACT.Identity, scale=columns[:, V_GAIN_A, k, b:b + 1],
                                   bias=columns[:, V_SHIFT_A, k, b:b + 1]).then_inc(u_ready, 1)

            def back(i, b):
                c = 2 * i + b
                act.wait_ge(state_ready, 2 * (c + 1))
                act.wait_ge(cy_ready, TT * c)
                act.activation(s_hi[:, :, :], state[b][:, :, :], ACT.Copy).then_inc(shi_ready, 1)

            steps(act, (front, back))

        @block.vector
        def _(dve):
            dve.sem_inc(prod_ready, 8)
            dve.sem_inc(gated_ready, 2)
            for b in range(B):
                dve.memset(state[b][:, :, CH - 1:CH], 0.0).then_inc(start, 1)
            dve.wait_ge(start, B)
            dve.wait_ge(gate_ld, 16 * B)

            def front(i, b):
                c = 2 * i + b
                dve.wait_ge(x_ld[b], 16 * (i + 1))
                ln_moments(dve, x[b], stats, mean2, var, diff, stat, MOMENT_STEPS * c)
                dve.wait_ge(root_ready, c + 1)
                ln_inverse(dve, root, mean2, var, inv, off, ln_chain, INVERSE_STEPS * c)
                dve.wait_ge(ln_chain, INVERSE_STEPS * (c + 1))
                dve.wait_ge(tr_ready, KT * c)
                for t in range(TT):
                    nrm = dve.tensor_scalar(norm[:, t, :], x[b][:, t, :], inv[:, t:t + 1], off[:, t:t + 1], ALU.mult, ALU.add)
                nrm.then_inc(norm_ready, 1)
                for k in range(KT):
                    dve.wait_ge(u_ready, KT * c + k + 3)
                    dve.tensor_copy(u_hi[b][:, k, :], u[k % 2][:, :]).then_inc(uhi_ready, 1)

            def back(i, b):
                c = 2 * i + b
                re, im = psum[:, BU + 2 * b, :], psum[:, BU + 2 * b + 1, :]
                dve.wait_ge(bu_ready, c + 1)
                dve.wait_ge(state_ready, 2 * c)
                for n, (v, table) in enumerate(((re, cos), (im, sin), (im, cos), (re, sin))):
                    dve.tensor_tensor(prod[:, n, :], v, table[:, :], ALU.mult).then_inc(prod_ready, 1)
                for n in range(2):
                    dve.wait_ge(turned_ready, 2 * c + n + 1)
                    dve.wait_ge(back_ready, 4 * c)
                    dve.tensor_tensor_scan(scan[:, n, :], decay[:, :], turned[:, n, :], state[b][:, n, CH - 1:CH],
                                           ALU.mult, ALU.add).then_inc(scan_ready, 1)
                dve.wait_ge(scan_ready, 2 * (c + 1))
                for n, (v, table) in enumerate(((0, cos), (1, sin), (1, cos), (0, sin))):
                    dve.tensor_tensor(prod[:, n, :], scan[:, v, :], table[:, :], ALU.mult).then_inc(back_ready, 1)
                for t in range(TT):
                    dve.wait_ge(cy_ready, TT * c + t + 1)
                    dve.wait_ge(y_ready, TT * c + max(t - 1, 0))
                    dve.tensor_tensor(gated[t % 2][:, :], psum[:, CY + t % 2, :], gate[b][:, :], ALU.mult).then_inc(gated_ready, 1)

            steps(dve, (front, back))

        @block.gpsimd
        def _(pool):
            pool.sem_inc(ulo_ready, 2)

            def front(i, b):
                c = 2 * i + b
                for k in range(KT):
                    pool.wait_ge(uhi_ready, KT * c + k + 1)
                    pool.tensor_tensor(u_lo[b][:, k, :], u[k % 2][:, :], u_hi[b][:, k, :].bitcast(F32), ALU.subtract).then_inc(ulo_ready, 1)

            def back(i, b):
                c = 2 * i + b
                for n, op in enumerate((ALU.add, ALU.subtract)):
                    pool.wait_ge(prod_ready, 4 * c + 2 * n + 10)
                    pool.wait_ge(scan_ready, 2 * c)
                    pool.tensor_tensor(turned[:, n, :], prod[:, 2 * n, :], prod[:, 2 * n + 1, :], op).then_inc(turned_ready, 1)
                for n, op in enumerate((ALU.subtract, ALU.add)):
                    pool.wait_ge(back_ready, 4 * c + 2 * n + 2)
                    pool.wait_ge(shi_ready, c)
                    pool.tensor_tensor(state[b][:, n, :], prod[:, 2 * n, :], prod[:, 2 * n + 1, :], op).then_inc(state_ready, 1)
                pool.wait_ge(shi_ready, c + 1)
                pool.tensor_tensor(s_lo[:, :, :], state[b][:, :, :], s_hi[:, :, :].bitcast(F32), ALU.subtract).then_inc(slo_ready, 1)
                pool.wait_ge(y_st[b], 16 * i)
                for t in range(TT):
                    pool.wait_ge(gated_ready, TT * c + t + 3)
                    pool.tensor_tensor(y[b][:, t, :], gated[t % 2][:, :], x[b][:, t, :], ALU.add).then_inc(y_ready, 1)

            steps(pool, (front, back))




def ffn_stage(nc, sb, sem, psum, a, ident, columns, vec_dram, y_dram, z_dram):
    w1_hi, w1_lo = (sb(f"w1_{n}", [P, KT, FF], F32R) for n in ("hi", "lo"))
    w2_hi, w2_lo = (sb(f"w2_{n}", [P, FT, D], F32R) for n in ("hi", "lo"))
    y = [sb(f"ffn_y{b}", [P, TT, D]) for b in range(B)]
    norm = sb("ffn_norm", [P, TT, D])
    gate = [sb(f"ffn_gate{b}", [P, D]) for b in range(B)]
    stats = sb("ffn_stats", [P, TT, 6])
    root, inv, off, mean2, var, diff = (sb(f"ffn_ln_{n}", [P, TT]) for n in ("root", "inv", "off", "mean2", "var", "diff"))
    u = [sb(f"ffn_u{n}", [P, CH]) for n in range(2)]
    u_hi = sb("ffn_u_hi", [P, KT, CH], F32R)
    u_lo = sb("ffn_u_lo", [P, KT, CH], F32R)
    b1_rows = sb("b1_rows", [FT, P])
    b1_col = sb("b1_col", [P, FT])
    b2_row = sb("b2_row", [1, D])
    b2_parts = sb("b2_parts", [P, D], F32R)
    ones_parts = sb("ones_parts", [P, P], F32R)
    NG_ = 2
    g = [sb(f"gelu{n}", [P, CH]) for n in range(NG_)]
    NH = 2
    h_hi = [sb(f"h_hi{n}", [P, CH], F32R) for n in range(NH)]
    h_lo = [sb(f"h_lo{n}", [P, CH], F32R) for n in range(NH)]
    gated = [sb(f"ffn_gated{n}", [P, D]) for n in range(2)]

    w_ld = [sem(f"ffn_w_ld{n}") for n in range(2)]
    y_ld = [sem(f"ffn_y_ld{b}") for b in range(B)]
    z_st = [sem(f"ffn_z_st{b}") for b in range(B)]
    small_ld, b1_tp, b1_ready, b2_ready, zeroed = (sem(f"ffn_{n}") for n in ("small_ld", "b1_tp", "b1_ready", "b2_ready", "zeroed"))
    whi_ready, wlo_ready = sem("ffn_whi"), sem("ffn_wlo")
    stat, root_ready, ln_chain, norm_ready = (sem(f"ffn_{n}") for n in ("stat", "root", "ln_chain", "norm"))
    tr_ready, uhi_ready, u_ready, ulo_ready = (sem(f"ffn_{n}") for n in ("tr", "uhi", "u", "ulo"))
    h_ready, g_ready, ghi_ready, glo_ready = (sem(f"ffn_{n}") for n in ("h", "g", "ghi", "glo"))
    down_ready, acc_ready, gated_ready, z_ready = (sem(f"ffn_{n}") for n in ("down", "acc", "gated", "z"))

    ACC, H, TR = 0, 4, 6
    NW = 2 * KT
    C1 = FF // KT

    def chunk(dram, i, b):
        return dram[b].rearrange("(i t p) d -> i p t d", p=P, t=TT)[bass.ds(i, 1)].rearrange("o p t d -> (o p) t d")

    def piece(n):
        if n < KT:
            return a["L0_cond_W1"][n * P:(n + 1) * P, :]
        return a["L0_cond_W2"][(n - KT) * TT * P:(n - KT + 1) * TT * P, :].rearrange("(f p) d -> p f d", p=P)

    def raw(n):
        return y[n % 2].rearrange("p t d -> p (t d)") if n < KT else y[n % 2][:, :, :]

    def place(hi, n):
        w1, w2 = (w1_hi, w2_hi) if hi else (w1_lo, w2_lo)
        return w1[:, n, :] if n < KT else w2[:, (n - KT) * TT:(n - KT + 1) * TT, :]

    def steps(engine, front, back):
        front(0, 0)
        with engine.Fori(0, NCH - 1) as i:
            back(i, 0, lambda: front(i, 1))
            back(i, 1, lambda: front(i + 1, 0))
        back(NCH - 1, 0, lambda: front(NCH - 1, 1))
        back(NCH - 1, 1, None)

    with nc.Block() as block:
        @block.sync
        def _(sp):
            sp.dma_start(b1_rows[:, :], a["L0_cond_b1"].rearrange("(f p) -> f p", p=P)).then_inc(small_ld, 16)
            sp.dma_start(b2_row[:, :], a["L0_cond_b2"].rearrange("(o d) -> o d", o=1)).then_inc(small_ld, 16)
            for b in range(B):
                sp.dma_start(gate[b][:, :], vec_dram[V_GATE_F, b:b + 1, :].broadcast_to((P, D))).then_inc(small_ld, 16)
            for n in range(NW):
                if n >= 2:
                    sp.wait_ge(whi_ready, n - 1)
                    sp.wait_ge(wlo_ready, n - 1)
                sp.dma_start(raw(n), piece(n)).then_inc(w_ld[n % 2], 16)
            for b in range(B):
                sp.wait_ge(whi_ready, NW - 1 + b)
                sp.wait_ge(wlo_ready, NW - 1 + b)
                sp.dma_start(y[b][:, :, :], chunk(y_dram, 0, b)).then_inc(y_ld[b], 16)

            def store(i, b):
                sp.wait_ge(z_ready, TT * (2 * i + b + 1))
                sp.dma_start(chunk(z_dram, i, b), y[b][:, :, :]).then_inc(z_st[b], 16)

            with sp.Fori(0, NCH - 1) as i:
                for b in range(B):
                    store(i, b)
                    sp.wait_ge(z_st[b], 16 * (i + 1))
                    sp.dma_start(y[b][:, :, :], chunk(y_dram, i + 1, b)).then_inc(y_ld[b], 16)
            for b in range(B):
                store(NCH - 1, b)
            for b in range(B):
                sp.wait_ge(z_st[b], 16 * NCH)

        @block.tensor
        def _(pe):
            pe.wait_ge(small_ld, 16 * (2 + B))
            pe.transpose(psum[:, TR, 0:FT], b1_rows[:, :], ident[0:FT, 0:FT]).then_inc(b1_tp, 1)
            pe.wait_ge(b1_ready, 1)

            def front(i, b):
                c = 2 * i + b
                pe.wait_ge(norm_ready, c + 1)
                for k in range(KT):
                    pe.wait_ge(u_ready, KT * c + k + 1)
                    for t in range(TT):
                        mm = pe.transpose(psum[:, TR + k % 2, t * P:(t + 1) * P], norm[:, t, k * P:(k + 1) * P], ident[:, :])
                    mm.then_inc(tr_ready, 1)

            def up(c, j):
                if j == 0:
                    pe.wait_ge(uhi_ready, KT * (c + 1))
                    pe.wait_ge(ulo_ready, KT * (c + 1) + 2)
                pe.wait_ge(g_ready, FT * c + j + 1)
                for k in range(KT):
                    f = slice(j * P, (j + 1) * P)
                    mm = split_matmuls(nc, psum[:, H + j % 2, :], w1_hi[:, k, f], w1_lo[:, k, f], u_hi[:, k, :], u_lo[:, k, :],
                                       k == 0, k == KT - 1)
                mm.then_inc(h_ready, 1)

            def down(c, j):
                pe.wait_ge(ghi_ready, FT * c + j + 1)
                pe.wait_ge(glo_ready, FT * c + j + 1)
                for t in range(TT):
                    tok = slice(t * P, (t + 1) * P)
                    if j == 0:
                        pe.wait_ge(gated_ready, TT * c + t + 1)
                        pe.matmul(psum[:, ACC + t, :], ones_parts[:, :], b2_parts[:, :], start=True, stop=False)
                    mm = split_matmuls(nc, psum[:, ACC + t, :], h_hi[j % NH][:, tok], h_lo[j % NH][:, tok], w2_hi[:, j, :], w2_lo[:, j, :],
                                       False, j == FT - 1)
                    if j == FT - 1:
                        mm.then_inc(acc_ready, 1)
                if j < FT - 1:
                    mm.then_inc(down_ready, 1)

            def back(i, b, following):
                c = 2 * i + b
                for j in range(FT):
                    up(c, j)
                    if j == FT - 1 and following:
                        following()
                    if j >= 1:
                        down(c, j - 1)
                down(c, FT - 1)

            pe.wait_ge(b2_ready, 1)
            pe.wait_ge(whi_ready, NW)
            pe.wait_ge(wlo_ready, NW)
            steps(pe, front, back)

        @block.scalar
        def _(act):
            act.sem_inc(u_ready, 2)
            act.sem_inc(g_ready, 2)
            for n in range(NW):
                act.wait_ge(w_ld[n % 2], 16 * (n // 2 + 1))
                act.activation(place(True, n), raw(n), ACT.Copy).then_inc(whi_ready, 1)
            act.wait_ge(b1_ready, 1)

            def front(i, b):
                c = 2 * i + b
                act.wait_ge(stat, MOMENT_STEPS * (c + 1))
                act.activation(root[:, :], var[:, :], ACT.Sqrt).then_inc(root_ready, 1)

            def split(i, b):
                c = 2 * i + b
                for k in range(KT):
                    act.wait_ge(tr_ready, KT * c + k + 1)
                    act.wait_ge(ulo_ready, KT * c + k + 1)
                    act.activation(u[k % 2][:, :], psum[:, TR + k % 2, :], ACT.Identity, scale=columns[:, V_GAIN_F, k, b:b + 1],
                                   bias=columns[:, V_SHIFT_F, k, b:b + 1]).then_inc(u_ready, 1)

            def gelu(c, j):
                act.wait_ge(h_ready, FT * c + j + 1)
                act.wait_ge(glo_ready, FT * c + max(j - NG_ + 1, 0))
                act.activation(g[j % NG_][:, :], psum[:, H + j % 2, :], ACT.Gelu_apprx_tanh, bias=b1_col[:, j:j + 1]).then_inc(g_ready, 1)
                act.wait_ge(g_ready, FT * c + j + 3)
                if j == 1:
                    act.wait_ge(acc_ready, TT * c)
                else:
                    act.wait_ge(down_ready, (FT - 1) * c + max(j - NH + 1, 0))
                act.activation(h_hi[j % NH][:, :], g[j % NG_][:, :], ACT.Copy).then_inc(ghi_ready, 1)

            front(0, 0)
            split(0, 0)
            def back(i, b, nxt):
                c = 2 * i + b
                for j in range(FT):
                    if j == 6 and nxt:
                        front(*nxt)
                    gelu(c, j)
                if nxt:
                    split(*nxt)

            with act.Fori(0, NCH - 1) as i:
                back(i, 0, (i, 1))
                back(i, 1, (i + 1, 0))
            back(NCH - 1, 0, (NCH - 1, 1))
            back(NCH - 1, 1, None)

        @block.vector
        def _(dve):
            dve.sem_inc(gated_ready, TT)
            dve.wait_ge(b1_tp, 1)
            dve.tensor_copy(b1_col[:, :], psum[:, TR, 0:FT]).then_inc(b1_ready, 1)
            dve.memset(ones_parts[:, :].bitcast(F32), 0.0).then_inc(zeroed, 1)
            dve.memset(b2_parts[:, :].bitcast(F32), 0.0).then_inc(zeroed, 1)
            dve.wait_ge(zeroed, 2)
            for r in (0, 32):
                dve.memset(ones_parts[r:r + 1, :].bitcast(F32), 1.0).then_inc(zeroed, 1)
            dve.tensor_copy(b2_parts[0:1, :], b2_row[:, :]).then_inc(zeroed, 1)
            dve.wait_ge(zeroed, 5)
            dve.tensor_tensor(b2_parts[32:33, :], b2_row[:, :], b2_parts[0:1, :].bitcast(F32), ALU.subtract).then_inc(b2_ready, 1)
            for n in range(NW):
                dve.wait_ge(whi_ready, n + 1)
                dve.tensor_tensor(place(False, n), raw(n), place(True, n).bitcast(F32), ALU.subtract).then_inc(wlo_ready, 1)

            def moments(i, b):
                c = 2 * i + b
                dve.wait_ge(y_ld[b], 16 * (i + 1))
                ln_moments(dve, y[b], stats, mean2, var, diff, stat, MOMENT_STEPS * c)

            def normalise(i, b):
                c = 2 * i + b
                dve.wait_ge(root_ready, c + 1)
                ln_inverse(dve, root, mean2, var, inv, off, ln_chain, INVERSE_STEPS * c)
                dve.wait_ge(ln_chain, INVERSE_STEPS * (c + 1))
                dve.wait_ge(tr_ready, KT * c)
                for t in range(TT):
                    nrm = dve.tensor_scalar(norm[:, t, :], y[b][:, t, :], inv[:, t:t + 1], off[:, t:t + 1], ALU.mult, ALU.add)
                nrm.then_inc(norm_ready, 1)

            def split(i, b):
                c = 2 * i + b
                for k in range(KT):
                    dve.wait_ge(u_ready, KT * c + k + 3)
                    dve.tensor_copy(u_hi[:, k, :], u[k % 2][:, :]).then_inc(uhi_ready, 1)

            def back(i, b, nxt):
                c = 2 * i + b
                for j in range(FT):
                    if j == 4 and nxt:
                        moments(*nxt)
                    if j == 6 and nxt:
                        normalise(*nxt)
                    dve.wait_ge(ghi_ready, FT * c + j + 1)
                    dve.tensor_tensor(h_lo[j % NH][:, :], g[j % NG_][:, :], h_hi[j % NH][:, :].bitcast(F32), ALU.subtract).then_inc(glo_ready, 1)
                if nxt:
                    split(*nxt)
                for t in range(TT):
                    dve.wait_ge(acc_ready, TT * c + t + 1)
                    dve.wait_ge(z_ready, TT * c + max(t - 1, 0))
                    dve.tensor_tensor(gated[t % 2][:, :], psum[:, ACC + t, :], gate[b][:, :], ALU.mult).then_inc(gated_ready, 1)

            moments(0, 0)
            normalise(0, 0)
            split(0, 0)
            with dve.Fori(0, NCH - 1) as i:
                back(i, 0, (i, 1))
                back(i, 1, (i + 1, 0))
            back(NCH - 1, 0, (NCH - 1, 1))
            back(NCH - 1, 1, None)

        @block.gpsimd
        def _(pool):
            pool.sem_inc(ulo_ready, 2)

            def split(i, b):
                c = 2 * i + b
                for k in range(KT):
                    pool.wait_ge(uhi_ready, KT * c + k + 1)
                    pool.tensor_tensor(u_lo[:, k, :], u[k % 2][:, :], u_hi[:, k, :].bitcast(F32), ALU.subtract).then_inc(ulo_ready, 1)

            def back(i, b, nxt):
                c = 2 * i + b
                if nxt:
                    split(*nxt)
                for t in range(TT):
                    pool.wait_ge(gated_ready, TT * c + t + 1 + TT)
                    pool.tensor_tensor(y[b][:, t, :], gated[t % 2][:, :], y[b][:, t, :], ALU.add).then_inc(z_ready, 1)

            split(0, 0)
            with pool.Fori(0, NCH - 1) as i:
                back(i, 0, (i, 1))
                back(i, 1, (i + 1, 0))
            back(NCH - 1, 0, (NCH - 1, 1))
            back(NCH - 1, 1, None)


def qkv_stage(nc, sb, sem, psum, a, ident, columns, z_dram, q_dram, k_dram, v_dram):
    wt_hi, wt_lo = (sb(f"wqkv_{n}", [P, KT, 3 * D], F32R) for n in ("hi", "lo"))
    w_raw = [sb(f"wqkv_raw{n}", [P, KT, D]) for n in range(3)]
    z = [sb(f"qkv_z{b}", [P, TT, D]) for b in range(B)]
    norm = sb("qkv_norm", [P, TT, D])
    stats = sb("qkv_stats", [P, TT, 6])
    root, inv, off, mean2, var, diff = (sb(f"qkv_ln_{n}", [P, TT]) for n in ("root", "inv", "off", "mean2", "var", "diff"))
    u = [sb(f"qkv_u{n}", [P, CH]) for n in range(2)]
    u_hi = [sb(f"qkv_u_hi{b}", [P, KT, CH], F32R) for b in range(B)]
    u_lo = [sb(f"qkv_u_lo{b}", [P, KT, CH], F32R) for b in range(B)]
    NO = 4
    o_hi = [sb(f"qk_hi{n}", [P, CH], F32R) for n in range(NO)]
    o_lo = [sb(f"qk_lo{n}", [P, CH], F32R) for n in range(NO)]
    v_out = [sb(f"v_out{n}", [P, D]) for n in range(2)]
    b_nat = sb("bqkv_nat", [1, 3 * D])
    b_sorted = sb("bqkv_sorted", [1, 3 * D])
    b_col = sb("bqkv_col", [P, 2 * KT])
    bv_parts = sb("bv_parts", [P, D], F32R)
    bqkv_ones = sb("bqkv_ones", [P, P], F32R)

    w_ld, small_ld = sem("qkv_w_ld"), sem("qkv_small_ld")
    z_ld = [sem(f"qkv_z_ld{b}") for b in range(B)]
    o_st = [sem(f"qk_st{n}") for n in range(NO)]
    v_st = [sem(f"v_st{n}") for n in range(2)]
    b_tp, b_ready, bv_ready, zeroed, col_done = (sem(f"qkv_{n}") for n in ("b_tp", "b_ready", "bv_ready", "zeroed", "col_done"))
    wt_tp, whi_ready, wlo_ready = sem("qkv_wt"), sem("qkv_whi"), sem("qkv_wlo")
    stat, root_ready, ln_chain, norm_ready = (sem(f"qkv_{n}") for n in ("stat", "root", "ln_chain", "norm"))
    tr_ready, uhi_ready, u_ready, ulo_ready = (sem(f"qkv_{n}") for n in ("tr", "uhi", "u", "ulo"))
    o_ready, ohi_ready, olo_ready = sem("qk_ready"), sem("qk_hi_ready"), sem("qk_lo_ready")
    v_ready, v_copied = sem("v_ready"), sem("v_copied")

    TR, QK, V = 0, 2, 5
    NM = 2 * KT

    def chunk(dram, i, b):
        return dram[b].rearrange("(i t p) d -> i p t d", p=P, t=TT)[bass.ds(i, 1)].rearrange("o p t d -> (o p) t d")

    def steps(engine, front, back):
        front(0, 0)
        with engine.Fori(0, NCH - 1) as i:
            front(i, 1)
            back(i, 0)
            front(i + 1, 0)
            back(i, 1)
        front(NCH - 1, 1)
        back(NCH - 1, 0)
        back(NCH - 1, 1)

    with nc.Block() as block:
        @block.sync
        def _(sp):
            w = a["L1_cond_Wqkv"].rearrange("(m p j) k -> j p m k", p=P, j=3)
            for n in range(3):
                sp.dma_start(w_raw[n][:, :, :], w[n]).then_inc(w_ld, 16)
            sp.dma_start(b_nat[:, :], a["L1_cond_bqkv"].rearrange("(o c) -> o c", o=1)).then_inc(small_ld, 16)
            for b in range(B):
                sp.dma_start(z[b][:, :, :], chunk(z_dram, 0, b)).then_inc(z_ld[b], 16)

            def stores(i, b):
                c = 2 * i + b
                for m in range(NM):
                    sp.wait_ge(ohi_ready, NM * c + m + 1)
                    sp.wait_ge(olo_ready, NM * c + m + 1)
                    dram = (q_dram, k_dram)[m // KT]
                    at = b * L + i * CH
                    for part, tile in enumerate((o_hi[m % NO], o_lo[m % NO])):
                        sp.dma_start(dram[part, (m % KT) * P:(m % KT + 1) * P, bass.ds(at, CH)], tile[:, :].bitcast(F32)).then_inc(o_st[m % NO], 16)
                for t in range(TT):
                    sp.wait_ge(v_copied, TT * c + t + 1 + 2)
                    sp.dma_start(v_dram[bass.ds(b * L + i * CH + t * P, P), :], v_out[t % 2][:, :]).then_inc(v_st[t % 2], 16)

            with sp.Fori(0, NCH - 1) as i:
                for b in range(B):
                    sp.wait_ge(norm_ready, 2 * i + b + 1)
                    sp.dma_start(z[b][:, :, :], chunk(z_dram, i + 1, b)).then_inc(z_ld[b], 16)
                    stores(i, b)
            for b in range(B):
                stores(NCH - 1, b)
            for n in range(NO):
                sp.wait_ge(o_st[n], 16 * 2 * (NM // NO) * B * NCH)
            for n in range(2):
                sp.wait_ge(v_st[n], 16 * (TT // 2) * B * NCH)

        @block.tensor
        def _(pe):
            pe.wait_ge(b_ready, 1)
            for m in range(NM):
                mm = pe.transpose(psum[:, 7, m:m + 1], b_sorted[:, m * P:(m + 1) * P], ident[0:1, 0:1])
            mm.then_inc(b_tp, 1)
            pe.wait_ge(w_ld, 48)
            for n in range(3 * KT):
                j, k = divmod(n, KT)
                if n >= 6:
                    pe.wait_ge(wlo_ready, n - 5)
                for m in range(KT):
                    mm = pe.transpose(psum[:, n % 6, m * P:(m + 1) * P], w_raw[j][:, m, k * P:(k + 1) * P], ident[:, :])
                mm.then_inc(wt_tp, 1)
            pe.wait_ge(wlo_ready, 3 * KT)
            pe.wait_ge(bv_ready, 1)

            def front(i, b):
                c = 2 * i + b
                pe.wait_ge(norm_ready, c + 1)
                for k in range(KT):
                    pe.wait_ge(u_ready, KT * c + k + 1)
                    for t in range(TT):
                        mm = pe.transpose(psum[:, TR + k % 2, t * P:(t + 1) * P], norm[:, t, k * P:(k + 1) * P], ident[:, :])
                    mm.then_inc(tr_ready, 1)

            def back(i, b):
                c = 2 * i + b
                pe.wait_ge(uhi_ready, KT * (c + 1))
                pe.wait_ge(ulo_ready, KT * (c + 1) + 2)
                for m in range(NM):
                    pe.wait_ge(olo_ready, NM * c + max(m - 2, 0))
                    cols = slice(m * P, (m + 1) * P)
                    for k in range(KT):
                        mm = split_matmuls(nc, psum[:, QK + m % 3, :], wt_hi[:, k, cols], wt_lo[:, k, cols],
                                           u_hi[b][:, k, :], u_lo[b][:, k, :], k == 0, k == KT - 1)
                    mm.then_inc(o_ready, 1)
                for t in range(TT):
                    pe.wait_ge(v_copied, TT * c + t + 1)
                    tok = slice(t * P, (t + 1) * P)
                    nc.tensor.matmul(psum[:, V + t % 2, :], bqkv_ones[:, :], bv_parts[:, :], start=True, stop=False)
                    for k in range(KT):
                        mm = split_matmuls(nc, psum[:, V + t % 2, :], u_hi[b][:, k, tok], u_lo[b][:, k, tok],
                                           wt_hi[:, k, 2 * D:3 * D], wt_lo[:, k, 2 * D:3 * D], False, k == KT - 1)
                    mm.then_inc(v_ready, 1)

            steps(pe, front, back)

        @block.scalar
        def _(act):
            act.sem_inc(u_ready, 2)
            act.sem_inc(v_copied, 2)
            for n in range(3 * KT):
                j, k = divmod(n, KT)
                act.wait_ge(wt_tp, n + 1)
                act.activation(wt_hi[:, k, j * D:(j + 1) * D], psum[:, n % 6, :], ACT.Copy).then_inc(whi_ready, 1)
            act.wait_ge(col_done, 1)

            def front(i, b):
                c = 2 * i + b
                act.wait_ge(stat, MOMENT_STEPS * (c + 1))
                act.activation(root[:, :], var[:, :], ACT.Sqrt).then_inc(root_ready, 1)
                for k in range(KT):
                    act.wait_ge(tr_ready, KT * c + k + 1)
                    act.wait_ge(ulo_ready, KT * c + k + 1)
                    act.activation(u[k % 2][:, :], psum[:, TR + k % 2, :], ACT.Identity, scale=columns[:, V_GAIN_1, k, b:b + 1],
                                   bias=columns[:, V_SHIFT_1, k, b:b + 1]).then_inc(u_ready, 1)

            def back(i, b):
                c = 2 * i + b
                for m in range(NM):
                    act.wait_ge(o_ready, NM * c + m + 1)
                    act.wait_ge(o_st[m % NO], 32 * ((NM // NO) * c + m // NO))
                    act.activation(o_hi[m % NO][:, :], psum[:, QK + m % 3, :], ACT.Identity, bias=b_col[:, m:m + 1]).then_inc(ohi_ready, 1)
                for t in range(TT):
                    act.wait_ge(v_ready, TT * c + t + 1)
                    act.wait_ge(v_st[t % 2], 16 * ((TT // 2) * c + t // 2))
                    act.activation(v_out[t % 2][:, :], psum[:, V + t % 2, :], ACT.Copy).then_inc(v_copied, 1)

            steps(act, front, back)

        @block.vector
        def _(dve):
            dve.memset(bqkv_ones[:, :].bitcast(F32), 0.0).then_inc(zeroed, 1)
            dve.memset(bv_parts[:, :].bitcast(F32), 0.0).then_inc(zeroed, 1)
            dve.wait_ge(zeroed, 2)
            for r in (0, 32):
                dve.memset(bqkv_ones[r:r + 1, :].bitcast(F32), 1.0).then_inc(zeroed, 1)
            dve.wait_ge(small_ld, 16)
            for j in range(3):
                dve.tensor_copy(b_sorted[:, j * D:(j + 1) * D], b_nat[:, :].rearrange("o (c j) -> o j c", j=3)[:, j, :]).then_inc(zeroed, 1)
            dve.wait_ge(zeroed, 7)
            dve.tensor_copy(bv_parts[0:1, :], b_sorted[:, 2 * D:3 * D]).then_inc(b_ready, 1)
            dve.wait_ge(b_ready, 1)
            dve.tensor_tensor(bv_parts[32:33, :], b_sorted[:, 2 * D:3 * D], bv_parts[0:1, :].bitcast(F32), ALU.subtract).then_inc(bv_ready, 1)
            dve.wait_ge(b_tp, 1)
            dve.tensor_copy(b_col[:, :], psum[:, 7, 0:NM]).then_inc(col_done, 1)
            dve.wait_ge(col_done, 1)
            for n in range(3 * KT):
                j, k = divmod(n, KT)
                dve.wait_ge(whi_ready, n + 1)
                dve.tensor_tensor(wt_lo[:, k, j * D:(j + 1) * D], psum[:, n % 6, :], wt_hi[:, k, j * D:(j + 1) * D].bitcast(F32),
                                  ALU.subtract).then_inc(wlo_ready, 1)

            def front(i, b):
                c = 2 * i + b
                dve.wait_ge(z_ld[b], 16 * (i + 1))
                ln_moments(dve, z[b], stats, mean2, var, diff, stat, MOMENT_STEPS * c)
                dve.wait_ge(root_ready, c + 1)
                ln_inverse(dve, root, mean2, var, inv, off, ln_chain, INVERSE_STEPS * c)
                dve.wait_ge(ln_chain, INVERSE_STEPS * (c + 1))
                dve.wait_ge(tr_ready, KT * c)
                for t in range(TT):
                    nrm = dve.tensor_scalar(norm[:, t, :], z[b][:, t, :], inv[:, t:t + 1], off[:, t:t + 1], ALU.mult, ALU.add)
                nrm.then_inc(norm_ready, 1)
                for k in range(KT):
                    dve.wait_ge(u_ready, KT * c + k + 3)
                    dve.tensor_copy(u_hi[b][:, k, :], u[k % 2][:, :]).then_inc(uhi_ready, 1)

            def back(i, b):
                c = 2 * i + b
                for m in range(NM):
                    dve.wait_ge(ohi_ready, NM * c + m + 1)
                    dve.scalar_tensor_tensor(out=o_lo[m % NO][:, :], in0=psum[:, QK + m % 3, :], scalar=b_col[:, m:m + 1],
                                             in1=o_hi[m % NO][:, :].bitcast(F32), op0=ALU.add, op1=ALU.subtract).then_inc(olo_ready, 1)

            steps(dve, front, back)

        @block.gpsimd
        def _(pool):
            pool.sem_inc(ulo_ready, 2)

            def front(i, b):
                c = 2 * i + b
                for k in range(KT):
                    pool.wait_ge(uhi_ready, KT * c + k + 1)
                    pool.tensor_tensor(u_lo[b][:, k, :], u[k % 2][:, :], u_hi[b][:, k, :].bitcast(F32), ALU.subtract).then_inc(ulo_ready, 1)

            def back(i, b):
                pass

            steps(pool, front, back)


def attention_stage(nc, sb, sem, psum, q_dram, k_dram, v_dram, att_dram):
    R = 3 * HD
    NKT = L // P
    NKC = L // CH
    NQ = L // CH
    STEP = NQ * NKT
    ITER = B * STEP
    PAIRS = NKT // 2
    NP_ = 8
    MAXES = HG * TT * NKC
    INVERT_AT, NORMALISE_AT = (24, 30, 36, 42), 46
    AV_LAG, SUM_LAG = 2, 5

    keys = [sb(f"keys{b}", [P, HG, L], F32R) for b in range(B)]
    queries = [sb(f"queries{n}", [P, HG, CH], F32R) for n in range(2)]
    values = [sb(f"values{b}", [P, NKT, P]) for b in range(B)]
    ones = sb("att_ones", [P, HD])
    probs = [sb(f"probs{n}", [P, HG, CH]) for n in range(NP_)]
    pair = [sb(f"pair{n}", [P, HG, CH]) for n in range(2)]
    part_max = sb("part_max", [P, HG * TT, NKC])
    maxima = sb("maxima", [P, 32])
    max_rows = sb("max_rows", [P, 32])
    neg_rows = sb("neg_rows", [P, 32], F32R)
    o_sum = sb("o_sum", [P, CH])
    den, recip = sb("den", [P, CH]), sb("recip", [P, CH])
    att = sb("att", [P, CH])
    att_hi = [sb(f"att_hi{n}", [P, CH], F32R) for n in range(2)]
    att_lo = [sb(f"att_lo{n}", [P, CH], F32R) for n in range(2)]

    k_ld = [sem(f"k_ld{b}") for b in range(B)]
    v_ld = [sem(f"v_ld{b}") for b in range(B)]
    q_ld = [sem(f"q_ld{n}") for n in range(2)]
    neg_ld = [sem(f"neg_ld{n}") for n in range(2)]
    att_st = [sem(f"att_st{n}") for n in range(2)]
    consts = sem("att_consts")
    sc_a, sc_b, exp_a, exp_b = sem("scores_a"), sem("scores_b"), sem("exp_a"), sem("exp_b")
    av_ready, pair_ready, sums_ready = sem("av_ready"), sem("pair_ready"), sem("sums_ready")
    max_ready, max_read, turning, neg_ready = (sem(n) for n in ("max_ready", "max_read", "max_turning", "neg_ready"))
    o_copied, den_read, inverted, att_ready, hi_ready, lo_ready = (sem(n) for n in ("o_copied", "den_read", "den_inverted", "att_ready", "att_hi_ready", "att_lo_ready"))

    SA, SB, MX, OUT, DEN = 0, 2, 4, 6, 7

    def where(m):
        return m // STEP, m % STEP // NKT, m % NKT

    with nc.Block() as block:
        @block.sync
        def _(sp):
            def load_keys(i, b):
                src = k_dram.rearrange("e (g h d) t -> e g d h t", h=HG, d=HD)
                for n, part in enumerate((0, 1, 0)):
                    sp.dma_start(keys[b][n * HD:(n + 1) * HD, :, :].bitcast(F32),
                                 src[part, bass.ds(i, 1), :, :, b * L:(b + 1) * L].rearrange("o d h t -> (o d) h t")).then_inc(k_ld[b], 16)

            def load_values(i, b):
                sp.dma_start(values[b][:, :, :], v_dram[b * L:(b + 1) * L, bass.ds(i * P, P)].rearrange("(n p) c -> p n c", p=P)).then_inc(v_ld[b], 16)

            def load_queries(i, b, qb):
                src = q_dram.rearrange("e (g h d) t -> e g d h t", h=HG, d=HD)
                at = b * L + qb * CH
                for n, part in enumerate((0, 0, 1)):
                    sp.dma_start(queries[qb % 2][n * HD:(n + 1) * HD, :, :].bitcast(F32),
                                 src[part, bass.ds(i, 1), :, :, at:at + CH].rearrange("o d h t -> (o d) h t")).then_inc(q_ld[qb % 2], 16)

            def load_max_row(count, qb):
                sp.wait_ge(neg_ready, count + 1)
                row = queries[qb % 2][R:R + 1, :, :].bitcast(F32).rearrange("o h (t r i) -> o (h t) r i", r=4, i=32)
                for r in range(4):
                    sp.dma_start(row[:, :, r, :], neg_rows[32 * r:32 * r + HG * TT, :].bitcast(F32)).then_inc(neg_ld[qb % 2], 16)

            def store(count, i, b, qb):
                sp.wait_ge(hi_ready, count + 1)
                sp.wait_ge(lo_ready, count + 1)
                at = b * L + qb * CH
                for part, tile in enumerate((att_hi[qb % 2], att_lo[qb % 2])):
                    sp.dma_start(att_dram[part, bass.ds(i * P, P), at:at + CH], tile[:, :].bitcast(F32)).then_inc(att_st[qb % 2], 16)

            load_keys(0, 0)
            load_queries(0, 0, 0)
            load_values(0, 0)
            load_queries(0, 0, 1)
            load_keys(0, 1)
            load_values(0, 1)
            load_max_row(0, 0)

            def iteration(i, last):
                for w in range(B * NQ):
                    b, qb = divmod(w, NQ)
                    count = B * NQ * i + w
                    if w > 0:
                        store(count - 1, i, (w - 1) // NQ, (w - 1) % NQ)
                    if qb == 0 and b == 1 and not last:
                        sp.wait_ge(sc_b, ITER * i + STEP)
                        load_keys(i + 1, 0)
                        sp.wait_ge(av_ready, ITER * i + STEP)
                        load_values(i + 1, 0)
                    if not (last and w == B * NQ - 1):
                        load_max_row(count + 1, (qb + 1) % NQ)
                    if qb < NQ - 2:
                        following = (i, b, qb + 2)
                    elif b == 0:
                        following = (i, 1, qb + 2 - NQ)
                    else:
                        following = None if last else (i + 1, 0, qb + 2 - NQ)
                    if following:
                        sp.wait_ge(sc_b, ITER * i + (w + 1) * NKT)
                        load_queries(*following)
                if not last:
                    sp.wait_ge(av_ready, ITER * (i + 1))
                    load_keys(i + 1, 1)
                    load_values(i + 1, 1)
                store(B * NQ * (i + 1) - 1, i, 1, NQ - 1)

            with sp.Fori(0, NG - 1) as i:
                iteration(i, False)
            iteration(NG - 1, True)
            for n in range(2):
                sp.wait_ge(att_st[n], 16 * 2 * B * NQ * NG // 2)

        @block.tensor
        def _(pe):
            pe.wait_ge(consts, B + 2)

            def search(count, i, b, qb, j):
                qt, h, kc = j // (HG * NKC), j // NKC % HG, j % NKC
                x = MAXES * count + j
                if j == 0:
                    pe.wait_ge(q_ld[qb % 2], 48 * (B * NQ // 2 * i + b * (NQ // 2) + qb // 2 + 1))
                    if qb == 0:
                        pe.wait_ge(k_ld[b], 48 * (i + 1))
                pe.wait_ge(max_read, x + 1)
                nc.tensor.matmul(psum[:, MX + j % 2, :], queries[qb % 2][0:R, h, qt * P:(qt + 1) * P],
                                 keys[b][0:R, h, kc * CH:(kc + 1) * CH], start=True, stop=True).then_inc(max_ready, 1)

            def scores(i, m, heads, bank, signal, free):
                b, qb, kt = where(m)
                if kt == 0:
                    pe.wait_ge(neg_ld[qb % 2], 64 * (B * NQ // 2 * i + b * (NQ // 2) + qb // 2 + 1))
                pe.wait_ge(free, ITER * i + m)
                for n, h in enumerate(heads):
                    mm = nc.tensor.matmul(psum[:, bank + n, :], keys[b][0:R + 1, h, kt * P:(kt + 1) * P], queries[qb % 2][0:R + 1, h, :], start=True, stop=True)
                mm.then_inc(signal, 1)

            def weigh(i, m):
                b, qb, kt = where(m)
                pe.wait_ge(exp_a, ITER * i + m + 1)
                pe.wait_ge(exp_b, ITER * i + m + 1)
                if kt == 0:
                    pe.wait_ge(o_copied, B * NQ * i + m // NKT)
                    if qb == 0:
                        pe.wait_ge(v_ld[b], 16 * (i + 1))
                for h in range(HG):
                    mm = nc.tensor.matmul(psum[h * HD:(h + 1) * HD, OUT, :], values[b][:, kt, h * HD:(h + 1) * HD], probs[m % NP_][:, h, :],
                                          start=(kt == 0), stop=(kt == NKT - 1))
                mm.then_inc(av_ready, 1)

            def total(i, p):
                pe.wait_ge(pair_ready, ITER // 2 * i + p + 1)
                if p % PAIRS == 0:
                    pe.wait_ge(den_read, B * NQ * i + p // PAIRS)
                for h in range(HG):
                    mm = nc.tensor.matmul(psum[h * HD:(h + 1) * HD, DEN, :], ones[:, :], pair[p % 2][:, h, :],
                                          start=(p % PAIRS == 0), stop=(p % PAIRS == PAIRS - 1))
                mm.then_inc(sums_ready, 1)

            def iteration(i, last):
                per = MAXES // NKT
                for m in range(ITER):
                    b, qb, kt = where(m)
                    w = m // NKT
                    ahead = None
                    if qb < NQ - 1:
                        ahead = (i, b, qb + 1)
                    elif b == 0:
                        ahead = (i, 1, 0)
                    elif not last:
                        ahead = (i + 1, 0, 0)

                    def searches(n):
                        if ahead:
                            search(B * NQ * i + w + 1, *ahead, per * kt + n)

                    scores(i, m, (0, 1), SA, sc_a, exp_a)
                    searches(0)
                    if m >= AV_LAG:
                        weigh(i, m - AV_LAG)
                    searches(1)
                    scores(i, m, (2, 3), SB, sc_b, exp_b)
                    searches(2)
                    if m >= SUM_LAG and (m - SUM_LAG) % 2 == 0:
                        total(i, (m - SUM_LAG) // 2)
                    searches(3)
                for m in range(ITER - AV_LAG, ITER):
                    weigh(i, m)
                for p in range((ITER - SUM_LAG + 1) // 2, ITER // 2):
                    total(i, p)

            for j in range(MAXES):
                search(0, 0, 0, 0, j)
            with pe.Fori(0, NG - 1) as i:
                iteration(i, False)
            iteration(NG - 1, True)

        @block.scalar
        def _(act):
            def copy_out(i, w):
                act.wait_ge(av_ready, ITER * i + (w + 1) * NKT)
                act.wait_ge(att_ready, B * NQ * i + w)
                act.activation(o_sum[:, :], psum[:, OUT, :], ACT.Copy).then_inc(o_copied, 1)

            def copy_sums(i, w):
                act.wait_ge(sums_ready, ITER // 2 * i + (w + 1) * PAIRS)
                act.activation(den[:, :], psum[:, DEN, :], ACT.Copy).then_inc(den_read, 1)

            def split(i, w):
                act.wait_ge(att_ready, B * NQ * i + w + 1)
                act.wait_ge(att_st[w % 2], 32 * (B * NQ // 2 * i + w // 2))
                act.activation(att_hi[w % 2][:, :], att[:, :], ACT.Copy).then_inc(hi_ready, 1)

            def iteration(i):
                for m in range(ITER):
                    w, kt = divmod(m, NKT)
                    act.wait_ge(av_ready, ITER * i + max(m - NP_ + 1, 0))
                    act.wait_ge(pair_ready, ITER // 2 * i + max((m - NP_) // 2 + 1, 0))
                    for bank, ready, done, h in ((SA, sc_a, exp_a, 0), (SB, sc_b, exp_b, 2)):
                        act.wait_ge(ready, ITER * i + m + 1)
                        act.activation(probs[m % NP_][:, h:h + 2, :], psum[:, bank:bank + 2, :], ACT.Exp).then_inc(done, 1)
                    if w > 0 and kt == 1:
                        copy_out(i, w - 1)
                    if w > 0 and kt == 4:
                        copy_sums(i, w - 1)
                    if w > 0 and kt == 13:
                        split(i, w - 1)
                copy_out(i, B * NQ - 1)
                copy_sums(i, B * NQ - 1)
                split(i, B * NQ - 1)

            with act.Fori(0, NG) as i:
                iteration(i)

        @block.vector
        def _(dve):
            dve.sem_inc(max_read, 2)
            for b in range(B):
                dve.memset(keys[b][R:R + 1, :, :].bitcast(F32), 1.0).then_inc(consts, 1)
            dve.memset(ones[:, :], 1.0).then_inc(consts, 1)
            dve.memset(maxima[:, :], 0.0).then_inc(consts, 1)

            def find(count, j):
                qt, h, kc = j // (HG * NKC), j // NKC % HG, j % NKC
                dve.wait_ge(max_ready, MAXES * count + j + 1)
                at = h * TT + qt
                dve.tensor_reduce(part_max[:, at, kc:kc + 1], psum[:, MX + j % 2, :], AX.X, ALU.max).then_inc(max_read, 1)

            def finish(count):
                dve.wait_ge(max_read, MAXES * (count + 1) + 2)
                dve.tensor_reduce(maxima[:, 0:HG * TT], part_max[:, :, :], AX.X, ALU.max).then_inc(turning, 1)
                dve.wait_ge(turning, 2 * count + 1)
                dve.transpose(max_rows[:, :], maxima[:, :]).then_inc(turning, 1)
                dve.wait_ge(turning, 2 * count + 2)
                dve.tensor_scalar(neg_rows[:, :], max_rows[:, :], -1.0, None, ALU.mult).then_inc(neg_ready, 1)

            def invert(i, w, n):
                dve.wait_ge(den_read, B * NQ * i + w + 1)
                part = slice(n * P, (n + 1) * P)
                dve.reciprocal(recip[:, part], den[:, part]).then_inc(inverted, 1)

            def normalise(i, w):
                dve.wait_ge(inverted, TT * (B * NQ * i + w + 1))
                dve.wait_ge(o_copied, B * NQ * i + w + 1)
                dve.wait_ge(hi_ready, B * NQ * i + w)
                dve.wait_ge(lo_ready, B * NQ * i + w)
                dve.scalar_tensor_tensor(out=att[:, :], in0=o_sum[:, :], scalar=float(D) ** -0.5, in1=recip[:, :],
                                         op0=ALU.mult, op1=ALU.mult).then_inc(att_ready, 1)

            dve.wait_ge(consts, B + 2)
            for j in range(MAXES):
                find(0, j)
            finish(0)

            def iteration(i, last):
                for w in range(B * NQ):
                    searching = not (last and w == B * NQ - 1)
                    for j in range(MAXES):
                        if w > 0 and j in INVERT_AT:
                            invert(i, w - 1, INVERT_AT.index(j))
                        if w > 0 and j == NORMALISE_AT:
                            normalise(i, w - 1)
                        if searching:
                            find(B * NQ * i + w + 1, j)
                    if searching:
                        dve.wait_ge(neg_ld[w % 2], 64 * (B * NQ // 2 * i + w // 2 + 1))
                        finish(B * NQ * i + w + 1)
                for n in range(TT):
                    invert(i, B * NQ - 1, n)
                normalise(i, B * NQ - 1)

            with dve.Fori(0, NG - 1) as i:
                iteration(i, False)
            iteration(NG - 1, True)

        @block.gpsimd
        def _(pool):
            def split(i, w):
                pool.wait_ge(hi_ready, B * NQ * i + w + 1)
                pool.tensor_tensor(att_lo[w % 2][:, :], att[:, :], att_hi[w % 2][:, :].bitcast(F32), ALU.subtract).then_inc(lo_ready, 1)

            def iteration(i):
                for p in range(ITER // 2):
                    w, at = divmod(p, PAIRS)
                    if w > 0 and at == 7:
                        split(i, w - 1)
                    pool.wait_ge(exp_a, ITER * i + 2 * p + 2)
                    pool.wait_ge(exp_b, ITER * i + 2 * p + 2)
                    pool.wait_ge(sums_ready, ITER // 2 * i + max(p - 1, 0))
                    pool.tensor_tensor(pair[p % 2][:, :, :], probs[2 * p % NP_][:, :, :], probs[(2 * p + 1) % NP_][:, :, :], ALU.add).then_inc(pair_ready, 1)
                split(i, B * NQ - 1)

            with pool.Fori(0, NG) as i:
                iteration(i)


def project_stage(nc, sb, sem, psum, a, ident, vec_dram, att_dram, z_dram, out):
    wp = sb("wp", [P, KT, D])
    wt_hi, wt_lo = (sb(f"wp_{n}", [P, KT, D], F32R) for n in ("hi", "lo"))
    bp_row = sb("bp_row", [1, D])
    bp_parts = sb("bp_parts", [P, D], F32R)
    bp_ones = sb("bp_ones", [P, P], F32R)
    gain = [sb(f"gain{b}", [P, D]) for b in range(B)]
    shift = [sb(f"shift{b}", [P, D]) for b in range(B)]
    att_hi, att_lo = ([sb(f"p_att_{n}{b}", [P, KT, CH], F32R) for b in range(B)] for n in ("hi", "lo"))
    z = [sb(f"p_z{b}", [P, TT, D]) for b in range(B)]
    h = [sb(f"p_h{b}", [P, TT, D]) for b in range(B)]
    shifted = [sb(f"p_shifted{b}", [P, TT, D]) for b in range(B)]
    norm = [sb(f"p_norm{b}", [P, TT, D]) for b in range(B)]
    result = [sb(f"p_result{b}", [P, TT, D]) for b in range(B)]
    stats = sb("p_stats", [P, TT, 6])
    root, mean2, var, diff = (sb(f"p_{n}", [P, TT]) for n in ("root", "mean2", "var", "diff"))
    inv = [sb(f"p_inv{b}", [P, TT]) for b in range(B)]
    off = [sb(f"p_off{b}", [P, TT]) for b in range(B)]

    small_ld = sem("p_small_ld")
    att_ld = [sem(f"p_att_ld{b}") for b in range(B)]
    z_ld = [sem(f"p_z_ld{b}") for b in range(B)]
    out_st = [sem(f"p_out_st{b}") for b in range(B)]
    consts, wt_tp, whi_ready, wlo_ready = (sem(f"p_{n}") for n in ("consts", "wt_tp", "whi", "wlo"))
    sum_ready, h_ready, stat, root_ready, ln_chain = (sem(f"p_{n}") for n in ("sum", "h", "stat", "root", "ln_chain"))
    shifted_ready, norm_ready, scaled_ready, result_ready = (sem(f"p_{n}") for n in ("shifted", "norm", "scaled", "result"))

    def chunk(dram, i, b):
        return dram[b].rearrange("(i t p) d -> i p t d", p=P, t=TT)[bass.ds(i, 1)].rearrange("o p t d -> (o p) t d")

    def steps(engine, front, back):
        front(0, 0)
        with engine.Fori(0, NCH - 1) as i:
            front(i, 1)
            back(i, 0)
            front(i + 1, 0)
            back(i, 1)
        front(NCH - 1, 1)
        back(NCH - 1, 0)
        back(NCH - 1, 1)

    with nc.Block() as block:
        @block.sync
        def _(sp):
            sp.dma_start(wp[:, :, :], a["L1_cond_Wp"].rearrange("(m p) k -> p m k", p=P)).then_inc(small_ld, 16)
            sp.dma_start(bp_row[:, :], a["L1_cond_bp"].rearrange("(o d) -> o d", o=1)).then_inc(small_ld, 16)

            def load(i, b):
                for part, tile in enumerate((att_hi[b], att_lo[b])):
                    sp.dma_start(tile[:, :, :].bitcast(F32), att_dram[part, :, bass.ds(b * L + i * CH, CH)].rearrange("(k p) t -> p k t", p=P)).then_inc(att_ld[b], 16)
                sp.dma_start(z[b][:, :, :], chunk(z_dram, i, b)).then_inc(z_ld[b], 16)

            for b in range(B):
                load(0, b)
            for b in range(B):
                sp.dma_start(gain[b][:, :], vec_dram[V_GAIN_1, b:b + 1, :].broadcast_to((P, D))).then_inc(small_ld, 16)
                sp.dma_start(shift[b][:, :], vec_dram[V_SHIFT_1, b:b + 1, :].broadcast_to((P, D))).then_inc(small_ld, 16)

            def store(i, b):
                sp.wait_ge(result_ready, TT * (2 * i + b + 1))
                sp.dma_start(chunk(out, i, b), result[b][:, :, :]).then_inc(out_st[b], 16)

            with sp.Fori(0, NCH - 1) as i:
                for b in range(B):
                    sp.wait_ge(h_ready, TT * (2 * i + b + 1))
                    load(i + 1, b)
                    store(i, b)
            for b in range(B):
                store(NCH - 1, b)
            for b in range(B):
                sp.wait_ge(out_st[b], 16 * NCH)

        @block.tensor
        def _(pe):
            pe.wait_ge(small_ld, 16 * (2 + 2 * B))
            for k in range(KT):
                for m in range(KT):
                    mm = pe.transpose(psum[:, 4 + k, m * P:(m + 1) * P], wp[:, m, k * P:(k + 1) * P], ident[:, :])
                mm.then_inc(wt_tp, 1)
            pe.wait_ge(consts, 6)
            pe.wait_ge(wlo_ready, KT)

            def front(i, b):
                c = 2 * i + b
                pe.wait_ge(att_ld[b], 32 * (i + 1))
                for t in range(TT):
                    pe.wait_ge(h_ready, TT * c)
                    tok = slice(t * P, (t + 1) * P)
                    nc.tensor.matmul(psum[:, t, :], bp_ones[:, :], bp_parts[:, :], start=True, stop=False)
                    for k in range(KT):
                        mm = split_matmuls(nc, psum[:, t, :], att_hi[b][:, k, tok], att_lo[b][:, k, tok], wt_hi[:, k, :], wt_lo[:, k, :],
                                           False, k == KT - 1)
                    mm.then_inc(sum_ready, 1)

            def back(i, b):
                pass

            steps(pe, front, back)

        @block.scalar
        def _(act):
            for k in range(KT):
                act.wait_ge(wt_tp, k + 1)
                act.activation(wt_hi[:, k, :], psum[:, 4 + k, :], ACT.Copy).then_inc(whi_ready, 1)

            def front(i, b):
                c = 2 * i + b
                act.wait_ge(stat, MOMENT_STEPS * (c + 1))
                act.activation(root[:, :], var[:, :], ACT.Sqrt).then_inc(root_ready, 1)
                act.wait_ge(ln_chain, INVERSE_STEPS * (c + 1))
                act.wait_ge(result_ready, TT * 2 * i)
                for t in range(TT):
                    act.activation(norm[b][:, t, :], h[b][:, t, :], ACT.Identity, scale=inv[b][:, t:t + 1], bias=off[b][:, t:t + 1]).then_inc(norm_ready, 1)

            def back(i, b):
                pass

            steps(act, front, back)

        @block.vector
        def _(dve):
            dve.memset(bp_ones[:, :].bitcast(F32), 0.0).then_inc(consts, 1)
            dve.memset(bp_parts[:, :].bitcast(F32), 0.0).then_inc(consts, 1)
            dve.wait_ge(consts, 2)
            for r in (0, 32):
                dve.memset(bp_ones[r:r + 1, :].bitcast(F32), 1.0).then_inc(consts, 1)
            dve.wait_ge(small_ld, 16 * (2 + 2 * B))
            dve.tensor_copy(bp_parts[0:1, :], bp_row[:, :]).then_inc(consts, 1)
            dve.wait_ge(consts, 5)
            dve.tensor_tensor(bp_parts[32:33, :], bp_row[:, :], bp_parts[0:1, :].bitcast(F32), ALU.subtract).then_inc(consts, 1)
            for k in range(KT):
                dve.wait_ge(whi_ready, k + 1)
                dve.tensor_tensor(wt_lo[:, k, :], psum[:, 4 + k, :], wt_hi[:, k, :].bitcast(F32), ALU.subtract).then_inc(wlo_ready, 1)

            def front(i, b):
                c = 2 * i + b
                dve.wait_ge(z_ld[b], 16 * (i + 1))
                for t in range(TT):
                    dve.wait_ge(sum_ready, TT * c + t + 1)
                    dve.tensor_tensor(h[b][:, t, :], psum[:, t, :], z[b][:, t, :], ALU.add).then_inc(h_ready, 1)
                dve.wait_ge(h_ready, TT * (c + 1))
                ln_moments(dve, h[b], stats, mean2, var, diff, stat, MOMENT_STEPS * c)
                dve.wait_ge(root_ready, c + 1)
                ln_inverse(dve, root, mean2, var, inv[b], off[b], ln_chain, INVERSE_STEPS * c)

            def back(i, b):
                c = 2 * i + b
                for t in range(TT):
                    dve.wait_ge(norm_ready, TT * c + t + 1)
                    dve.tensor_tensor(norm[b][:, t, :], norm[b][:, t, :], gain[b][:, :], ALU.mult).then_inc(scaled_ready, 1)
                dve.wait_ge(out_st[b], 16 * i)
                for t in range(TT):
                    dve.wait_ge(scaled_ready, TT * c + t + 1)
                    dve.wait_ge(shifted_ready, TT * c + t + 1)
                    dve.tensor_tensor(result[b][:, t, :], norm[b][:, t, :], shifted[b][:, t, :], ALU.add).then_inc(result_ready, 1)

            steps(dve, front, back)

        @block.gpsimd
        def _(pool):
            pool.wait_ge(small_ld, 16 * (2 + 2 * B))

            def front(i, b):
                c = 2 * i + b
                for t in range(TT):
                    pool.wait_ge(h_ready, TT * c + t + 1)
                    pool.wait_ge(result_ready, TT * 2 * i)
                    pool.tensor_tensor(shifted[b][:, t, :], h[b][:, t, :], shift[b][:, :], ALU.add).then_inc(shifted_ready, 1)

            def back(i, b):
                pass

            steps(pool, front, back)


def cond_seq_kernel(nc, a, out):
    with ExitStack() as whole:
        def sem(name):
            return whole.enter_context(nc.semaphore(name))

        def scope(stack):
            def sb(name, shape, dtype=F32):
                return stack.enter_context(nc.sbuf_tensor(name, list(shape), dtype))
            return sb

        psum = whole.enter_context(nc.psum_tensor("psum", [P, 8, CH], F32))
        sb = scope(whole)
        ident = sb("ident", [P, P])
        columns = sb("columns", [P, NVC, KT, B])

        def scratch(name, shape, dtype=F32):
            return nc.dram_tensor(name, list(shape), dtype).ap()

        vec_dram = scratch("vec_rows", [NV, B, D])
        y_dram, z_dram = scratch("y_rows", [B, L, D]), scratch("z_rows", [B, L, D])
        q_dram, k_dram = scratch("q_parts", [2, D, B * L]), scratch("k_parts", [2, D, B * L])
        v_dram, att_dram = scratch("v_rows", [B * L, D]), scratch("att_parts", [2, D, B * L])

        with ExitStack() as state_space:
            own = scope(state_space)
            s5 = {n: own(f"s5_{n}", [P, CH]) for n in ("cos", "sin", "decay")}
            for part in ("hi", "lo"):
                s5[f"b_{part}"] = own(f"s5_b_{part}", [P, KT, 2 * P], F32R)
                s5[f"c_{part}"] = own(f"s5_c_{part}", [P, 2, D], F32R)
                s5[f"d_{part}"] = own(f"s5_d_{part}", [P, KT, P], F32R)
            with ExitStack() as stage:
                prep_stage(nc, scope(stage), sem, psum, a, ident, columns, s5, vec_dram)
            with ExitStack() as stage:
                s5_stage(nc, scope(stage), sem, psum, a, ident, columns, s5, vec_dram, y_dram)
        with ExitStack() as stage:
            ffn_stage(nc, scope(stage), sem, psum, a, ident, columns, vec_dram, y_dram, z_dram)
        with ExitStack() as stage:
            qkv_stage(nc, scope(stage), sem, psum, a, ident, columns, z_dram, q_dram, k_dram, v_dram)
        with ExitStack() as stage:
            attention_stage(nc, scope(stage), sem, psum, q_dram, k_dram, v_dram, att_dram)
        with ExitStack() as stage:
            project_stage(nc, scope(stage), sem, psum, a, ident, vec_dram, att_dram, z_dram, out)


_INS = ["x", "cond_1024"] + [f"L0_cond_{n}" for n in (
    "Wm", "bm", "Lam_re", "Lam_im", "B_re", "B_im", "C_re", "C_im", "D_diag", "log_step", "Wc", "bc", "W1", "b1", "W2", "b2")] + [
    f"L1_cond_{n}" for n in ("ln_g", "ln_b", "Wg", "bg", "Wb", "bb", "Wqkv", "bqkv", "Wp", "bp")]


def kernel(**inputs):
    import numpy as _np
    import concourse.bacc as _bacc
    from concourse import mybir as _mybir
    from concourse.bass_utils import run_bass_kernel_spmd as _run

    nc = _bacc.Bacc("TRN2", target_bir_lowering=False, num_devices=1)
    arrays, args = {}, {}
    for name in _INS:
        v = _np.ascontiguousarray(inputs[name])
        arrays[f"in_{name}_dram"] = v
        args[name] = nc.dram_tensor(f"in_{name}_dram", v.shape, _mybir.dt.from_np(v.dtype), kind="ExternalInput").ap()
    out = nc.dram_tensor("out_dram", (B, L, D), F32, kind="ExternalOutput").ap()
    cond_seq_kernel(nc, args, out)
    r = _run(nc, [arrays], core_ids=[0])
    return r.results[0]["out_dram"]
```

```python
import concourse.bass as bass
from concourse import mybir
from contextlib import ExitStack

B, L, D = 2, 2048, 512
P = 128
KT = D // P
FF = 2048
FT = FF // P
HEADS, HD = 16, 32
HG = P // HD
NG = HEADS // HG
CH = 512
NCH = L // CH
TT = CH // P
EPS = 1e-5

F32 = mybir.dt.float32
F32R = mybir.dt.float32r
I32 = mybir.dt.int32
ALU = mybir.AluOpType
ACT = mybir.ActivationFunctionType
AX = mybir.AxisListType

V_GAIN_A, V_SHIFT_A, V_GAIN_F, V_SHIFT_F, V_GAIN_1, V_SHIFT_1, V_GATE_A, V_GATE_F = range(8)
NV, NVC = 8, 6



def split_matmuls(nc, out, w_hi, w_lo, x_hi, x_lo, first, last):
    nc.tensor.matmul(out, w_hi, x_hi, start=first, stop=False)
    nc.tensor.matmul(out, w_lo, x_hi, start=False, stop=False)
    return nc.tensor.matmul(out, w_hi, x_lo, start=False, stop=last)


def wait_count(engine, semaphore, count):
    if not isinstance(count, int) or count > 0:
        engine.wait_ge(semaphore, count)


MOMENT_STEPS, INVERSE_STEPS = TT + 6, 6


def ln_moments(dve, x, stats, mean2, var, diff, stat, at):
    for t in range(TT):
        dve.bn_stats(stats[:, t, :], x[:, t, :]).then_inc(stat, 1)
    dve.wait_ge(stat, at + TT)
    dve.tensor_tensor(mean2[:, :], stats[:, :, 1], stats[:, :, 4], ALU.add).then_inc(stat, 1)
    dve.tensor_tensor(diff[:, :], stats[:, :, 1], stats[:, :, 4], ALU.subtract).then_inc(stat, 1)
    dve.tensor_tensor(var[:, :], stats[:, :, 2], stats[:, :, 5], ALU.add).then_inc(stat, 1)
    dve.wait_ge(stat, at + TT + 2)
    dve.scalar_tensor_tensor(out=diff[:, :], in0=diff[:, :], scalar=0.25, in1=diff[:, :], op0=ALU.mult, op1=ALU.mult).then_inc(stat, 1)
    dve.wait_ge(stat, at + TT + 3)
    dve.tensor_scalar(var[:, :], var[:, :], 1.0 / D, EPS, ALU.mult, ALU.add).then_inc(stat, 1)
    dve.wait_ge(stat, at + TT + 5)
    dve.tensor_tensor(var[:, :], var[:, :], diff[:, :], ALU.add).then_inc(stat, 1)


def ln_inverse(dve, root, mean2, var, inv, off, chain, at):
    dve.reciprocal(inv[:, :], root[:, :]).then_inc(chain, 1)
    dve.wait_ge(chain, at + 1)
    dve.tensor_tensor(off[:, :], inv[:, :], inv[:, :], ALU.mult).then_inc(chain, 1)
    dve.wait_ge(chain, at + 2)
    dve.tensor_tensor(off[:, :], off[:, :], var[:, :], ALU.mult).then_inc(chain, 1)
    dve.wait_ge(chain, at + 3)
    dve.tensor_scalar(off[:, :], off[:, :], -0.5, 1.5, ALU.mult, ALU.add).then_inc(chain, 1)
    dve.wait_ge(chain, at + 4)
    dve.tensor_tensor(inv[:, :], inv[:, :], off[:, :], ALU.mult).then_inc(chain, 1)
    dve.wait_ge(chain, at + 5)
    dve.scalar_tensor_tensor(out=off[:, :], in0=mean2[:, :], scalar=-0.5, in1=inv[:, :], op0=ALU.mult, op1=ALU.mult).then_inc(chain, 1)


def prep_stage(nc, sb, sem, psum, a, ident, columns, s5, vec_dram):
    wm = sb("wm", [P, KT, 6 * D])
    wc = sb("wc", [P, KT, 2 * D])
    wgb = sb("wgb", [P, 2, KT, D])
    wgb_t = sb("wgb_t", [P, 2, KT, D])
    cond = sb("cond", [B, D])
    cond_t = sb("cond_t", [P, KT, B])
    bias = sb("bias", [B, 10, D])
    ln_gb = sb("ln_gb", [B, 2, D])
    mod = sb("mod", [B, 10, D])
    vec = sb("vec", [B, NV, D])
    d_rows = sb("d_rows", [KT, P])
    d_col = sb("d_col", [P, KT])
    lam = sb("lam", [P, 3])
    b_in = sb("b_in", [P, 2, D])
    c_in = sb("c_in", [P, 2, KT, P])
    b_bar = sb("b_bar", [P, 2, D])
    tmp = sb("prep_tmp", [P, D])
    scr = sb("prep_scr", [P, 64])
    pow2 = sb("prep_pow2", [P, 1], I32)

    ld_ssm, ld_row, ld_wm, ld_wc, ld_wgb = (sem(f"prep_ld_{n}") for n in ("ssm", "row", "wm", "wc", "wgb"))
    ident_ready = sem("ident_ready")
    cond_tp, cond_ready = sem("cond_tp"), sem("cond_ready")
    sec_ready, sec_read = sem("sec_ready"), sem("sec_read")
    gb_tp, gb_ready = sem("gb_tp"), sem("gb_ready")
    d_tp, d_ready = sem("d_tp"), sem("d_ready")
    chain = sem("prep_chain")
    bbar_ready, bc_tp, bc_hi, bc_lo = sem("bbar_ready"), sem("bc_tp"), sem("bc_hi"), sem("bc_lo")
    vec_ready, col_tp = sem("vec_ready"), sem("col_tp")
    vec_stored = sem("vec_stored")

    def rows(v, n):
        return v.rearrange("(o n d) -> o n d", o=1, n=n)

    with nc.Block() as block:
        @block.sync
        def _(sp):
            for n, name in enumerate(("Lam_re", "Lam_im", "log_step")):
                sp.dma_start(lam[:, n:n + 1], a["L0_cond_" + name].rearrange("(p o) -> p o", o=1)).then_inc(ld_ssm, 16)
            for n, name in enumerate(("B_re", "B_im")):
                sp.dma_start(b_in[:, n, :], a["L0_cond_" + name]).then_inc(ld_ssm, 16)
            for n, name in enumerate(("C_re", "C_im")):
                sp.dma_start(c_in[:, n], a["L0_cond_" + name].rearrange("(k d) p -> d k p", d=P)).then_inc(ld_ssm, 16)
            sp.dma_start(d_rows[:, :], a["L0_cond_D_diag"].rearrange("(k p) -> k p", p=P)).then_inc(ld_ssm, 16)
            sp.dma_start(cond[:, :], a["cond_1024"]).then_inc(ld_row, 16)
            for b in range(B):
                for at, n, name in ((0, 6, "L0_cond_bm"), (6, 2, "L0_cond_bc"), (8, 1, "L1_cond_bg"), (9, 1, "L1_cond_bb")):
                    sp.dma_start(bias[b:b + 1, at:at + n, :], rows(a[name], n)).then_inc(ld_row, 16)
                for at, name in enumerate(("L1_cond_ln_g", "L1_cond_ln_b")):
                    sp.dma_start(ln_gb[b:b + 1, at:at + 1, :], rows(a[name], 1)).then_inc(ld_row, 16)
            sp.dma_start(wm[:, :, :], a["L0_cond_Wm"].rearrange("(k p) n -> p k n", p=P)).then_inc(ld_wm, 16)
            sp.dma_start(wc[:, :, :], a["L0_cond_Wc"].rearrange("(k p) n -> p k n", p=P)).then_inc(ld_wc, 16)
            for n, name in enumerate(("Wg", "Wb")):
                sp.dma_start(wgb[:, n], a["L1_cond_" + name].rearrange("(m p) k -> p m k", p=P)).then_inc(ld_wgb, 16)
            sp.wait_ge(vec_ready, 1)
            sp.dma_start(vec_dram.rearrange("v b d -> b v d"), vec[:, :, :]).then_inc(vec_stored, 16)
            sp.wait_ge(vec_stored, 16)

        @block.gpsimd
        def _(pool):
            pool.memset(ident[:, :], 0.0).then_inc(ident_ready, 1)
            pool.wait_ge(ident_ready, 1)
            pool.affine_select(out=ident[:, :], in_=ident[:, :], compare_op=ALU.not_equal, fill=1.0, base=0,
                               pattern=[[-1, P]], channel_multiplier=1).then_inc(ident_ready, 1)

        @block.tensor
        def _(pe):
            pe.wait_ge(ident_ready, 2)
            pe.wait_ge(ld_ssm, 16 * 8)
            pe.transpose(psum[:, 7, 0:KT], d_rows[:, :], ident[0:KT, 0:KT]).then_inc(d_tp, 1)
            for n in range(2):
                for k in range(KT):
                    mm = pe.transpose(psum[:, n, k * P:(k + 1) * P], c_in[:, n, k, :], ident[:, :])
                mm.then_inc(bc_tp, 1)
            pe.wait_ge(ld_row, 16 * (1 + 6 * B))
            for k in range(KT):
                mm = pe.transpose(psum[:, 6, k * B:(k + 1) * B], cond[:, k * P:(k + 1) * P], ident[0:B, 0:B])
            mm.then_inc(cond_tp, 1)
            pe.wait_ge(bbar_ready, 1)
            for n in range(2):
                for k in range(KT):
                    mm = pe.transpose(psum[:, 2 + n, k * P:(k + 1) * P], b_bar[:, n, k * P:(k + 1) * P], ident[:, :])
                mm.then_inc(bc_tp, 1)
            pe.wait_ge(cond_ready, 1)
            for n in range(10):
                if n == 0:
                    pe.wait_ge(ld_wm, 16)
                if n == 6:
                    pe.wait_ge(ld_wc, 16)
                if n == 8:
                    pe.wait_ge(ld_wgb, 32)
                    pe.wait_ge(bc_hi, 4)
                    pe.wait_ge(bc_lo, 4)
                    for j in range(2 * KT):
                        if j >= 4:
                            pe.wait_ge(gb_ready, j - 3)
                        for m in range(KT):
                            mm = pe.transpose(psum[:, j % 4, m * P:(m + 1) * P],
                                              wgb[:, j // KT, m, (j % KT) * P:(j % KT + 1) * P], ident[:, :])
                        mm.then_inc(gb_tp, 1)
                    pe.wait_ge(gb_ready, 2 * KT)
                if n >= 2:
                    pe.wait_ge(sec_read, n - 1)
                for k in range(KT):
                    w = wm[:, k, n * D:(n + 1) * D] if n < 6 else (
                        wc[:, k, (n - 6) * D:(n - 5) * D] if n < 8 else wgb_t[:, n - 8, k, :])
                    mm = pe.matmul(psum[0:B, 4 + n % 2, :], cond_t[:, k, :], w, start=(k == 0), stop=(k == KT - 1))
                mm.then_inc(sec_ready, 1)
            pe.wait_ge(vec_ready, 1)
            for v in range(NVC):
                for k in range(KT):
                    at = (v * KT + k) * B
                    mm = pe.transpose(psum[:, 6, at:at + B], vec[:, v, k * P:(k + 1) * P], ident[0:B, 0:B])
            mm.then_inc(col_tp, 1)

        @block.scalar
        def _(act):
            for n, times in enumerate((2.0, -2.0)):
                act.wait_ge(bc_tp, n + 1)
                act.activation(s5["c_hi"][:, n, :], psum[:, n, :], ACT.Copy, scale=times).then_inc(bc_hi, 1)
            act.wait_ge(cond_tp, 1)
            act.activation(cond_t[:, :, :], psum[:, 6, 0:KT * B].rearrange("p (k b) -> p k b", b=B), ACT.Copy).then_inc(cond_ready, 1)
            for n in range(2):
                act.wait_ge(bc_tp, 3 + n)
                act.activation(s5["b_hi"][:, :, n * P:(n + 1) * P], psum[:, 2 + n, :].rearrange("p (k s) -> p k s", s=P),
                               ACT.Copy).then_inc(bc_hi, 1)
            for j in range(2 * KT):
                act.wait_ge(gb_tp, j + 1)
                act.activation(wgb_t[:, j // KT, j % KT, :], psum[:, j % 4, :], ACT.Copy).then_inc(gb_ready, 1)
            act.wait_ge(col_tp, 1)
            act.activation(columns[:, :, :, :], psum[:, 6, 0:NVC * KT * B].rearrange("p (v k b) -> p v k b", k=KT, b=B),
                           ACT.Copy)

        @block.vector
        def _(dve):
            done = [0]

            def link(instruction):
                done[0] += 1
                instruction.then_inc(chain, 1)
                dve.wait_ge(chain, done[0])

            used = [0]

            def col():
                used[0] += 1
                return scr[:, used[0] - 1:used[0]]

            def polynomial(out, y, coefficients):
                top, following, *rest = coefficients[::-1]
                link(dve.tensor_scalar(out, y, top, following, ALU.mult, ALU.add))
                for c in rest:
                    link(dve.tensor_scalar(out, out, y, c, ALU.mult, ALU.add))

            MAGIC = 1.5 * 2 ** 23

            def exponential(out, x):
                n, f, p = col(), col(), col()
                link(dve.tensor_scalar(f, x, 88.0, -87.0, ALU.min, ALU.max))
                link(dve.tensor_scalar(n, f, 1.4426950408889634, MAGIC, ALU.mult, ALU.add))
                link(dve.tensor_scalar(n, n, MAGIC, None, ALU.subtract))
                for part in (0.693359375, -2.12194440e-4):
                    link(dve.scalar_tensor_tensor(out=f, in0=n, scalar=-part, in1=f, op0=ALU.mult, op1=ALU.add))
                polynomial(p, f, [1.0, 1.0, 1 / 2, 1 / 6, 1 / 24, 1 / 120, 1 / 720, 1 / 5040, 1 / 40320])
                link(dve.tensor_scalar(pow2[:, :], n, 127.0, float(2 ** 23), ALU.add, ALU.mult))
                link(dve.tensor_tensor(out, p, pow2[:, :].bitcast(F32), ALU.mult))

            def sine_cosine(sine, cosine, x):
                n, f, y, s, c, j, q, t = (col() for _ in range(8))
                link(dve.tensor_scalar(n, x, 0.6366197723675814, MAGIC, ALU.mult, ALU.add))
                link(dve.tensor_scalar(n, n, MAGIC, None, ALU.subtract))
                link(dve.scalar_tensor_tensor(out=f, in0=n, scalar=-1.5703125, in1=x, op0=ALU.mult, op1=ALU.add))
                for part in (4.837512969970703125e-4, 7.54978995489188216e-8):
                    link(dve.scalar_tensor_tensor(out=f, in0=n, scalar=-part, in1=f, op0=ALU.mult, op1=ALU.add))
                link(dve.tensor_tensor(y, f, f, ALU.mult))
                polynomial(s, y, [1.0, -1 / 6, 1 / 120, -1 / 5040, 1 / 362880])
                link(dve.tensor_tensor(s, s, f, ALU.mult))
                polynomial(c, y, [1.0, -1 / 2, 1 / 24, -1 / 720, 1 / 40320, -1 / 3628800])
                link(dve.tensor_scalar(j, n, 0.25, MAGIC, ALU.mult, ALU.add))
                link(dve.tensor_scalar(j, j, MAGIC, None, ALU.subtract))
                link(dve.scalar_tensor_tensor(out=j, in0=j, scalar=-4.0, in1=n, op0=ALU.mult, op1=ALU.add))
                link(dve.scalar_tensor_tensor(out=t, in0=j, scalar=-1.0, in1=j, op0=ALU.mult, op1=ALU.max))
                link(dve.tensor_scalar(t, t, -1.0, 2.0, ALU.mult, ALU.add))
                link(dve.tensor_tensor(t, t, j, ALU.mult))
                link(dve.tensor_tensor(q, j, j, ALU.mult))
                link(dve.tensor_scalar(q, q, -1.0, 1.0, ALU.mult, ALU.add))
                link(dve.tensor_scalar(q, q, -1.0, None, ALU.max))
                link(dve.tensor_tensor(sine, c, t, ALU.mult))
                link(dve.scalar_tensor_tensor(out=sine, in0=s, scalar=q, in1=sine, op0=ALU.mult, op1=ALU.add))
                link(dve.tensor_tensor(cosine, s, t, ALU.mult))
                link(dve.scalar_tensor_tensor(out=cosine, in0=c, scalar=q, in1=cosine, op0=ALU.mult, op1=ALU.subtract))

            cos, sin, decay = s5["cos"], s5["sin"], s5["decay"]
            dve.wait_ge(ld_ssm, 16 * 8)
            dt, x, r, l_re, l_im, c_re, c_im, mag, u, w = (col() for _ in range(10))
            lr, li = lam[:, 0:1], lam[:, 1:2]
            exponential(dt, lam[:, 2:3])
            link(dve.tensor_tensor(x, lr, dt, ALU.mult))
            exponential(r, x)
            link(dve.tensor_tensor(x, li, dt, ALU.mult))
            sine_cosine(sin[:, 0:1], cos[:, 0:1], x)
            link(dve.tensor_tensor(l_re, r, cos[:, 0:1], ALU.mult))
            link(dve.tensor_tensor(l_im, r, sin[:, 0:1], ALU.mult))
            link(dve.tensor_scalar(l_re, l_re, 1.0, None, ALU.subtract))
            link(dve.tensor_tensor(mag, lr, lr, ALU.mult))
            link(dve.scalar_tensor_tensor(out=mag, in0=li, scalar=li, in1=mag, op0=ALU.mult, op1=ALU.add))
            link(dve.reciprocal(mag, mag))
            link(dve.tensor_tensor(u, l_im, li, ALU.mult))
            link(dve.scalar_tensor_tensor(out=u, in0=l_re, scalar=lr, in1=u, op0=ALU.mult, op1=ALU.add))
            link(dve.tensor_tensor(c_re, u, mag, ALU.mult))
            link(dve.tensor_tensor(w, l_re, li, ALU.mult))
            link(dve.scalar_tensor_tensor(out=w, in0=l_im, scalar=lr, in1=w, op0=ALU.mult, op1=ALU.subtract))
            link(dve.tensor_tensor(c_im, w, mag, ALU.mult))
            link(dve.tensor_scalar(tmp[:, :], b_in[:, 1, :], c_im, None, ALU.mult))
            link(dve.scalar_tensor_tensor(out=b_bar[:, 0, :], in0=b_in[:, 0, :], scalar=c_re, in1=tmp[:, :], op0=ALU.mult, op1=ALU.subtract))
            link(dve.tensor_scalar(tmp[:, :], b_in[:, 0, :], c_im, None, ALU.mult))
            dve.scalar_tensor_tensor(out=b_bar[:, 1, :], in0=b_in[:, 1, :], scalar=c_re, in1=tmp[:, :], op0=ALU.mult, op1=ALU.add).then_inc(bbar_ready, 1)
            dve.wait_ge(d_tp, 1)
            link(dve.tensor_copy(d_col[:, :], psum[:, 7, 0:KT]))
            dve.wait_ge(ident_ready, 2)
            for k in range(KT):
                link(dve.tensor_scalar(s5["d_hi"][:, k, :], ident[:, :], d_col[:, k:k + 1], None, ALU.mult))
                dve.scalar_tensor_tensor(out=s5["d_lo"][:, k, :], in0=ident[:, :], scalar=d_col[:, k:k + 1],
                                         in1=s5["d_hi"][:, k, :].bitcast(F32), op0=ALU.mult, op1=ALU.subtract).then_inc(d_ready, 1)
            for n, times in enumerate((2.0, -2.0)):
                dve.wait_ge(bc_hi, n + 1)
                dve.scalar_tensor_tensor(out=s5["c_lo"][:, n, :], in0=psum[:, n, :], scalar=times, in1=s5["c_hi"][:, n, :].bitcast(F32),
                                         op0=ALU.mult, op1=ALU.subtract).then_inc(bc_lo, 1)
            for n in range(2):
                dve.wait_ge(bc_hi, 3 + n)
                dve.tensor_tensor(s5["b_lo"][:, :, n * P:(n + 1) * P], psum[:, 2 + n, :].rearrange("p (k s) -> p k s", s=P),
                                  s5["b_hi"][:, :, n * P:(n + 1) * P].bitcast(F32), ALU.subtract).then_inc(bc_lo, 1)
            dve.memset(decay[:, :], 1.0).then_inc(chain, 1)
            done[0] += 1
            dve.wait_ge(chain, done[0])
            link(dve.tensor_scalar(decay[:, :], decay[:, :], r, None, ALU.mult))
            s = 1
            while s < CH:
                w_re, w_im = cos[:, s - 1:s], sin[:, s - 1:s]
                link(dve.tensor_scalar(tmp[:, 0:s], sin[:, 0:s], w_im, None, ALU.mult))
                link(dve.scalar_tensor_tensor(out=cos[:, s:2 * s], in0=cos[:, 0:s], scalar=w_re, in1=tmp[:, 0:s], op0=ALU.mult, op1=ALU.subtract))
                link(dve.tensor_scalar(tmp[:, 0:s], sin[:, 0:s], w_re, None, ALU.mult))
                link(dve.scalar_tensor_tensor(out=sin[:, s:2 * s], in0=cos[:, 0:s], scalar=w_im, in1=tmp[:, 0:s], op0=ALU.mult, op1=ALU.add))
                s *= 2
            dve.wait_ge(ld_row, 16 * (1 + 6 * B))
            for n in range(10):
                dve.wait_ge(sec_ready, n + 1)
                dve.tensor_tensor(mod[:, n, :], psum[0:B, 4 + n % 2, :], bias[:, n, :], ALU.add).then_inc(sec_read, 1)
            dve.wait_ge(sec_read, 10)
            shift_a, scale_a, gate_a, shift_f, scale_f, gate_f, scale_c, shift_c, gamma, beta = (mod[:, n, :] for n in range(10))
            link(dve.tensor_scalar(vec[:, V_GAIN_A, :], scale_a, 1.0, None, ALU.add))
            link(dve.tensor_copy(vec[:, V_SHIFT_A, :], shift_a))
            link(dve.tensor_scalar(scale_f, scale_f, 1.0, None, ALU.add))
            link(dve.scalar_tensor_tensor(out=vec[:, V_GAIN_F, :], in0=scale_c, scalar=1.0, in1=scale_f, op0=ALU.add, op1=ALU.mult))
            link(dve.tensor_tensor(shift_c, shift_c, scale_f, ALU.mult))
            link(dve.tensor_tensor(vec[:, V_SHIFT_F, :], shift_c, shift_f, ALU.add))
            link(dve.tensor_tensor(vec[:, V_GAIN_1, :], gamma, ln_gb[:, 0, :], ALU.mult))
            link(dve.tensor_tensor(gamma, gamma, ln_gb[:, 1, :], ALU.mult))
            link(dve.tensor_tensor(vec[:, V_SHIFT_1, :], gamma, beta, ALU.add))
            link(dve.tensor_copy(vec[:, V_GATE_A, :], gate_a))
            dve.tensor_copy(vec[:, V_GATE_F, :], gate_f).then_inc(vec_ready, 1)


def s5_stage(nc, sb, sem, psum, a, ident, columns, s5, vec_dram, y_dram):
    x = [sb(f"x{b}", [P, TT, D]) for b in range(B)]
    y = [sb(f"y{b}", [P, TT, D]) for b in range(B)]
    norm = sb("norm", [P, TT, D])
    gate = [sb(f"gate{b}", [P, D]) for b in range(B)]
    stats = sb("stats", [P, TT, 6])
    root, inv, off, mean2, var, diff = (sb(f"ln_{n}", [P, TT]) for n in ("root", "inv", "off", "mean2", "var", "diff"))
    u = [sb(f"u{n}", [P, CH]) for n in range(2)]
    u_hi = [sb(f"u_hi{b}", [P, KT, CH], F32R) for b in range(B)]
    u_lo = [sb(f"u_lo{b}", [P, KT, CH], F32R) for b in range(B)]
    prod = sb("prod", [P, 4, CH])
    turned = sb("turned", [P, 2, CH])
    scan = sb("scan", [P, 2, CH])
    state = [sb(f"state{b}", [P, 2, CH]) for b in range(B)]
    s_hi, s_lo = sb("s_hi", [P, 2, CH], F32R), sb("s_lo", [P, 2, CH], F32R)
    gated = [sb(f"gated{n}", [P, D]) for n in range(2)]

    x_ld, y_ld, y_st = ([sem(f"s5_{n}{b}") for b in range(B)] for n in ("x_ld", "y_ld", "y_st"))
    gate_ld, start = sem("s5_gate_ld"), sem("s5_start")
    stat, root_ready, ln_chain, norm_ready = sem("s5_stat"), sem("s5_root"), sem("s5_ln_chain"), sem("s5_norm")
    tr_ready, u_ready, uhi_ready = sem("s5_tr"), sem("s5_u"), sem("s5_uhi")
    ulo_even, ulo_odd = sem("s5_ulo_even"), sem("s5_ulo_odd")
    bu_ready, prod_ready, turned_ready, scan_ready = sem("s5_bu"), sem("s5_prod"), sem("s5_turned"), sem("s5_scan")
    back_ready, state_ready, shi_ready, slo_ready = sem("s5_back"), sem("s5_state"), sem("s5_shi"), sem("s5_slo")
    cy_ready, gated_ready, y_ready = sem("s5_cy"), sem("s5_gated"), sem("s5_y")

    cos, sin, decay = s5["cos"], s5["sin"], s5["decay"]
    TR, BU, CY = 0, 2, 6
    PROD_FREE, U_FREE, GATED_FREE, Y_FREE = 4, 2, 2, 2

    def chunk(dram, i, b):
        return dram.rearrange("b l d -> (b l) d")[bass.ds(b * L + i * CH, CH)].rearrange("(t p) d -> p t d", p=P)

    def steps(engine, step):
        step(0, 0, None, (0, 1), (1, 0))
        with engine.Fori(0, NCH - 2) as i:
            step(i, 1, (i, 0), (i + 1, 0), (i + 1, 1))
            step(i + 1, 0, (i, 1), (i + 1, 1), (i + 2, 0))
        step(NCH - 2, 1, (NCH - 2, 0), (NCH - 1, 0), (NCH - 1, 1))
        step(NCH - 1, 0, (NCH - 2, 1), (NCH - 1, 1), None)
        step(NCH - 1, 1, (NCH - 1, 0), None, None)

    with nc.Block() as block:
        @block.sync
        def _(sp):
            def load_x(i, b):
                sp.dma_start(x[b][:, :, :], chunk(a["x"], i, b)).then_inc(x_ld[b], 16)

            def load_y(i, b):
                wait_count(sp, y_st[b], 16 * i)
                sp.dma_start(y[b][:, :, :], chunk(a["x"], i, b)).then_inc(y_ld[b], 16)

            def store(i, b):
                sp.wait_ge(y_ready, Y_FREE + TT * (B * i + b + 1))
                sp.dma_start(chunk(y_dram, i, b), y[b][:, :, :]).then_inc(y_st[b], 16)

            def step(i, b, previous, following, second):
                if second:
                    sp.wait_ge(norm_ready, B * i + b + 1)
                    load_x(*second)
                load_y(i, b)
                if previous:
                    store(*previous)

            for b in range(B):
                load_x(0, b)
            for b in range(B):
                sp.dma_start(gate[b][:, :], vec_dram[V_GATE_A, b:b + 1, :].broadcast_to((P, D))).then_inc(gate_ld, 16)
            steps(sp, step)
            store(NCH - 1, 1)
            for b in range(B):
                sp.wait_ge(y_st[b], 16 * NCH)

        @block.tensor
        def _(pe):
            def turn(i, b):
                c = B * i + b
                pe.wait_ge(norm_ready, c + 1)
                for k in range(KT):
                    pe.wait_ge(u_ready, KT * c + k - 1 + U_FREE)
                    for t in range(TT):
                        mm = pe.transpose(psum[:, TR + k % 2, t * P:(t + 1) * P], norm[:, t, k * P:(k + 1) * P], ident[:, :])
                    mm.then_inc(tr_ready, 1)

            def project_in(i, b):
                c = B * i + b
                wait_count(pe, prod_ready, 4 * (c - 1) + PROD_FREE)
                for k in range(KT):
                    pe.wait_ge((ulo_even, ulo_odd)[k % 2], KT // 2 * c + k // 2 + 1)
                    for n in range(2):
                        mm = split_matmuls(nc, psum[:, BU + 2 * b + n, :], s5["b_hi"][:, k, n * P:(n + 1) * P],
                                           s5["b_lo"][:, k, n * P:(n + 1) * P], u_hi[b][:, k, :], u_lo[b][:, k, :], k == 0, k == KT - 1)
                mm.then_inc(bu_ready, 1)

            def project_out(i, b):
                c = B * i + b
                for t in range(TT):
                    pe.wait_ge(gated_ready, TT * c + t - 1 + GATED_FREE)
                    tok = slice(t * P, (t + 1) * P)
                    out = psum[:, CY + t % 2, :]
                    for n in range(2):
                        if t == 0:
                            pe.wait_ge(slo_ready, 2 * c + n + 1)
                        split_matmuls(nc, out, s_hi[:, n, tok], s_lo[:, n, tok], s5["c_hi"][:, n, :], s5["c_lo"][:, n, :], n == 0, False)
                    for k in range(KT):
                        mm = split_matmuls(nc, out[:, k * P:(k + 1) * P], u_hi[b][:, k, tok], u_lo[b][:, k, tok],
                                           s5["d_hi"][:, k, :], s5["d_lo"][:, k, :], False, k == KT - 1)
                    mm.then_inc(cy_ready, 1)

            def step(i, b, previous, following, second):
                project_in(i, b)
                if previous:
                    project_out(*previous)
                if following:
                    turn(*following)

            turn(0, 0)
            steps(pe, step)
            project_out(NCH - 1, 1)

        @block.scalar
        def _(act):
            act.sem_inc(u_ready, U_FREE)

            def take_root(i, b):
                c = B * i + b
                act.wait_ge(stat, MOMENT_STEPS * (c + 1))
                act.activation(root[:, :], var[:, :], ACT.Sqrt).then_inc(root_ready, 1)

            def split(i, b):
                c = B * i + b
                for k in range(KT):
                    act.wait_ge(tr_ready, KT * c + k + 1)
                    wait_count(act, (ulo_even, ulo_odd)[k % 2], KT // 2 * c + k // 2)
                    act.activation(u[k % 2][:, :], psum[:, TR + k % 2, :], ACT.Identity, scale=columns[:, V_GAIN_A, k, b:b + 1],
                                   bias=columns[:, V_SHIFT_A, k, b:b + 1]).then_inc(u_ready, 1)
                    act.wait_ge(u_ready, KT * c + k + 1 + U_FREE)
                    wait_count(act, cy_ready, TT * (c - 1))
                    act.activation(u_hi[b][:, k, :], u[k % 2][:, :], ACT.Copy).then_inc(uhi_ready, 1)

            def step(i, b, previous, following, second):
                c = B * i + b
                for n in range(2):
                    act.wait_ge(state_ready, 2 * c + n + 1)
                    wait_count(act, cy_ready, TT * c)
                    act.activation(s_hi[:, n, :], state[b][:, n, :], ACT.Copy).then_inc(shi_ready, 1)
                if following:
                    split(*following)
                if second:
                    take_root(*second)

            take_root(0, 0)
            split(0, 0)
            take_root(0, 1)
            steps(act, step)

        @block.vector
        def _(dve):
            dve.sem_inc(prod_ready, PROD_FREE)
            dve.sem_inc(gated_ready, GATED_FREE)
            for b in range(B):
                dve.memset(state[b][:, :, CH - 1:CH], 0.0).then_inc(start, 1)
            dve.wait_ge(start, B)

            def moments(i, b):
                c = B * i + b
                dve.wait_ge(x_ld[b], 16 * (i + 1))
                wait_count(dve, ln_chain, INVERSE_STEPS * c)
                ln_moments(dve, x[b], stats, mean2, var, diff, stat, MOMENT_STEPS * c)

            def normalise(i, b):
                c = B * i + b
                dve.wait_ge(root_ready, c + 1)
                ln_inverse(dve, root, mean2, var, inv, off, ln_chain, INVERSE_STEPS * c)
                dve.wait_ge(ln_chain, INVERSE_STEPS * (c + 1))
                wait_count(dve, tr_ready, KT * c)
                for t in range(TT):
                    nrm = dve.tensor_scalar(norm[:, t, :], x[b][:, t, :], inv[:, t:t + 1], off[:, t:t + 1], ALU.mult, ALU.add)
                nrm.then_inc(norm_ready, 1)

            def split(i, b):
                c = B * i + b
                for k in range(1, KT, 2):
                    dve.wait_ge(uhi_ready, KT * c + k + 1)
                    dve.tensor_tensor(u_lo[b][:, k, :], u[k % 2][:, :], u_hi[b][:, k, :].bitcast(F32), ALU.subtract).then_inc(ulo_odd, 1)

            def apply_gate(i, b, t):
                c = B * i + b
                dve.wait_ge(cy_ready, TT * c + t + 1)
                dve.wait_ge(y_ready, TT * c + t - 1 + Y_FREE)
                dve.tensor_tensor(gated[t % 2][:, :], psum[:, CY + t % 2, :], gate[b][:, :], ALU.mult).then_inc(gated_ready, 1)

            def step(i, b, previous, following, second):
                c = B * i + b
                if following:
                    normalise(*following)
                re, im = psum[:, BU + 2 * b, :], psum[:, BU + 2 * b + 1, :]
                dve.wait_ge(bu_ready, c + 1)
                wait_count(dve, state_ready, 2 * c)
                for n, (v, table) in enumerate(((re, cos), (im, sin), (im, cos), (re, sin))):
                    dve.tensor_tensor(prod[:, n, :], v, table[:, :], ALU.mult).then_inc(prod_ready, 1)
                if previous:
                    apply_gate(*previous, 0)
                for n in range(2):
                    dve.wait_ge(turned_ready, 2 * c + n + 1)
                    wait_count(dve, back_ready, 4 * c)
                    dve.tensor_tensor_scan(scan[:, n, :], decay[:, :], turned[:, n, :], state[b][:, n, CH - 1:CH],
                                           ALU.mult, ALU.add).then_inc(scan_ready, 1)
                if previous:
                    apply_gate(*previous, 1)
                dve.wait_ge(scan_ready, 2 * (c + 1))
                for n, (v, table) in enumerate(((0, cos), (1, sin), (1, cos), (0, sin))):
                    dve.tensor_tensor(prod[:, n, :], scan[:, v, :], table[:, :], ALU.mult).then_inc(back_ready, 1)
                if second:
                    moments(*second)
                if previous:
                    for t in range(2, TT):
                        apply_gate(*previous, t)
                if following:
                    split(*following)

            moments(0, 0)
            normalise(0, 0)
            moments(0, 1)
            split(0, 0)
            dve.wait_ge(gate_ld, 16 * B)
            steps(dve, step)
            for t in range(TT):
                apply_gate(NCH - 1, 1, t)

        @block.gpsimd
        def _(pool):
            pool.sem_inc(y_ready, Y_FREE)

            def split(i, b, k):
                c = B * i + b
                pool.wait_ge(uhi_ready, KT * c + k + 1)
                pool.tensor_tensor(u_lo[b][:, k, :], u[k % 2][:, :], u_hi[b][:, k, :].bitcast(F32), ALU.subtract).then_inc(ulo_even, 1)

            def add(i, b, t):
                c = B * i + b
                if t == 0:
                    pool.wait_ge(y_ld[b], 16 * (i + 1))
                pool.wait_ge(gated_ready, TT * c + t + 1 + GATED_FREE)
                pool.tensor_tensor(y[b][:, t, :], gated[t % 2][:, :], y[b][:, t, :], ALU.add).then_inc(y_ready, 1)

            def step(i, b, previous, following, second):
                c = B * i + b
                for n, op in enumerate((ALU.add, ALU.subtract)):
                    pool.wait_ge(prod_ready, 4 * c + 2 * n + 2 + PROD_FREE)
                    wait_count(pool, scan_ready, 2 * c)
                    pool.tensor_tensor(turned[:, n, :], prod[:, 2 * n, :], prod[:, 2 * n + 1, :], op).then_inc(turned_ready, 1)
                if previous:
                    add(*previous, 0)
                    add(*previous, 1)
                for n, op in enumerate((ALU.subtract, ALU.add)):
                    pool.wait_ge(back_ready, 4 * c + 2 * n + 2)
                    wait_count(pool, shi_ready, 2 * c)
                    pool.tensor_tensor(state[b][:, n, :], prod[:, 2 * n, :], prod[:, 2 * n + 1, :], op).then_inc(state_ready, 1)
                for n in range(2):
                    pool.wait_ge(shi_ready, 2 * c + n + 1)
                    pool.tensor_tensor(s_lo[:, n, :], state[b][:, n, :], s_hi[:, n, :].bitcast(F32), ALU.subtract).then_inc(slo_ready, 1)
                    if following:
                        split(*following, 2 * n)
                if previous:
                    for t in range(2, TT):
                        add(*previous, t)

            for k in range(0, KT, 2):
                split(0, 0, k)
            steps(pool, step)
            for t in range(TT):
                add(NCH - 1, 1, t)




def ffn_stage(nc, sb, sem, psum, a, ident, columns, vec_dram, y_dram, z_dram):
    w1_hi, w1_lo = (sb(f"w1_{n}", [P, KT, FF], F32R) for n in ("hi", "lo"))
    w2_hi, w2_lo = (sb(f"w2_{n}", [P, FT, D], F32R) for n in ("hi", "lo"))
    y = [sb(f"ffn_y{b}", [P, TT, D]) for b in range(B)]
    norm = sb("ffn_norm", [P, TT, D])
    gate = [sb(f"ffn_gate{b}", [P, D]) for b in range(B)]
    stats = sb("ffn_stats", [P, TT, 6])
    root, inv, off, mean2, var, diff = (sb(f"ffn_ln_{n}", [P, TT]) for n in ("root", "inv", "off", "mean2", "var", "diff"))
    u = [sb(f"ffn_u{n}", [P, CH]) for n in range(2)]
    u_hi = sb("ffn_u_hi", [P, KT, CH], F32R)
    u_lo = sb("ffn_u_lo", [P, KT, CH], F32R)
    b1_rows = sb("b1_rows", [FT, P])
    b1_col = sb("b1_col", [P, FT])
    b2_row = sb("b2_row", [1, D])
    b2_parts = sb("b2_parts", [P, D], F32R)
    ones_parts = sb("ones_parts", [P, P], F32R)
    NG_ = 2
    g = [sb(f"gelu{n}", [P, CH]) for n in range(NG_)]
    NH = 2
    h_hi = [sb(f"h_hi{n}", [P, CH], F32R) for n in range(NH)]
    h_lo = [sb(f"h_lo{n}", [P, CH], F32R) for n in range(NH)]
    gated = [sb(f"ffn_gated{n}", [P, D]) for n in range(2)]

    w_ld = [sem(f"ffn_w_ld{n}") for n in range(2)]
    y_ld = [sem(f"ffn_y_ld{b}") for b in range(B)]
    z_st = [sem(f"ffn_z_st{b}") for b in range(B)]
    small_ld, b1_tp, consts = (sem(f"ffn_{n}") for n in ("small_ld", "b1_tp", "consts"))
    whi_ready, wlo_ready = sem("ffn_whi"), sem("ffn_wlo")
    stat, root_ready, ln_chain, norm_ready = (sem(f"ffn_{n}") for n in ("stat", "root", "ln_chain", "norm"))
    tr_ready, uhi_ready, u_ready, ulo_ready = (sem(f"ffn_{n}") for n in ("tr", "uhi", "u", "ulo"))
    h_ready, g_ready, ghi_ready, glo_ready = (sem(f"ffn_{n}") for n in ("h", "g", "ghi", "glo"))
    down_ready, acc_ready, gated_ready, z_ready = (sem(f"ffn_{n}") for n in ("down", "acc", "gated", "z"))

    ACC, H, TR = 0, 4, 6
    NW = 2 * KT
    C1 = FF // KT

    def chunk(dram, i, b):
        return dram[b].rearrange("(i t p) d -> i p t d", p=P, t=TT)[bass.ds(i, 1)].rearrange("o p t d -> (o p) t d")

    def piece(n):
        if n < KT:
            return a["L0_cond_W1"][n * P:(n + 1) * P, :]
        return a["L0_cond_W2"][(n - KT) * TT * P:(n - KT + 1) * TT * P, :].rearrange("(f p) d -> p f d", p=P)

    def raw(n):
        return y[n % 2].rearrange("p t d -> p (t d)") if n < KT else y[n % 2][:, :, :]

    def place(hi, n):
        w1, w2 = (w1_hi, w2_hi) if hi else (w1_lo, w2_lo)
        return w1[:, n, :] if n < KT else w2[:, (n - KT) * TT:(n - KT + 1) * TT, :]

    def steps(engine, front, back):
        front(0, 0)
        with engine.Fori(0, NCH - 1) as i:
            back(i, 0, lambda: front(i, 1))
            back(i, 1, lambda: front(i + 1, 0))
        back(NCH - 1, 0, lambda: front(NCH - 1, 1))
        back(NCH - 1, 1, None)

    with nc.Block() as block:
        @block.sync
        def _(sp):
            sp.dma_start(b1_rows[:, :], a["L0_cond_b1"].rearrange("(f p) -> f p", p=P)).then_inc(small_ld, 16)
            sp.dma_start(b2_row[:, :], a["L0_cond_b2"].rearrange("(o d) -> o d", o=1)).then_inc(small_ld, 16)
            for b in range(B):
                sp.dma_start(gate[b][:, :], vec_dram[V_GATE_F, b:b + 1, :].broadcast_to((P, D))).then_inc(small_ld, 16)
            for n in range(NW):
                if n >= 2:
                    sp.wait_ge(whi_ready, n - 1)
                    sp.wait_ge(wlo_ready, n - 1)
                sp.dma_start(raw(n), piece(n)).then_inc(w_ld[n % 2], 16)
            for b in range(B):
                sp.wait_ge(whi_ready, NW - 1 + b)
                sp.wait_ge(wlo_ready, NW - 1 + b)
                sp.dma_start(y[b][:, :, :], chunk(y_dram, 0, b)).then_inc(y_ld[b], 16)

            def store(i, b):
                sp.wait_ge(z_ready, TT * (2 * i + b + 1))
                sp.dma_start(chunk(z_dram, i, b), y[b][:, :, :]).then_inc(z_st[b], 16)

            with sp.Fori(0, NCH - 1) as i:
                for b in range(B):
                    store(i, b)
                    sp.wait_ge(z_st[b], 16 * (i + 1))
                    sp.dma_start(y[b][:, :, :], chunk(y_dram, i + 1, b)).then_inc(y_ld[b], 16)
            for b in range(B):
                store(NCH - 1, b)
            for b in range(B):
                sp.wait_ge(z_st[b], 16 * NCH)

        @block.tensor
        def _(pe):
            pe.wait_ge(small_ld, 16 * (2 + B))
            pe.transpose(psum[:, TR, 0:FT], b1_rows[:, :], ident[0:FT, 0:FT]).then_inc(b1_tp, 1)
            pe.wait_ge(consts, 1)

            def front(i, b):
                c = 2 * i + b
                pe.wait_ge(norm_ready, c + 1)
                for k in range(KT):
                    pe.wait_ge(u_ready, KT * c + k + 1)
                    for t in range(TT):
                        mm = pe.transpose(psum[:, TR + k % 2, t * P:(t + 1) * P], norm[:, t, k * P:(k + 1) * P], ident[:, :])
                    mm.then_inc(tr_ready, 1)

            def up(c, j):
                if j == 0:
                    pe.wait_ge(uhi_ready, KT * (c + 1))
                    pe.wait_ge(ulo_ready, KT * (c + 1) + 2)
                pe.wait_ge(g_ready, FT * c + j + 1)
                for k in range(KT):
                    f = slice(j * P, (j + 1) * P)
                    mm = split_matmuls(nc, psum[:, H + j % 2, :], w1_hi[:, k, f], w1_lo[:, k, f], u_hi[:, k, :], u_lo[:, k, :],
                                       k == 0, k == KT - 1)
                mm.then_inc(h_ready, 1)

            def down(c, j):
                pe.wait_ge(ghi_ready, FT * c + j + 1)
                pe.wait_ge(glo_ready, FT * c + j + 1)
                for t in range(TT):
                    tok = slice(t * P, (t + 1) * P)
                    if j == 0:
                        pe.wait_ge(gated_ready, TT * c + t + 1)
                        pe.matmul(psum[:, ACC + t, :], ones_parts[:, :], b2_parts[:, :], start=True, stop=False)
                    mm = split_matmuls(nc, psum[:, ACC + t, :], h_hi[j % NH][:, tok], h_lo[j % NH][:, tok], w2_hi[:, j, :], w2_lo[:, j, :],
                                       False, j == FT - 1)
                    if j == FT - 1:
                        mm.then_inc(acc_ready, 1)
                if j < FT - 1:
                    mm.then_inc(down_ready, 1)

            def back(i, b, following):
                c = 2 * i + b
                for j in range(FT):
                    up(c, j)
                    if j == FT - 1 and following:
                        following()
                    if j >= 1:
                        down(c, j - 1)
                down(c, FT - 1)

            pe.wait_ge(consts, 7)
            pe.wait_ge(whi_ready, NW)
            pe.wait_ge(wlo_ready, NW)
            steps(pe, front, back)

        @block.scalar
        def _(act):
            act.sem_inc(u_ready, 2)
            act.sem_inc(g_ready, 2)
            for n in range(NW):
                act.wait_ge(w_ld[n % 2], 16 * (n // 2 + 1))
                act.activation(place(True, n), raw(n), ACT.Copy).then_inc(whi_ready, 1)
            act.wait_ge(consts, 1)

            def front(i, b):
                c = 2 * i + b
                act.wait_ge(stat, MOMENT_STEPS * (c + 1))
                act.activation(root[:, :], var[:, :], ACT.Sqrt).then_inc(root_ready, 1)

            def split(i, b):
                c = 2 * i + b
                for k in range(KT):
                    act.wait_ge(tr_ready, KT * c + k + 1)
                    act.wait_ge(ulo_ready, KT * c + k + 1)
                    act.activation(u[k % 2][:, :], psum[:, TR + k % 2, :], ACT.Identity, scale=columns[:, V_GAIN_F, k, b:b + 1],
                                   bias=columns[:, V_SHIFT_F, k, b:b + 1]).then_inc(u_ready, 1)

            def gelu(c, j):
                act.wait_ge(h_ready, FT * c + j + 1)
                act.wait_ge(glo_ready, FT * c + max(j - NG_ + 1, 0))
                act.activation(g[j % NG_][:, :], psum[:, H + j % 2, :], ACT.Gelu_apprx_tanh, bias=b1_col[:, j:j + 1]).then_inc(g_ready, 1)
                act.wait_ge(g_ready, FT * c + j + 3)
                if j == 1:
                    act.wait_ge(acc_ready, TT * c)
                else:
                    act.wait_ge(down_ready, (FT - 1) * c + max(j - NH + 1, 0))
                act.activation(h_hi[j % NH][:, :], g[j % NG_][:, :], ACT.Copy).then_inc(ghi_ready, 1)

            front(0, 0)
            split(0, 0)
            def back(i, b, nxt):
                c = 2 * i + b
                for j in range(FT):
                    if j == 6 and nxt:
                        front(*nxt)
                    gelu(c, j)
                if nxt:
                    split(*nxt)

            with act.Fori(0, NCH - 1) as i:
                back(i, 0, (i, 1))
                back(i, 1, (i + 1, 0))
            back(NCH - 1, 0, (NCH - 1, 1))
            back(NCH - 1, 1, None)

        @block.vector
        def _(dve):
            dve.sem_inc(gated_ready, TT)
            dve.wait_ge(b1_tp, 1)
            dve.tensor_copy(b1_col[:, :], psum[:, TR, 0:FT]).then_inc(consts, 1)
            dve.memset(ones_parts[:, :].bitcast(F32), 0.0).then_inc(consts, 1)
            dve.memset(b2_parts[:, :].bitcast(F32), 0.0).then_inc(consts, 1)
            dve.wait_ge(consts, 3)
            for r in (0, 32):
                dve.memset(ones_parts[r:r + 1, :].bitcast(F32), 1.0).then_inc(consts, 1)
            dve.tensor_copy(b2_parts[0:1, :], b2_row[:, :]).then_inc(consts, 1)
            dve.wait_ge(consts, 6)
            dve.tensor_tensor(b2_parts[32:33, :], b2_row[:, :], b2_parts[0:1, :].bitcast(F32), ALU.subtract).then_inc(consts, 1)
            for n in range(NW):
                dve.wait_ge(whi_ready, n + 1)
                dve.tensor_tensor(place(False, n), raw(n), place(True, n).bitcast(F32), ALU.subtract).then_inc(wlo_ready, 1)

            def moments(i, b):
                c = 2 * i + b
                dve.wait_ge(y_ld[b], 16 * (i + 1))
                ln_moments(dve, y[b], stats, mean2, var, diff, stat, MOMENT_STEPS * c)

            def normalise(i, b):
                c = 2 * i + b
                dve.wait_ge(root_ready, c + 1)
                ln_inverse(dve, root, mean2, var, inv, off, ln_chain, INVERSE_STEPS * c)
                dve.wait_ge(ln_chain, INVERSE_STEPS * (c + 1))
                dve.wait_ge(tr_ready, KT * c)
                for t in range(TT):
                    nrm = dve.tensor_scalar(norm[:, t, :], y[b][:, t, :], inv[:, t:t + 1], off[:, t:t + 1], ALU.mult, ALU.add)
                nrm.then_inc(norm_ready, 1)

            def split(i, b):
                c = 2 * i + b
                for k in range(KT):
                    dve.wait_ge(u_ready, KT * c + k + 3)
                    dve.tensor_copy(u_hi[:, k, :], u[k % 2][:, :]).then_inc(uhi_ready, 1)

            def back(i, b, nxt):
                c = 2 * i + b
                for j in range(FT):
                    if j == 4 and nxt:
                        moments(*nxt)
                    if j == 6 and nxt:
                        normalise(*nxt)
                    dve.wait_ge(ghi_ready, FT * c + j + 1)
                    dve.tensor_tensor(h_lo[j % NH][:, :], g[j % NG_][:, :], h_hi[j % NH][:, :].bitcast(F32), ALU.subtract).then_inc(glo_ready, 1)
                if nxt:
                    split(*nxt)
                for t in range(TT):
                    dve.wait_ge(acc_ready, TT * c + t + 1)
                    dve.wait_ge(z_ready, TT * c + max(t - 1, 0))
                    dve.tensor_tensor(gated[t % 2][:, :], psum[:, ACC + t, :], gate[b][:, :], ALU.mult).then_inc(gated_ready, 1)

            moments(0, 0)
            normalise(0, 0)
            split(0, 0)
            with dve.Fori(0, NCH - 1) as i:
                back(i, 0, (i, 1))
                back(i, 1, (i + 1, 0))
            back(NCH - 1, 0, (NCH - 1, 1))
            back(NCH - 1, 1, None)

        @block.gpsimd
        def _(pool):
            pool.sem_inc(ulo_ready, 2)

            def split(i, b):
                c = 2 * i + b
                for k in range(KT):
                    pool.wait_ge(uhi_ready, KT * c + k + 1)
                    pool.tensor_tensor(u_lo[:, k, :], u[k % 2][:, :], u_hi[:, k, :].bitcast(F32), ALU.subtract).then_inc(ulo_ready, 1)

            def back(i, b, nxt):
                c = 2 * i + b
                if nxt:
                    split(*nxt)
                for t in range(TT):
                    pool.wait_ge(gated_ready, TT * c + t + 1 + TT)
                    pool.tensor_tensor(y[b][:, t, :], gated[t % 2][:, :], y[b][:, t, :], ALU.add).then_inc(z_ready, 1)

            split(0, 0)
            with pool.Fori(0, NCH - 1) as i:
                back(i, 0, (i, 1))
                back(i, 1, (i + 1, 0))
            back(NCH - 1, 0, (NCH - 1, 1))
            back(NCH - 1, 1, None)


def qkv_stage(nc, sb, sem, psum, a, ident, columns, z_dram, q_dram, k_dram, v_dram):
    wt_hi, wt_lo = (sb(f"wqkv_{n}", [P, KT, 3 * D], F32R) for n in ("hi", "lo"))
    w_raw = [sb(f"wqkv_raw{n}", [P, KT, D]) for n in range(3)]
    z = [sb(f"qkv_z{b}", [P, TT, D]) for b in range(B)]
    norm = sb("qkv_norm", [P, TT, D])
    stats = sb("qkv_stats", [P, TT, 6])
    root, inv, off, mean2, var, diff = (sb(f"qkv_ln_{n}", [P, TT]) for n in ("root", "inv", "off", "mean2", "var", "diff"))
    u = [sb(f"qkv_u{n}", [P, CH]) for n in range(2)]
    u_hi = [sb(f"qkv_u_hi{b}", [P, KT, CH], F32R) for b in range(B)]
    u_lo = [sb(f"qkv_u_lo{b}", [P, KT, CH], F32R) for b in range(B)]
    NO = 4
    o_hi = [sb(f"qk_hi{n}", [P, CH], F32R) for n in range(NO)]
    o_lo = [sb(f"qk_lo{n}", [P, CH], F32R) for n in range(NO)]
    v_out = [sb(f"v_out{n}", [P, D]) for n in range(2)]
    b_nat = sb("bqkv_nat", [1, 3 * D])
    b_sorted = sb("bqkv_sorted", [1, 3 * D])
    b_col = sb("bqkv_col", [P, 2 * KT])
    bv_parts = sb("bv_parts", [P, D], F32R)
    bqkv_ones = sb("bqkv_ones", [P, P], F32R)

    w_ld, small_ld = sem("qkv_w_ld"), sem("qkv_small_ld")
    z_ld = [sem(f"qkv_z_ld{b}") for b in range(B)]
    o_st = [sem(f"qk_st{n}") for n in range(NO)]
    v_st = [sem(f"v_st{n}") for n in range(2)]
    b_tp, consts = sem("qkv_b_tp"), sem("qkv_consts")
    wt_tp, whi_ready, wlo_ready = sem("qkv_wt"), sem("qkv_whi"), sem("qkv_wlo")
    stat, root_ready, ln_chain, norm_ready = (sem(f"qkv_{n}") for n in ("stat", "root", "ln_chain", "norm"))
    tr_ready, uhi_ready, u_ready, ulo_ready = (sem(f"qkv_{n}") for n in ("tr", "uhi", "u", "ulo"))
    o_ready, ohi_ready, olo_ready = sem("qk_ready"), sem("qk_hi_ready"), sem("qk_lo_ready")
    v_ready, v_copied = sem("v_ready"), sem("v_copied")

    TR, QK, V = 0, 2, 5
    NM = 2 * KT

    def chunk(dram, i, b):
        return dram[b].rearrange("(i t p) d -> i p t d", p=P, t=TT)[bass.ds(i, 1)].rearrange("o p t d -> (o p) t d")

    def steps(engine, front, back):
        front(0, 0)
        with engine.Fori(0, NCH - 1) as i:
            front(i, 1)
            back(i, 0)
            front(i + 1, 0)
            back(i, 1)
        front(NCH - 1, 1)
        back(NCH - 1, 0)
        back(NCH - 1, 1)

    with nc.Block() as block:
        @block.sync
        def _(sp):
            w = a["L1_cond_Wqkv"].rearrange("(m p j) k -> j p m k", p=P, j=3)
            for n in range(3):
                sp.dma_start(w_raw[n][:, :, :], w[n]).then_inc(w_ld, 16)
            sp.dma_start(b_nat[:, :], a["L1_cond_bqkv"].rearrange("(o c) -> o c", o=1)).then_inc(small_ld, 16)
            for b in range(B):
                sp.dma_start(z[b][:, :, :], chunk(z_dram, 0, b)).then_inc(z_ld[b], 16)

            def stores(i, b):
                c = 2 * i + b
                for m in range(NM):
                    sp.wait_ge(ohi_ready, NM * c + m + 1)
                    sp.wait_ge(olo_ready, NM * c + m + 1)
                    dram = (q_dram, k_dram)[m // KT]
                    at = b * L + i * CH
                    for part, tile in enumerate((o_hi[m % NO], o_lo[m % NO])):
                        sp.dma_start(dram[part, (m % KT) * P:(m % KT + 1) * P, bass.ds(at, CH)], tile[:, :].bitcast(F32)).then_inc(o_st[m % NO], 16)
                for t in range(TT):
                    sp.wait_ge(v_copied, TT * c + t + 1 + 2)
                    sp.dma_start(v_dram[bass.ds(b * L + i * CH + t * P, P), :], v_out[t % 2][:, :]).then_inc(v_st[t % 2], 16)

            with sp.Fori(0, NCH - 1) as i:
                for b in range(B):
                    sp.wait_ge(norm_ready, 2 * i + b + 1)
                    sp.dma_start(z[b][:, :, :], chunk(z_dram, i + 1, b)).then_inc(z_ld[b], 16)
                    stores(i, b)
            for b in range(B):
                stores(NCH - 1, b)
            for n in range(NO):
                sp.wait_ge(o_st[n], 16 * 2 * (NM // NO) * B * NCH)
            for n in range(2):
                sp.wait_ge(v_st[n], 16 * (TT // 2) * B * NCH)

        @block.tensor
        def _(pe):
            pe.wait_ge(consts, 7)
            for m in range(NM):
                mm = pe.transpose(psum[:, 7, m:m + 1], b_sorted[:, m * P:(m + 1) * P], ident[0:1, 0:1])
            mm.then_inc(b_tp, 1)
            pe.wait_ge(w_ld, 48)
            for n in range(3 * KT):
                j, k = divmod(n, KT)
                if n >= 6:
                    pe.wait_ge(wlo_ready, n - 5)
                for m in range(KT):
                    mm = pe.transpose(psum[:, n % 6, m * P:(m + 1) * P], w_raw[j][:, m, k * P:(k + 1) * P], ident[:, :])
                mm.then_inc(wt_tp, 1)
            pe.wait_ge(wlo_ready, 3 * KT)
            pe.wait_ge(consts, 9)

            def front(i, b):
                c = 2 * i + b
                pe.wait_ge(norm_ready, c + 1)
                for k in range(KT):
                    pe.wait_ge(u_ready, KT * c + k + 1)
                    for t in range(TT):
                        mm = pe.transpose(psum[:, TR + k % 2, t * P:(t + 1) * P], norm[:, t, k * P:(k + 1) * P], ident[:, :])
                    mm.then_inc(tr_ready, 1)

            def back(i, b):
                c = 2 * i + b
                pe.wait_ge(uhi_ready, KT * (c + 1))
                pe.wait_ge(ulo_ready, KT * (c + 1) + 2)
                for m in range(NM):
                    pe.wait_ge(olo_ready, NM * c + max(m - 2, 0))
                    cols = slice(m * P, (m + 1) * P)
                    for k in range(KT):
                        mm = split_matmuls(nc, psum[:, QK + m % 3, :], wt_hi[:, k, cols], wt_lo[:, k, cols],
                                           u_hi[b][:, k, :], u_lo[b][:, k, :], k == 0, k == KT - 1)
                    mm.then_inc(o_ready, 1)
                for t in range(TT):
                    pe.wait_ge(v_copied, TT * c + t + 1)
                    tok = slice(t * P, (t + 1) * P)
                    nc.tensor.matmul(psum[:, V + t % 2, :], bqkv_ones[:, :], bv_parts[:, :], start=True, stop=False)
                    for k in range(KT):
                        mm = split_matmuls(nc, psum[:, V + t % 2, :], u_hi[b][:, k, tok], u_lo[b][:, k, tok],
                                           wt_hi[:, k, 2 * D:3 * D], wt_lo[:, k, 2 * D:3 * D], False, k == KT - 1)
                    mm.then_inc(v_ready, 1)

            steps(pe, front, back)

        @block.scalar
        def _(act):
            act.sem_inc(u_ready, 2)
            act.sem_inc(v_copied, 2)
            for n in range(3 * KT):
                j, k = divmod(n, KT)
                act.wait_ge(wt_tp, n + 1)
                act.activation(wt_hi[:, k, j * D:(j + 1) * D], psum[:, n % 6, :], ACT.Copy).then_inc(whi_ready, 1)
            act.wait_ge(consts, 10)

            def front(i, b):
                c = 2 * i + b
                act.wait_ge(stat, MOMENT_STEPS * (c + 1))
                act.activation(root[:, :], var[:, :], ACT.Sqrt).then_inc(root_ready, 1)
                for k in range(KT):
                    act.wait_ge(tr_ready, KT * c + k + 1)
                    act.wait_ge(ulo_ready, KT * c + k + 1)
                    act.activation(u[k % 2][:, :], psum[:, TR + k % 2, :], ACT.Identity, scale=columns[:, V_GAIN_1, k, b:b + 1],
                                   bias=columns[:, V_SHIFT_1, k, b:b + 1]).then_inc(u_ready, 1)

            def back(i, b):
                c = 2 * i + b
                for m in range(NM):
                    act.wait_ge(o_ready, NM * c + m + 1)
                    act.wait_ge(o_st[m % NO], 32 * ((NM // NO) * c + m // NO))
                    act.activation(o_hi[m % NO][:, :], psum[:, QK + m % 3, :], ACT.Identity, bias=b_col[:, m:m + 1]).then_inc(ohi_ready, 1)
                for t in range(TT):
                    act.wait_ge(v_ready, TT * c + t + 1)
                    act.wait_ge(v_st[t % 2], 16 * ((TT // 2) * c + t // 2))
                    act.activation(v_out[t % 2][:, :], psum[:, V + t % 2, :], ACT.Copy).then_inc(v_copied, 1)

            steps(act, front, back)

        @block.vector
        def _(dve):
            dve.memset(bqkv_ones[:, :].bitcast(F32), 0.0).then_inc(consts, 1)
            dve.memset(bv_parts[:, :].bitcast(F32), 0.0).then_inc(consts, 1)
            dve.wait_ge(consts, 2)
            for r in (0, 32):
                dve.memset(bqkv_ones[r:r + 1, :].bitcast(F32), 1.0).then_inc(consts, 1)
            dve.wait_ge(small_ld, 16)
            for j in range(3):
                dve.tensor_copy(b_sorted[:, j * D:(j + 1) * D], b_nat[:, :].rearrange("o (c j) -> o j c", j=3)[:, j, :]).then_inc(consts, 1)
            dve.wait_ge(consts, 7)
            dve.tensor_copy(bv_parts[0:1, :], b_sorted[:, 2 * D:3 * D]).then_inc(consts, 1)
            dve.wait_ge(consts, 8)
            dve.tensor_tensor(bv_parts[32:33, :], b_sorted[:, 2 * D:3 * D], bv_parts[0:1, :].bitcast(F32), ALU.subtract).then_inc(consts, 1)
            dve.wait_ge(b_tp, 1)
            dve.tensor_copy(b_col[:, :], psum[:, 7, 0:NM]).then_inc(consts, 1)
            dve.wait_ge(consts, 10)
            for n in range(3 * KT):
                j, k = divmod(n, KT)
                dve.wait_ge(whi_ready, n + 1)
                dve.tensor_tensor(wt_lo[:, k, j * D:(j + 1) * D], psum[:, n % 6, :], wt_hi[:, k, j * D:(j + 1) * D].bitcast(F32),
                                  ALU.subtract).then_inc(wlo_ready, 1)

            def front(i, b):
                c = 2 * i + b
                dve.wait_ge(z_ld[b], 16 * (i + 1))
                ln_moments(dve, z[b], stats, mean2, var, diff, stat, MOMENT_STEPS * c)
                dve.wait_ge(root_ready, c + 1)
                ln_inverse(dve, root, mean2, var, inv, off, ln_chain, INVERSE_STEPS * c)
                dve.wait_ge(ln_chain, INVERSE_STEPS * (c + 1))
                dve.wait_ge(tr_ready, KT * c)
                for t in range(TT):
                    nrm = dve.tensor_scalar(norm[:, t, :], z[b][:, t, :], inv[:, t:t + 1], off[:, t:t + 1], ALU.mult, ALU.add)
                nrm.then_inc(norm_ready, 1)
                for k in range(KT):
                    dve.wait_ge(u_ready, KT * c + k + 3)
                    dve.tensor_copy(u_hi[b][:, k, :], u[k % 2][:, :]).then_inc(uhi_ready, 1)

            def back(i, b):
                c = 2 * i + b
                for m in range(NM):
                    dve.wait_ge(ohi_ready, NM * c + m + 1)
                    dve.scalar_tensor_tensor(out=o_lo[m % NO][:, :], in0=psum[:, QK + m % 3, :], scalar=b_col[:, m:m + 1],
                                             in1=o_hi[m % NO][:, :].bitcast(F32), op0=ALU.add, op1=ALU.subtract).then_inc(olo_ready, 1)

            steps(dve, front, back)

        @block.gpsimd
        def _(pool):
            pool.sem_inc(ulo_ready, 2)

            def front(i, b):
                c = 2 * i + b
                for k in range(KT):
                    pool.wait_ge(uhi_ready, KT * c + k + 1)
                    pool.tensor_tensor(u_lo[b][:, k, :], u[k % 2][:, :], u_hi[b][:, k, :].bitcast(F32), ALU.subtract).then_inc(ulo_ready, 1)

            def back(i, b):
                pass

            steps(pool, front, back)


def attention_stage(nc, sb, sem, psum, q_dram, k_dram, v_dram, att_dram):
    R = 3 * HD
    NKT = L // P
    NKC = L // CH
    NB = 2 * B
    PER_GROUP = B * NCH // NB
    ITERS = NG * PER_GROUP
    PAIRS = NKT // 2
    NPROB = 8
    MAXES = HG * TT * NKC
    SHARES = [4, 5] * (NKT // 2 - 1) + [1, 0]
    AV_LAG, SUM_LAG = 2, 5
    Q_LD, ROW_LD = 3 * 16, 4 * 16

    keys = [sb(f"keys{b}", [P, HG, L], F32R) for b in range(B)]
    queries = [sb(f"queries{n}", [P, HG, CH], F32R) for n in range(NB)]
    values = [sb(f"values{b}", [P, NKT, P]) for b in range(B)]
    ones = sb("att_ones", [P, HD])
    probs = [sb(f"probs{n}", [P, HG, CH]) for n in range(NPROB)]
    pair = [sb(f"pair{n}", [P, HG, CH]) for n in range(2)]
    part_max = sb("part_max", [P, HG * TT, NKC])
    maxima = sb("maxima", [P, 32])
    max_rows = sb("max_rows", [P, 32])
    neg_rows = sb("neg_rows", [P, 32], F32R)
    o_sum, den, att = sb("o_sum", [P, CH]), sb("den", [P, CH]), sb("att", [P, CH])

    k_ld = [[sem(f"k_ld{b}{half}") for half in range(2)] for b in range(B)]
    v_ld = [sem(f"v_ld{b}") for b in range(B)]
    q_ld = [sem(f"q_ld{n}") for n in range(NB)]
    att_st, consts = sem("att_st"), sem("att_consts")
    sc_ready, exp_ready = sem("scores_ready"), sem("exp_ready")
    av_ready, pair_ready, sums_ready = sem("av_ready"), sem("pair_ready"), sem("sums_ready")
    max_ready, max_read, turning, neg_ready = (sem(n) for n in ("max_ready", "max_read", "max_turning", "neg_ready"))
    o_copied, den_copied, inverted, att_ready = (sem(n) for n in ("o_copied", "den_copied", "den_inverted", "att_ready"))

    SC, MX, OUT, DEN = 0, 3, 6, 7
    UNITS = HG * NKT

    def blocks(engine, block):
        block(0, 0, True, False)
        with engine.Fori(0, ITERS - 1) as it:
            for n in range(1, NB):
                block(it, n, False, False)
            block(it + 1, 0, False, False)
        for n in range(1, NB):
            block(ITERS - 1, n, False, n == NB - 1)

    with nc.Block() as block:
        @block.sync
        def _(sp):
            def load_keys(g, b, half):
                src = k_dram.rearrange("e (g h d) t -> e g d h t", h=HG, d=HD)
                at, n_tok = half * (L // 2), L // 2
                for n, part in enumerate((0, 1, 0)):
                    sp.dma_start(keys[b][n * HD:(n + 1) * HD, :, at:at + n_tok].bitcast(F32),
                                 src[part, bass.ds(g, 1), :, :, b * L + at:b * L + at + n_tok].rearrange("o d h t -> (o d) h t")).then_inc(k_ld[b][half], 16)

            def load_values(g, b):
                sp.dma_start(values[b][:, :, :], v_dram[b * L:(b + 1) * L, bass.ds(g * P, P)].rearrange("(n p) c -> p n c", p=P)).then_inc(v_ld[b], 16)

            def load_queries(g, chunk, n):
                src = q_dram.rearrange("e (g h d) t -> e g d h t", h=HG, d=HD)
                at = (n % B) * L + chunk * CH
                for row, part in enumerate((0, 0, 1)):
                    sp.dma_start(queries[n][row * HD:(row + 1) * HD, :, :].bitcast(F32),
                                 src[part, bass.ds(g, 1), :, :, at:at + CH].rearrange("o d h t -> (o d) h t")).then_inc(q_ld[n], 16)

            def load_max_row(count, n):
                sp.wait_ge(neg_ready, count + 1)
                row = queries[n][R:R + 1, :, :].bitcast(F32).rearrange("o h (t r i) -> o (h t) r i", r=4, i=32)
                for r in range(4):
                    sp.dma_start(row[:, :, r, :], neg_rows[32 * r:32 * r + HG * TT, :].bitcast(F32)).then_inc(q_ld[n], 16)

            def store(count, g, chunk, b):
                sp.wait_ge(att_ready, count + 2)
                sp.dma_start(att_dram[bass.ds(g * P, P), b * L + chunk * CH:b * L + (chunk + 1) * CH], att[:, :]).then_inc(att_st, 16)

            sp.sem_inc(att_st, 16)
            load_keys(0, 0, 0)
            load_queries(0, 0, 0)
            load_keys(0, 0, 1)
            load_queries(0, 0, 1)
            for half in range(2):
                load_keys(0, 1, half)
            for b in range(B):
                load_values(0, b)
            for n in range(B, NB):
                load_queries(0, n // B, n)
            load_max_row(0, 0)

            def group(g, first, last):
                in_group = B * NCH
                for w in range(in_group):
                    n, count = w % NB, in_group * g + w
                    ends = w >= in_group - B and not last
                    if ends:
                        sp.wait_ge(sc_ready, UNITS * count + UNITS // 2)
                        load_keys(g + 1, w % B, 0)
                    if not (last and w == in_group - 1):
                        load_max_row(count + 1, (n + 1) % NB)
                    sp.wait_ge(sc_ready, UNITS * (count + 1))
                    if ends:
                        load_keys(g + 1, w % B, 1)
                    if w + NB < in_group:
                        load_queries(g, (w + NB) // B, n)
                    elif not last:
                        load_queries(g + 1, (w + NB - in_group) // B, n)
                    if ends:
                        sp.wait_ge(av_ready, NKT * (count + 1))
                        load_values(g + 1, w % B)
                    if w > 0:
                        store(count - 1, g, (w - 1) // B, (w - 1) % B)
                    elif not first:
                        store(count - 1, g - 1, NCH - 1, B - 1)

            group(0, True, False)
            with sp.Fori(1, NG - 1) as g:
                group(g, False, False)
            group(NG - 1, False, True)
            store(B * NCH * NG - 1, NG - 1, NCH - 1, B - 1)
            sp.wait_ge(att_st, 16 * (B * NCH * NG + 1))

        @block.tensor
        def _(pe):
            pe.wait_ge(consts, B + 2)

            def search(it, n, j, first=False):
                kc, qt, h = j // (HG * TT), j // HG % TT, j % HG
                if j == 0:
                    pe.wait_ge(q_ld[n], (Q_LD + ROW_LD) * it + Q_LD)
                if j in (0, MAXES // 2):
                    pe.wait_ge(k_ld[n % B][2 * j // MAXES], 48 * (it // PER_GROUP + 1))
                if j >= 3:
                    pe.wait_ge(max_read, MAXES * (NB * it + n) + j - 2)
                elif not first:
                    pe.wait_ge(max_read, MAXES * (NB * it + n))
                nc.tensor.matmul(psum[:, MX + j % 3, :], queries[n][0:R, h, qt * P:(qt + 1) * P],
                                 keys[n % B][0:R, h, kc * CH:(kc + 1) * CH], start=True, stop=True).then_inc(max_ready, 1)

            def score(it, n, kt, h):
                if kt == 0 and h == 0:
                    pe.wait_ge(q_ld[n], (Q_LD + ROW_LD) * (it + 1))
                unit = UNITS * n + HG * kt + h
                if unit >= 3:
                    pe.wait_ge(exp_ready, NB * UNITS * it + unit - 2)
                elif not (n == 0 and isinstance(it, int)):
                    pe.wait_ge(exp_ready, NB * UNITS * it)
                nc.tensor.matmul(psum[:, SC + unit % 3, :], keys[n % B][0:R + 1, h, kt * P:(kt + 1) * P], queries[n][0:R + 1, h, :],
                                 start=True, stop=True).then_inc(sc_ready, 1)

            def weigh(it, n, kt):
                tile = NKT * (NB * it + n) + kt
                pe.wait_ge(exp_ready, HG * (tile + 1))
                if kt == 0:
                    pe.wait_ge(o_copied, NB * it + n + 1)
                    pe.wait_ge(v_ld[n % B], 16 * (it // PER_GROUP + 1))
                for h in range(HG):
                    mm = nc.tensor.matmul(psum[h * HD:(h + 1) * HD, OUT, :], values[n % B][:, kt, h * HD:(h + 1) * HD], probs[kt % NPROB][:, h, :],
                                          start=(kt == 0), stop=(kt == NKT - 1))
                mm.then_inc(av_ready, 1)

            def total(it, n, p):
                pe.wait_ge(pair_ready, PAIRS * (NB * it + n) + p + 1)
                if p == 0:
                    pe.wait_ge(den_copied, NB * it + n + 1)
                for h in range(HG):
                    mm = nc.tensor.matmul(psum[h * HD:(h + 1) * HD, DEN, :], ones[:, :], pair[p % 2][:, h, :],
                                          start=(p == 0), stop=(p == PAIRS - 1))
                mm.then_inc(sums_ready, 1)

            def lagged(it, n, kt, lag):
                if kt >= lag:
                    return it, n, kt - lag
                return (it, n - 1, kt + NKT - lag) if n > 0 else (it - 1, NB - 1, kt + NKT - lag)

            def pair_of(it, n, kt):
                return it, n, kt // 2

            def one(it, n, first, last):
                following = (it, n + 1) if n < NB - 1 else (it + 1, 0)
                j = iter(() if last else range(MAXES))
                for kt in range(NKT):
                    share = [next(j, None) for _ in range(SHARES[kt])]

                    def searches():
                        if share and (at := share.pop(0)) is not None:
                            search(*following, at)

                    score(it, n, kt, 0)
                    searches()
                    score(it, n, kt, 1)
                    searches()
                    if kt >= AV_LAG or not first:
                        weigh(*lagged(it, n, kt, AV_LAG))
                    searches()
                    score(it, n, kt, 2)
                    searches()
                    score(it, n, kt, 3)
                    searches()
                    if (kt - SUM_LAG) % 2 == 0 and (kt >= SUM_LAG or not first):
                        total(*pair_of(*lagged(it, n, kt, SUM_LAG)))

            for j in range(MAXES):
                search(0, 0, j, True)
            blocks(pe, one)
            for kt in range(NKT, NKT + AV_LAG):
                weigh(ITERS - 1, NB - 1, kt - AV_LAG)
            for kt in range(NKT + 1, NKT + SUM_LAG, 2):
                total(ITERS - 1, NB - 1, (kt - SUM_LAG) // 2)

        @block.scalar
        def _(act):
            act.sem_inc(o_copied, 1)
            act.sem_inc(den_copied, 1)

            def copy_out(count):
                act.wait_ge(av_ready, NKT * (count + 1))
                act.wait_ge(att_ready, count + 1)
                act.activation(o_sum[:, :], psum[:, OUT, :], ACT.Copy).then_inc(o_copied, 1)

            def copy_sums(count):
                act.wait_ge(sums_ready, PAIRS * (count + 1))
                act.activation(den[:, :], psum[:, DEN, :], ACT.Copy).then_inc(den_copied, 1)

            def one(it, n, first, last):
                count = NB * it + n
                for kt in range(NKT):
                    tile = NKT * count + kt
                    if kt >= NPROB or not first:
                        act.wait_ge(av_ready, tile - NPROB + 1)
                        act.wait_ge(pair_ready, PAIRS * count + (kt - NPROB) // 2 + 1)
                    for h in range(HG):
                        act.wait_ge(sc_ready, HG * tile + h + 1)
                        unit = UNITS * n + HG * kt + h
                        act.activation(probs[kt % NPROB][:, h, :], psum[:, SC + unit % 3, :], ACT.Exp).then_inc(exp_ready, 1)
                    if not first:
                        if kt == AV_LAG - 1:
                            copy_out(count - 1)
                        if kt == SUM_LAG - 1:
                            copy_sums(count - 1)

            blocks(act, one)
            copy_out(NB * ITERS - 1)
            copy_sums(NB * ITERS - 1)

        @block.vector
        def _(dve):
            dve.sem_inc(att_ready, 1)
            for b in range(B):
                dve.memset(keys[b][R:R + 1, :, :].bitcast(F32), 1.0).then_inc(consts, 1)
            dve.memset(ones[:, :], 1.0).then_inc(consts, 1)
            dve.memset(maxima[:, :], 0.0).then_inc(consts, 1)

            def find(count, j):
                kc, qt, h = j // (HG * TT), j // HG % TT, j % HG
                dve.wait_ge(max_ready, MAXES * count + j + 1)
                at = h * TT + qt
                dve.tensor_reduce(part_max[:, at, kc:kc + 1], psum[:, MX + j % 3, :], AX.X, ALU.max).then_inc(max_read, 1)

            def finish(count):
                dve.wait_ge(max_read, MAXES * (count + 1))
                dve.tensor_reduce(maxima[:, 0:HG * TT], part_max[:, :, :], AX.X, ALU.max).then_inc(turning, 1)
                dve.wait_ge(turning, 2 * count + 1)
                dve.transpose(max_rows[:, :], maxima[:, :]).then_inc(turning, 1)
                dve.wait_ge(turning, 2 * count + 2)
                dve.tensor_scalar(neg_rows[:, :], max_rows[:, :], -1.0, None, ALU.mult).then_inc(neg_ready, 1)

            def normalise(count):
                dve.wait_ge(den_copied, count + 2)
                dve.reciprocal(den[:, :], den[:, :]).then_inc(inverted, 1)
                dve.wait_ge(inverted, count + 1)
                dve.wait_ge(o_copied, count + 2)
                dve.wait_ge(att_st, 16 * (count + 1))
                dve.scalar_tensor_tensor(out=att[:, :], in0=o_sum[:, :], scalar=float(D) ** -0.5, in1=den[:, :],
                                         op0=ALU.mult, op1=ALU.mult).then_inc(att_ready, 1)

            dve.wait_ge(consts, B + 2)
            for j in range(MAXES):
                find(0, j)
            finish(0)

            def one(it, n, first, last):
                count = NB * it + n
                if not last:
                    for j in range(MAXES):
                        find(count + 1, j)
                    dve.wait_ge(q_ld[n], (Q_LD + ROW_LD) * (it + 1))
                    finish(count + 1)
                if not first:
                    normalise(count - 1)

            blocks(dve, one)
            normalise(NB * ITERS - 1)

        @block.gpsimd
        def _(pool):
            def one(it, n, first, last):
                count = NB * it + n
                for p in range(PAIRS):
                    number = PAIRS * count + p
                    pool.wait_ge(exp_ready, 2 * HG * (number + 1))
                    if p >= 2 or not first:
                        pool.wait_ge(sums_ready, number - 1)
                    pool.tensor_tensor(pair[p % 2][:, :, :], probs[2 * p % NPROB][:, :, :], probs[(2 * p + 1) % NPROB][:, :, :],
                                       ALU.add).then_inc(pair_ready, 1)

            blocks(pool, one)


def project_stage(nc, sb, sem, psum, a, ident, vec_dram, att_dram, z_dram, out):
    wp = sb("wp", [P, KT, D])
    wt_hi, wt_lo = (sb(f"wp_{n}", [P, KT, D], F32R) for n in ("hi", "lo"))
    bp_row = sb("bp_row", [1, D])
    bp_parts = sb("bp_parts", [P, D], F32R)
    bp_ones = sb("bp_ones", [P, P], F32R)
    gain = [sb(f"gain{b}", [P, D]) for b in range(B)]
    shift = [sb(f"shift{b}", [P, D]) for b in range(B)]
    att = [sb(f"p_att{b}", [P, KT, CH]) for b in range(B)]
    att_hi, att_lo = ([sb(f"p_att_{n}{b}", [P, KT, CH], F32R) for b in range(B)] for n in ("hi", "lo"))
    z = [sb(f"p_z{b}", [P, TT, D]) for b in range(B)]
    h = [sb(f"p_h{b}", [P, TT, D]) for b in range(B)]
    shifted = [sb(f"p_shifted{b}", [P, TT, D]) for b in range(B)]
    norm = [sb(f"p_norm{b}", [P, TT, D]) for b in range(B)]
    result = [sb(f"p_result{b}", [P, TT, D]) for b in range(B)]
    stats = sb("p_stats", [P, TT, 6])
    root, mean2, var, diff, inv, off = (sb(f"p_{n}", [P, TT]) for n in ("root", "mean2", "var", "diff", "inv", "off"))

    w_ld, row_ld, vec_ld = sem("p_w_ld"), sem("p_row_ld"), sem("p_vec_ld")
    att_ld, z_ld, out_st = ([sem(f"p_{n}{b}") for b in range(B)] for n in ("att_ld", "z_ld", "out_st"))
    consts, wt_tp, whi_ready, wlo_ready = (sem(f"p_{n}") for n in ("consts", "wt_tp", "whi", "wlo"))
    ahi_ready, alo_ready, sum_ready, h_ready = (sem(f"p_{n}") for n in ("ahi", "alo", "sum", "h"))
    stat, root_ready, ln_chain = (sem(f"p_{n}") for n in ("stat", "root", "ln_chain"))
    shifted_ready, norm_ready, scaled_ready, result_ready = (sem(f"p_{n}") for n in ("shifted", "norm", "scaled", "result"))

    H_FREE = B * TT

    def chunk(dram, i, b):
        return dram[b].rearrange("(i t p) d -> i p t d", p=P, t=TT)[bass.ds(i, 1)].rearrange("o p t d -> (o p) t d")

    def steps(engine, step):
        step(0, 0, None, (0, 1))
        with engine.Fori(0, NCH - 1) as i:
            step(i, 1, (i, 0), (i + 1, 0))
            step(i + 1, 0, (i, 1), (i + 1, 1))
        step(NCH - 1, 1, (NCH - 1, 0), None)

    with nc.Block() as block:
        @block.sync
        def _(sp):
            def load(i, b):
                sp.dma_start(att[b][:, :, :], att_dram[:, bass.ds(b * L + i * CH, CH)].rearrange("(k p) t -> p k t", p=P)).then_inc(att_ld[b], 16)
                sp.dma_start(z[b][:, :, :], chunk(z_dram, i, b)).then_inc(z_ld[b], 16)

            def store(i, b):
                sp.wait_ge(result_ready, TT * (B * i + b + 1))
                sp.dma_start(chunk(out, i, b), result[b][:, :, :]).then_inc(out_st[b], 16)

            sp.dma_start(wp[:, :, :], a["L1_cond_Wp"].rearrange("(m p) k -> p m k", p=P)).then_inc(w_ld, 16)
            sp.dma_start(bp_row[:, :], a["L1_cond_bp"].rearrange("(o d) -> o d", o=1)).then_inc(row_ld, 16)
            for b in range(B):
                load(0, b)
            for b in range(B):
                sp.dma_start(gain[b][:, :], vec_dram[V_GAIN_1, b:b + 1, :].broadcast_to((P, D))).then_inc(vec_ld, 16)
                sp.dma_start(shift[b][:, :], vec_dram[V_SHIFT_1, b:b + 1, :].broadcast_to((P, D))).then_inc(vec_ld, 16)

            def step(i, b, previous, loads=True):
                if loads:
                    sp.wait_ge(h_ready, TT * (B * i + b + 1) + H_FREE)
                    load(i + 1, b)
                if previous:
                    store(*previous)

            step(0, 0, None)
            with sp.Fori(0, NCH - 2) as i:
                step(i, 1, (i, 0))
                step(i + 1, 0, (i, 1))
            step(NCH - 2, 1, (NCH - 2, 0))
            step(NCH - 1, 0, (NCH - 2, 1), False)
            step(NCH - 1, 1, (NCH - 1, 0), False)
            store(NCH - 1, 1)
            for b in range(B):
                sp.wait_ge(out_st[b], 16 * (NCH + 1))

        @block.tensor
        def _(pe):
            pe.wait_ge(w_ld, 16)
            for k in range(KT):
                for m in range(KT):
                    mm = pe.transpose(psum[:, TT + k, m * P:(m + 1) * P], wp[:, m, k * P:(k + 1) * P], ident[:, :])
                mm.then_inc(wt_tp, 1)
            pe.wait_ge(consts, 6)
            pe.wait_ge(wlo_ready, KT)

            def step(i, b, previous, following):
                c = B * i + b
                pe.wait_ge(alo_ready, KT * (c + 1))
                pe.wait_ge(h_ready, TT * (c - 1) + H_FREE)
                for t in range(TT):
                    tok, out = slice(t * P, (t + 1) * P), psum[:, TT * b + t, :]
                    nc.tensor.matmul(out, bp_ones[:, :], bp_parts[:, :], start=True, stop=False)
                    for k in range(KT):
                        mm = split_matmuls(nc, out, att_hi[b][:, k, tok], att_lo[b][:, k, tok], wt_hi[:, k, :], wt_lo[:, k, :], False, k == KT - 1)
                    mm.then_inc(sum_ready, 1)

            steps(pe, step)

        @block.scalar
        def _(act):
            def split(i, b):
                c = B * i + b
                act.wait_ge(att_ld[b], 16 * (i + 1))
                wait_count(act, sum_ready, TT * (c - 1))
                for k in range(KT):
                    act.activation(att_hi[b][:, k, :], att[b][:, k, :], ACT.Copy).then_inc(ahi_ready, 1)

            def step(i, b, previous, following):
                c = B * i + b
                if following:
                    split(*following)
                act.wait_ge(stat, MOMENT_STEPS * (c + 1))
                act.activation(root[:, :], var[:, :], ACT.Sqrt).then_inc(root_ready, 1)
                act.wait_ge(ln_chain, INVERSE_STEPS * (c + 1))
                for t in range(TT):
                    act.activation(norm[b][:, t, :], h[b][:, t, :], ACT.Identity, scale=inv[:, t:t + 1], bias=off[:, t:t + 1]).then_inc(norm_ready, 1)

            for k in range(KT):
                act.wait_ge(wt_tp, k + 1)
                act.activation(wt_hi[:, k, :], psum[:, TT + k, :], ACT.Copy).then_inc(whi_ready, 1)
            split(0, 0)
            steps(act, step)

        @block.vector
        def _(dve):
            dve.sem_inc(h_ready, H_FREE)
            for b in range(B):
                dve.sem_inc(out_st[b], 16)
            dve.memset(bp_ones[:, :].bitcast(F32), 0.0).then_inc(consts, 1)
            dve.memset(bp_parts[:, :].bitcast(F32), 0.0).then_inc(consts, 1)
            dve.wait_ge(consts, 2)
            for r in (0, 32):
                dve.memset(bp_ones[r:r + 1, :].bitcast(F32), 1.0).then_inc(consts, 1)
            dve.wait_ge(row_ld, 16)
            dve.tensor_copy(bp_parts[0:1, :], bp_row[:, :]).then_inc(consts, 1)
            dve.wait_ge(consts, 5)
            dve.tensor_tensor(bp_parts[32:33, :], bp_row[:, :], bp_parts[0:1, :].bitcast(F32), ALU.subtract).then_inc(consts, 1)
            for k in range(KT):
                dve.wait_ge(whi_ready, k + 1)
                dve.tensor_tensor(wt_lo[:, k, :], psum[:, TT + k, :], wt_hi[:, k, :].bitcast(F32), ALU.subtract).then_inc(wlo_ready, 1)

            def scale(i, b):
                c = B * i + b
                for t in range(TT):
                    dve.wait_ge(norm_ready, TT * c + t + 1)
                    dve.tensor_tensor(norm[b][:, t, :], norm[b][:, t, :], gain[b][:, :], ALU.mult).then_inc(scaled_ready, 1)

            def finish(i, b):
                c = B * i + b
                dve.wait_ge(out_st[b], 16 * (i + 1))
                for t in range(TT):
                    dve.wait_ge(scaled_ready, TT * c + t + 1)
                    dve.wait_ge(shifted_ready, TT * c + t + 1)
                    dve.tensor_tensor(result[b][:, t, :], norm[b][:, t, :], shifted[b][:, t, :], ALU.add).then_inc(result_ready, 1)

            def step(i, b, previous, following):
                c = B * i + b
                dve.wait_ge(z_ld[b], 16 * (i + 1))
                for t in range(TT):
                    dve.wait_ge(sum_ready, TT * c + t + 1)
                    dve.tensor_tensor(h[b][:, t, :], psum[:, TT * b + t, :], z[b][:, t, :], ALU.add).then_inc(h_ready, 1)
                dve.wait_ge(h_ready, TT * (c + 1) + H_FREE)
                ln_moments(dve, h[b], stats, mean2, var, diff, stat, MOMENT_STEPS * c)
                if previous:
                    scale(*previous)
                dve.wait_ge(root_ready, c + 1)
                ln_inverse(dve, root, mean2, var, inv, off, ln_chain, INVERSE_STEPS * c)
                if previous:
                    finish(*previous)

            dve.wait_ge(vec_ld, 32 * B)
            steps(dve, step)
            scale(NCH - 1, 1)
            finish(NCH - 1, 1)

        @block.gpsimd
        def _(pool):
            def split(i, b):
                c = B * i + b
                for k in range(KT):
                    pool.wait_ge(ahi_ready, KT * c + k + 1)
                    pool.tensor_tensor(att_lo[b][:, k, :], att[b][:, k, :], att_hi[b][:, k, :].bitcast(F32), ALU.subtract).then_inc(alo_ready, 1)

            def step(i, b, previous, following):
                c = B * i + b
                if following:
                    split(*following)
                for t in range(TT):
                    pool.wait_ge(h_ready, TT * c + t + 1 + H_FREE)
                    pool.tensor_tensor(shifted[b][:, t, :], h[b][:, t, :], shift[b][:, :], ALU.add).then_inc(shifted_ready, 1)

            split(0, 0)
            pool.wait_ge(vec_ld, 32 * B)
            steps(pool, step)


def cond_seq_kernel(nc, a, out):
    with ExitStack() as whole:
        def sem(name):
            return whole.enter_context(nc.semaphore(name))

        def scope(stack):
            def sb(name, shape, dtype=F32):
                return stack.enter_context(nc.sbuf_tensor(name, list(shape), dtype))
            return sb

        psum = whole.enter_context(nc.psum_tensor("psum", [P, 8, CH], F32))
        sb = scope(whole)
        ident = sb("ident", [P, P])
        columns = sb("columns", [P, NVC, KT, B])

        def scratch(name, shape, dtype=F32):
            return nc.dram_tensor(name, list(shape), dtype).ap()

        vec_dram = scratch("vec_rows", [NV, B, D])
        y_dram, z_dram = scratch("y_rows", [B, L, D]), scratch("z_rows", [B, L, D])
        q_dram, k_dram = scratch("q_parts", [2, D, B * L]), scratch("k_parts", [2, D, B * L])
        v_dram, att_dram = scratch("v_rows", [B * L, D]), scratch("att_columns", [D, B * L])

        with ExitStack() as state_space:
            own = scope(state_space)
            s5 = {n: own(f"s5_{n}", [P, CH]) for n in ("cos", "sin", "decay")}
            for part in ("hi", "lo"):
                s5[f"b_{part}"] = own(f"s5_b_{part}", [P, KT, 2 * P], F32R)
                s5[f"c_{part}"] = own(f"s5_c_{part}", [P, 2, D], F32R)
                s5[f"d_{part}"] = own(f"s5_d_{part}", [P, KT, P], F32R)
            with ExitStack() as stage:
                prep_stage(nc, scope(stage), sem, psum, a, ident, columns, s5, vec_dram)
            with ExitStack() as stage:
                s5_stage(nc, scope(stage), sem, psum, a, ident, columns, s5, vec_dram, y_dram)
        with ExitStack() as stage:
            ffn_stage(nc, scope(stage), sem, psum, a, ident, columns, vec_dram, y_dram, z_dram)
        with ExitStack() as stage:
            qkv_stage(nc, scope(stage), sem, psum, a, ident, columns, z_dram, q_dram, k_dram, v_dram)
        with ExitStack() as stage:
            attention_stage(nc, scope(stage), sem, psum, q_dram, k_dram, v_dram, att_dram)
        with ExitStack() as stage:
            project_stage(nc, scope(stage), sem, psum, a, ident, vec_dram, att_dram, z_dram, out)


_INS = ["x", "cond_1024"] + [f"L0_cond_{n}" for n in (
    "Wm", "bm", "Lam_re", "Lam_im", "B_re", "B_im", "C_re", "C_im", "D_diag", "log_step", "Wc", "bc", "W1", "b1", "W2", "b2")] + [
    f"L1_cond_{n}" for n in ("ln_g", "ln_b", "Wg", "bg", "Wb", "bb", "Wqkv", "bqkv", "Wp", "bp")]


def kernel(**inputs):
    import numpy as _np
    import concourse.bacc as _bacc
    from concourse import mybir as _mybir
    from concourse.bass_utils import run_bass_kernel_spmd as _run

    nc = _bacc.Bacc("TRN2", target_bir_lowering=False, num_devices=1)
    arrays, args = {}, {}
    for name in _INS:
        v = _np.ascontiguousarray(inputs[name])
        arrays[f"in_{name}_dram"] = v
        args[name] = nc.dram_tensor(f"in_{name}_dram", v.shape, _mybir.dt.from_np(v.dtype), kind="ExternalInput").ap()
    out = nc.dram_tensor("out_dram", (B, L, D), F32, kind="ExternalOutput").ap()
    cond_seq_kernel(nc, args, out)
    r = _run(nc, [arrays], core_ids=[0])
    return r.results[0]["out_dram"]
```

```python
import concourse.bass as bass
from concourse import mybir
from contextlib import ExitStack

B, L, D = 2, 2048, 512
P = 128
KT = D // P
FF = 2048
FT = FF // P
HEADS, HD = 16, 32
HG = P // HD
NG = HEADS // HG
CH = 512
NCH = L // CH
TT = CH // P
EPS = 1e-5

F32 = mybir.dt.float32
F32R = mybir.dt.float32r
I32 = mybir.dt.int32
ALU = mybir.AluOpType
ACT = mybir.ActivationFunctionType
AX = mybir.AxisListType

V_GAIN_A, V_SHIFT_A, V_GAIN_F, V_SHIFT_F, V_GAIN_1, V_SHIFT_1, V_GATE_A, V_GATE_F = range(8)
NV, NVC = 8, 6



def split_matmuls(nc, out, w_hi, w_lo, x_hi, x_lo, first, last):
    nc.tensor.matmul(out, w_hi, x_hi, start=first, stop=False)
    nc.tensor.matmul(out, w_lo, x_hi, start=False, stop=False)
    return nc.tensor.matmul(out, w_hi, x_lo, start=False, stop=last)


def wait_count(engine, semaphore, count):
    if not isinstance(count, int) or count > 0:
        engine.wait_ge(semaphore, count)


MOMENT_STEPS, INVERSE_STEPS = TT + 6, 6


def ln_moments(dve, x, stats, mean2, var, diff, stat, at):
    for t in range(TT):
        dve.bn_stats(stats[:, t, :], x[:, t, :]).then_inc(stat, 1)
    dve.wait_ge(stat, at + TT)
    dve.tensor_tensor(mean2[:, :], stats[:, :, 1], stats[:, :, 4], ALU.add).then_inc(stat, 1)
    dve.tensor_tensor(diff[:, :], stats[:, :, 1], stats[:, :, 4], ALU.subtract).then_inc(stat, 1)
    dve.tensor_tensor(var[:, :], stats[:, :, 2], stats[:, :, 5], ALU.add).then_inc(stat, 1)
    dve.wait_ge(stat, at + TT + 2)
    dve.scalar_tensor_tensor(out=diff[:, :], in0=diff[:, :], scalar=0.25, in1=diff[:, :], op0=ALU.mult, op1=ALU.mult).then_inc(stat, 1)
    dve.wait_ge(stat, at + TT + 3)
    dve.tensor_scalar(var[:, :], var[:, :], 1.0 / D, EPS, ALU.mult, ALU.add).then_inc(stat, 1)
    dve.wait_ge(stat, at + TT + 5)
    dve.tensor_tensor(var[:, :], var[:, :], diff[:, :], ALU.add).then_inc(stat, 1)


def ln_inverse(dve, root, mean2, var, inv, off, chain, at):
    dve.reciprocal(inv[:, :], root[:, :]).then_inc(chain, 1)
    dve.wait_ge(chain, at + 1)
    dve.tensor_tensor(off[:, :], inv[:, :], inv[:, :], ALU.mult).then_inc(chain, 1)
    dve.wait_ge(chain, at + 2)
    dve.tensor_tensor(off[:, :], off[:, :], var[:, :], ALU.mult).then_inc(chain, 1)
    dve.wait_ge(chain, at + 3)
    dve.tensor_scalar(off[:, :], off[:, :], -0.5, 1.5, ALU.mult, ALU.add).then_inc(chain, 1)
    dve.wait_ge(chain, at + 4)
    dve.tensor_tensor(inv[:, :], inv[:, :], off[:, :], ALU.mult).then_inc(chain, 1)
    dve.wait_ge(chain, at + 5)
    dve.scalar_tensor_tensor(out=off[:, :], in0=mean2[:, :], scalar=-0.5, in1=inv[:, :], op0=ALU.mult, op1=ALU.mult).then_inc(chain, 1)


def wqkv_rows(a):
    return a["L1_cond_Wqkv"].rearrange("(m p j) k -> j p m k", p=P, j=3)


def prep_stage(nc, sb, sem, psum, a, ident, columns, s5, x, wgb, vec_dram):
    wm = sb("wm", [P, KT, 6 * D])
    wc = sb("wc", [P, KT, 2 * D])
    cond = sb("cond", [B, D])
    cond_t = sb("cond_t", [P, KT, B])
    sec = sb("sec", [B, 2, D])
    ln_gb = sb("ln_gb", [B, 2, D])
    mod = sb("mod", [B, 10, D])
    vec = sb("vec", [B, NV, D])
    d_rows = sb("d_rows", [KT, P])
    d_col = sb("d_col", [P, KT])
    lam = sb("lam", [P, 3])
    b_in = sb("b_in", [P, 2, D])
    c_in = sb("c_in", [P, 2, KT, P])
    b_bar = sb("b_bar", [P, 2, D])
    tmp = sb("prep_tmp", [P, D])
    scr = sb("prep_scr", [P, 64])
    pow2 = sb("prep_pow2", [P, 1], I32)

    ld_ssm, ld_cond, ld_row, ld_wc, ld_wgb = (sem(f"prep_ld_{n}") for n in ("ssm", "cond", "row", "wc", "wgb"))
    ld_wm = [sem(f"prep_ld_wm{n}") for n in range(3)]
    ident_ready = sem("ident_ready")
    cond_tp, cond_ready = sem("cond_tp"), sem("cond_ready")
    sec_ready, sec_copied, sec_added = sem("sec_ready"), sem("sec_copied"), sem("sec_added")
    gb_tp, gb_ready = sem("gb_tp"), sem("gb_ready")
    d_tp, d_ready = sem("d_tp"), sem("d_ready")
    chain = sem("prep_chain")
    bbar_ready, bc_tp, bc_hi, bc_lo = sem("bbar_ready"), sem("bc_tp"), sem("bc_hi"), sem("bc_lo")
    vec_ready, col_tp = sem("vec_ready"), sem("col_tp")
    vec_stored, ld_x = sem("vec_stored"), sem("prep_ld_x")

    SIDE = P // 32

    def projection(n):
        at = n % SIDE * 32
        return psum[at:at + B, 4 + n // SIDE % 2, :]

    def rows(v, n):
        return v.rearrange("(o n d) -> o n d", o=1, n=n)

    with nc.Block() as block:
        @block.sync
        def _(sp):
            sp.dma_start(cond[:, :], a["cond_1024"]).then_inc(ld_cond, 16)
            for n, name in enumerate(("Lam_re", "Lam_im", "log_step")):
                sp.dma_start(lam[:, n:n + 1], a["L0_cond_" + name].rearrange("(p o) -> p o", o=1)).then_inc(ld_ssm, 16)
            for n, name in enumerate(("B_re", "B_im")):
                sp.dma_start(b_in[:, n, :], a["L0_cond_" + name]).then_inc(ld_ssm, 16)
            for n, name in enumerate(("C_re", "C_im")):
                sp.dma_start(c_in[:, n], a["L0_cond_" + name].rearrange("(k d) p -> d k p", d=P)).then_inc(ld_ssm, 16)
            sp.dma_start(d_rows[:, :], a["L0_cond_D_diag"].rearrange("(k p) -> k p", p=P)).then_inc(ld_ssm, 16)
            for n in range(3):
                cols = slice(2 * n * D, 2 * (n + 1) * D)
                sp.dma_start(wm[:, :, cols], a["L0_cond_Wm"].rearrange("(k p) n -> p k n", p=P)[:, :, cols]).then_inc(ld_wm[n], 16)
            for b in range(B):
                for at, n, name in ((0, 6, "L0_cond_bm"), (6, 2, "L0_cond_bc"), (8, 1, "L1_cond_bg"), (9, 1, "L1_cond_bb")):
                    sp.dma_start(mod[b:b + 1, at:at + n, :], rows(a[name], n)).then_inc(ld_row, 16)
                for at, name in enumerate(("L1_cond_ln_g", "L1_cond_ln_b")):
                    sp.dma_start(ln_gb[b:b + 1, at:at + 1, :], rows(a[name], 1)).then_inc(ld_row, 16)
            sp.dma_start(wc[:, :, :], a["L0_cond_Wc"].rearrange("(k p) n -> p k n", p=P)).then_inc(ld_wc, 16)
            for n, name in enumerate(("Wg", "Wb")):
                sp.dma_start(wgb[n][:, :, :], a["L1_cond_" + name].rearrange("(m p) k -> p m k", p=P)).then_inc(ld_wgb, 16)
            for b in range(B):
                sp.dma_start(x[b][:, :, :], a["x"][b, 0:CH].rearrange("(t p) d -> p t d", p=P)).then_inc(ld_x, 16)
            sp.wait_ge(vec_ready, 1)
            sp.dma_start(vec_dram.rearrange("v b d -> b v d"), vec[:, :, :]).then_inc(vec_stored, 16)
            sp.wait_ge(vec_stored, 16)
            sp.wait_ge(ld_x, 16 * B)

        @block.gpsimd
        def _(pool):
            pool.memset(ident[:, :], 0.0).then_inc(ident_ready, 1)
            pool.wait_ge(ident_ready, 1)
            pool.affine_select(out=ident[:, :], in_=ident[:, :], compare_op=ALU.not_equal, fill=1.0, base=0,
                               pattern=[[-1, P]], channel_multiplier=1).then_inc(ident_ready, 1)
            pool.wait_ge(ld_row, 16 * 6 * B)
            for n in range(10):
                pool.wait_ge(sec_copied, n + 1)
                pool.tensor_tensor(mod[:, n, :], sec[:, n % 2, :], mod[:, n, :], ALU.add).then_inc(sec_added, 1)

        @block.tensor
        def _(pe):
            pe.wait_ge(ident_ready, 2)
            pe.wait_ge(ld_ssm, 16 * 8)
            pe.transpose(psum[:, 7, 0:KT], d_rows[:, :], ident[0:KT, 0:KT]).then_inc(d_tp, 1)
            for n in range(2):
                for k in range(KT):
                    mm = pe.transpose(psum[:, n, k * P:(k + 1) * P], c_in[:, n, k, :], ident[:, :])
                mm.then_inc(bc_tp, 1)
            pe.wait_ge(ld_cond, 16)
            for k in range(KT):
                mm = pe.transpose(psum[:, 6, k * B:(k + 1) * B], cond[:, k * P:(k + 1) * P], ident[0:B, 0:B])
            mm.then_inc(cond_tp, 1)
            pe.wait_ge(cond_ready, 1)
            for group, first in enumerate(range(0, 10, SIDE)):
                if group == 0:
                    pe.wait_ge(ld_wm[0], 16)
                    pe.wait_ge(ld_wm[1], 16)
                if group == 1:
                    pe.wait_ge(bbar_ready, 1)
                    for part in range(2):
                        for k in range(KT):
                            mm = pe.transpose(psum[:, 2 + part, k * P:(k + 1) * P], b_bar[:, part, k * P:(k + 1) * P], ident[:, :])
                        mm.then_inc(bc_tp, 1)
                    pe.wait_ge(ld_wm[2], 16)
                    pe.wait_ge(ld_wc, 16)
                if group == 2:
                    pe.wait_ge(ld_wgb, 32)
                    pe.wait_ge(bc_hi, 4)
                    pe.wait_ge(bc_lo, 4)
                    for j in range(2 * KT):
                        if j >= 4:
                            pe.wait_ge(gb_ready, j - 3)
                        for m in range(KT):
                            mm = pe.transpose(psum[:, j % 4, m * P:(m + 1) * P],
                                              wgb[j // KT][:, m, (j % KT) * P:(j % KT + 1) * P], ident[:, :])
                        mm.then_inc(gb_tp, 1)
                    pe.wait_ge(gb_ready, 2 * KT)
                    pe.wait_ge(sec_copied, SIDE)
                for k in range(KT):
                    for n in range(first, min(first + SIDE, 10)):
                        w = wm[:, k, n * D:(n + 1) * D] if n < 6 else (
                            wc[:, k, (n - 6) * D:(n - 5) * D] if n < 8 else wm[:, k, (n - 8) * D:(n - 7) * D])
                        mm = pe.matmul(projection(n), cond_t[:, k, :], w, start=(k == 0), stop=(k == KT - 1))
                mm.then_inc(sec_ready, 1)
            pe.wait_ge(vec_ready, 1)
            for v in range(NVC):
                for k in range(KT):
                    at = (v * KT + k) * B
                    mm = pe.transpose(psum[:, 6, at:at + B], vec[:, v, k * P:(k + 1) * P], ident[0:B, 0:B])
            mm.then_inc(col_tp, 1)

        @block.scalar
        def _(act):
            def copy_projections(start, stop):
                for n in range(start, stop):
                    act.wait_ge(sec_ready, n // SIDE + 1)
                    if n >= 2:
                        act.wait_ge(sec_added, n - 1)
                    act.activation(sec[:, n % 2, :], projection(n), ACT.Copy).then_inc(sec_copied, 1)

            for n, times in enumerate((2.0, -2.0)):
                act.wait_ge(bc_tp, n + 1)
                act.activation(s5["c_hi"][:, n, :], psum[:, n, :], ACT.Copy, scale=times).then_inc(bc_hi, 1)
            act.wait_ge(cond_tp, 1)
            act.activation(cond_t[:, :, :], psum[:, 6, 0:KT * B].rearrange("p (k b) -> p k b", b=B), ACT.Copy).then_inc(cond_ready, 1)
            copy_projections(0, 4)
            for n in range(2):
                act.wait_ge(bc_tp, 3 + n)
                act.activation(s5["b_hi"][:, :, n * P:(n + 1) * P], psum[:, 2 + n, :].rearrange("p (k s) -> p k s", s=P),
                               ACT.Copy).then_inc(bc_hi, 1)
            copy_projections(4, 8)
            for j in range(2 * KT):
                act.wait_ge(gb_tp, j + 1)
                act.activation(wm[:, j % KT, j // KT * D:(j // KT + 1) * D], psum[:, j % 4, :], ACT.Copy).then_inc(gb_ready, 1)
            copy_projections(8, 10)
            act.wait_ge(col_tp, 1)
            act.activation(columns[:, :, :, :], psum[:, 6, 0:NVC * KT * B].rearrange("p (v k b) -> p v k b", k=KT, b=B),
                           ACT.Copy)

        @block.vector
        def _(dve):
            done = [0]

            def link(instruction):
                done[0] += 1
                instruction.then_inc(chain, 1)
                dve.wait_ge(chain, done[0])

            used = [0]

            def col():
                used[0] += 1
                return scr[:, used[0] - 1:used[0]]

            def polynomial(out, y, coefficients):
                top, following, *rest = coefficients[::-1]
                link(dve.tensor_scalar(out, y, top, following, ALU.mult, ALU.add))
                for c in rest:
                    link(dve.tensor_scalar(out, out, y, c, ALU.mult, ALU.add))

            MAGIC = 1.5 * 2 ** 23

            def exponential(out, x):
                n, f, p = col(), col(), col()
                link(dve.tensor_scalar(f, x, 88.0, -87.0, ALU.min, ALU.max))
                link(dve.tensor_scalar(n, f, 1.4426950408889634, MAGIC, ALU.mult, ALU.add))
                link(dve.tensor_scalar(n, n, MAGIC, None, ALU.subtract))
                for part in (0.693359375, -2.12194440e-4):
                    link(dve.scalar_tensor_tensor(out=f, in0=n, scalar=-part, in1=f, op0=ALU.mult, op1=ALU.add))
                polynomial(p, f, [1.0, 1.0, 1 / 2, 1 / 6, 1 / 24, 1 / 120, 1 / 720, 1 / 5040, 1 / 40320])
                link(dve.tensor_scalar(pow2[:, :], n, 127.0, float(2 ** 23), ALU.add, ALU.mult))
                link(dve.tensor_tensor(out, p, pow2[:, :].bitcast(F32), ALU.mult))

            def sine_cosine(sine, cosine, x):
                n, f, y, s, c, j, q, t = (col() for _ in range(8))
                link(dve.tensor_scalar(n, x, 0.6366197723675814, MAGIC, ALU.mult, ALU.add))
                link(dve.tensor_scalar(n, n, MAGIC, None, ALU.subtract))
                link(dve.scalar_tensor_tensor(out=f, in0=n, scalar=-1.5703125, in1=x, op0=ALU.mult, op1=ALU.add))
                for part in (4.837512969970703125e-4, 7.54978995489188216e-8):
                    link(dve.scalar_tensor_tensor(out=f, in0=n, scalar=-part, in1=f, op0=ALU.mult, op1=ALU.add))
                link(dve.tensor_tensor(y, f, f, ALU.mult))
                polynomial(s, y, [1.0, -1 / 6, 1 / 120, -1 / 5040, 1 / 362880])
                link(dve.tensor_tensor(s, s, f, ALU.mult))
                polynomial(c, y, [1.0, -1 / 2, 1 / 24, -1 / 720, 1 / 40320, -1 / 3628800])
                link(dve.tensor_scalar(j, n, 0.25, MAGIC, ALU.mult, ALU.add))
                link(dve.tensor_scalar(j, j, MAGIC, None, ALU.subtract))
                link(dve.scalar_tensor_tensor(out=j, in0=j, scalar=-4.0, in1=n, op0=ALU.mult, op1=ALU.add))
                link(dve.scalar_tensor_tensor(out=t, in0=j, scalar=-1.0, in1=j, op0=ALU.mult, op1=ALU.max))
                link(dve.tensor_scalar(t, t, -1.0, 2.0, ALU.mult, ALU.add))
                link(dve.tensor_tensor(t, t, j, ALU.mult))
                link(dve.tensor_tensor(q, j, j, ALU.mult))
                link(dve.tensor_scalar(q, q, -1.0, 1.0, ALU.mult, ALU.add))
                link(dve.tensor_scalar(q, q, -1.0, None, ALU.max))
                link(dve.tensor_tensor(sine, c, t, ALU.mult))
                link(dve.scalar_tensor_tensor(out=sine, in0=s, scalar=q, in1=sine, op0=ALU.mult, op1=ALU.add))
                link(dve.tensor_tensor(cosine, s, t, ALU.mult))
                link(dve.scalar_tensor_tensor(out=cosine, in0=c, scalar=q, in1=cosine, op0=ALU.mult, op1=ALU.subtract))

            cos, sin, decay = s5["cos"], s5["sin"], s5["decay"]
            dve.wait_ge(ld_ssm, 16 * 8)
            dt, x, r, l_re, l_im, c_re, c_im, mag, u, w = (col() for _ in range(10))
            lr, li = lam[:, 0:1], lam[:, 1:2]
            exponential(dt, lam[:, 2:3])
            link(dve.tensor_tensor(x, lr, dt, ALU.mult))
            exponential(r, x)
            link(dve.tensor_tensor(x, li, dt, ALU.mult))
            sine_cosine(sin[:, 0:1], cos[:, 0:1], x)
            link(dve.tensor_tensor(l_re, r, cos[:, 0:1], ALU.mult))
            link(dve.tensor_tensor(l_im, r, sin[:, 0:1], ALU.mult))
            link(dve.tensor_scalar(l_re, l_re, 1.0, None, ALU.subtract))
            link(dve.tensor_tensor(mag, lr, lr, ALU.mult))
            link(dve.scalar_tensor_tensor(out=mag, in0=li, scalar=li, in1=mag, op0=ALU.mult, op1=ALU.add))
            link(dve.reciprocal(mag, mag))
            link(dve.tensor_tensor(u, l_im, li, ALU.mult))
            link(dve.scalar_tensor_tensor(out=u, in0=l_re, scalar=lr, in1=u, op0=ALU.mult, op1=ALU.add))
            link(dve.tensor_tensor(c_re, u, mag, ALU.mult))
            link(dve.tensor_tensor(w, l_re, li, ALU.mult))
            link(dve.scalar_tensor_tensor(out=w, in0=l_im, scalar=lr, in1=w, op0=ALU.mult, op1=ALU.subtract))
            link(dve.tensor_tensor(c_im, w, mag, ALU.mult))
            link(dve.tensor_scalar(tmp[:, :], b_in[:, 1, :], c_im, None, ALU.mult))
            link(dve.scalar_tensor_tensor(out=b_bar[:, 0, :], in0=b_in[:, 0, :], scalar=c_re, in1=tmp[:, :], op0=ALU.mult, op1=ALU.subtract))
            link(dve.tensor_scalar(tmp[:, :], b_in[:, 0, :], c_im, None, ALU.mult))
            dve.scalar_tensor_tensor(out=b_bar[:, 1, :], in0=b_in[:, 1, :], scalar=c_re, in1=tmp[:, :], op0=ALU.mult, op1=ALU.add).then_inc(bbar_ready, 1)
            dve.wait_ge(d_tp, 1)
            link(dve.tensor_copy(d_col[:, :], psum[:, 7, 0:KT]))
            dve.wait_ge(ident_ready, 2)
            for k in range(KT):
                link(dve.tensor_scalar(s5["d_hi"][:, k, :], ident[:, :], d_col[:, k:k + 1], None, ALU.mult))
                dve.scalar_tensor_tensor(out=s5["d_lo"][:, k, :], in0=ident[:, :], scalar=d_col[:, k:k + 1],
                                         in1=s5["d_hi"][:, k, :].bitcast(F32), op0=ALU.mult, op1=ALU.subtract).then_inc(d_ready, 1)
            for n, times in enumerate((2.0, -2.0)):
                dve.wait_ge(bc_hi, n + 1)
                dve.scalar_tensor_tensor(out=s5["c_lo"][:, n, :], in0=psum[:, n, :], scalar=times, in1=s5["c_hi"][:, n, :].bitcast(F32),
                                         op0=ALU.mult, op1=ALU.subtract).then_inc(bc_lo, 1)
            for n in range(2):
                dve.wait_ge(bc_hi, 3 + n)
                dve.tensor_tensor(s5["b_lo"][:, :, n * P:(n + 1) * P], psum[:, 2 + n, :].rearrange("p (k s) -> p k s", s=P),
                                  s5["b_hi"][:, :, n * P:(n + 1) * P].bitcast(F32), ALU.subtract).then_inc(bc_lo, 1)
            dve.memset(decay[:, :], 1.0).then_inc(chain, 1)
            done[0] += 1
            dve.wait_ge(chain, done[0])
            link(dve.tensor_scalar(decay[:, :], decay[:, :], r, None, ALU.mult))
            s = 1
            while s < CH:
                w_re, w_im = cos[:, s - 1:s], sin[:, s - 1:s]
                link(dve.tensor_scalar(tmp[:, 0:s], sin[:, 0:s], w_im, None, ALU.mult))
                link(dve.scalar_tensor_tensor(out=cos[:, s:2 * s], in0=cos[:, 0:s], scalar=w_re, in1=tmp[:, 0:s], op0=ALU.mult, op1=ALU.subtract))
                link(dve.tensor_scalar(tmp[:, 0:s], sin[:, 0:s], w_re, None, ALU.mult))
                link(dve.scalar_tensor_tensor(out=sin[:, s:2 * s], in0=cos[:, 0:s], scalar=w_im, in1=tmp[:, 0:s], op0=ALU.mult, op1=ALU.add))
                s *= 2
            shift_a, scale_a, gate_a, shift_f, scale_f, gate_f, scale_c, shift_c, gamma, beta = (mod[:, n, :] for n in range(10))
            dve.wait_ge(sec_added, 8)
            link(dve.tensor_scalar(vec[:, V_GAIN_A, :], scale_a, 1.0, None, ALU.add))
            link(dve.tensor_copy(vec[:, V_SHIFT_A, :], shift_a))
            link(dve.tensor_scalar(scale_f, scale_f, 1.0, None, ALU.add))
            link(dve.scalar_tensor_tensor(out=vec[:, V_GAIN_F, :], in0=scale_c, scalar=1.0, in1=scale_f, op0=ALU.add, op1=ALU.mult))
            link(dve.tensor_tensor(shift_c, shift_c, scale_f, ALU.mult))
            link(dve.tensor_tensor(vec[:, V_SHIFT_F, :], shift_c, shift_f, ALU.add))
            link(dve.tensor_copy(vec[:, V_GATE_A, :], gate_a))
            link(dve.tensor_copy(vec[:, V_GATE_F, :], gate_f))
            dve.wait_ge(sec_added, 10)
            link(dve.tensor_tensor(vec[:, V_GAIN_1, :], gamma, ln_gb[:, 0, :], ALU.mult))
            link(dve.tensor_tensor(gamma, gamma, ln_gb[:, 1, :], ALU.mult))
            dve.tensor_tensor(vec[:, V_SHIFT_1, :], gamma, beta, ALU.add).then_inc(vec_ready, 1)


def s5_stage(nc, sb, sem, psum, a, ident, columns, s5, x, w1_stage, y_first, vec_dram, y_dram):
    y = [sb(f"y{b}", [P, TT, D]) for b in range(B)]
    norm = sb("norm", [P, TT, D])
    gate = [sb(f"gate{b}", [P, D]) for b in range(B)]
    stats = sb("stats", [P, TT, 6])
    root, inv, off, mean2, var, diff = (sb(f"ln_{n}", [P, TT]) for n in ("root", "inv", "off", "mean2", "var", "diff"))
    u = [sb(f"u{n}", [P, CH]) for n in range(2)]
    u_hi = [sb(f"u_hi{b}", [P, KT, CH], F32R) for b in range(B)]
    u_lo = [sb(f"u_lo{b}", [P, KT, CH], F32R) for b in range(B)]
    prod = sb("prod", [P, 4, CH])
    turned = sb("turned", [P, 2, CH])
    scan = sb("scan", [P, 2, CH])
    state = [sb(f"state{b}", [P, 2, CH]) for b in range(B)]
    s_hi, s_lo = sb("s_hi", [P, 2, CH], F32R), sb("s_lo", [P, 2, CH], F32R)
    gated = [sb(f"gated{n}", [P, D]) for n in range(2)]

    x_ld, y_ld, y_st = ([sem(f"s5_{n}{b}") for b in range(B)] for n in ("x_ld", "y_ld", "y_st"))
    gate_ld, w1_ld, y_first_ld, start = sem("s5_gate_ld"), sem("s5_w1_ld"), sem("s5_y_first_ld"), sem("s5_start")
    stat, root_ready, ln_chain, norm_ready = sem("s5_stat"), sem("s5_root"), sem("s5_ln_chain"), sem("s5_norm")
    tr_ready, u_ready, uhi_ready = sem("s5_tr"), sem("s5_u"), sem("s5_uhi")
    ulo_even, ulo_odd = sem("s5_ulo_even"), sem("s5_ulo_odd")
    bu_ready, prod_ready, turned_ready, scan_ready = sem("s5_bu"), sem("s5_prod"), sem("s5_turned"), sem("s5_scan")
    back_ready, state_ready, shi_ready, slo_ready = sem("s5_back"), sem("s5_state"), sem("s5_shi"), sem("s5_slo")
    cy_ready, gated_ready, y_ready = sem("s5_cy"), sem("s5_gated"), sem("s5_y")

    cos, sin, decay = s5["cos"], s5["sin"], s5["decay"]
    TR, BU, CY = 0, 2, 6
    PROD_FREE, U_FREE, GATED_FREE, Y_FREE = 4, 2, 2, 2

    def chunk(dram, i, b):
        return dram.rearrange("b l d -> (b l) d")[bass.ds(b * L + i * CH, CH)].rearrange("(t p) d -> p t d", p=P)

    def steps(engine, step):
        step(0, 0, None, (0, 1), (1, 0))
        with engine.Fori(0, NCH - 2) as i:
            step(i, 1, (i, 0), (i + 1, 0), (i + 1, 1))
            step(i + 1, 0, (i, 1), (i + 1, 1), (i + 2, 0))
        step(NCH - 2, 1, (NCH - 2, 0), (NCH - 1, 0), (NCH - 1, 1))
        step(NCH - 1, 0, (NCH - 2, 1), (NCH - 1, 1), None)
        step(NCH - 1, 1, (NCH - 1, 0), None, None)

    with nc.Block() as block:
        @block.sync
        def _(sp):
            def load_x(i, b):
                sp.dma_start(x[b][:, :, :], chunk(a["x"], i, b)).then_inc(x_ld[b], 16)

            def load_y(i, b):
                sp.wait_ge(y_st[b], 16 * (i + 1))
                sp.dma_start(y[b][:, :, :], chunk(a["x"], i, b)).then_inc(y_ld[b], 16)

            def store(i, b):
                sp.wait_ge(y_ready, Y_FREE + TT * (B * i + b + 1))
                sp.dma_start(chunk(y_dram, i, b), y[b][:, :, :]).then_inc(y_st[b], 16)

            def step(i, b, previous, following, second):
                if second:
                    sp.wait_ge(norm_ready, B * i + b + 1)
                    load_x(*second)
                load_y(i, b)
                if following is None:
                    sp.dma_start(y_first[:, :, :], chunk(y_dram, 0, 0)).then_inc(y_first_ld, 16)
                if previous:
                    store(*previous)

            for b in range(B):
                sp.sem_inc(y_st[b], 16)
                sp.sem_inc(x_ld[b], 16)
            for b in range(B):
                sp.dma_start(gate[b][:, :], vec_dram[V_GATE_A, b:b + 1, :].broadcast_to((P, D))).then_inc(gate_ld, 16)
            for tile, piece in zip(w1_stage, (0, 1, 3)):
                sp.dma_start(tile[:, :, :], a["L0_cond_W1"].rearrange("(k p) f -> p k f", p=P)[:, :, piece * D:(piece + 1) * D]).then_inc(w1_ld, 16)
            steps(sp, step)
            store(NCH - 1, 1)
            sp.wait_ge(w1_ld, 48)
            sp.wait_ge(y_first_ld, 16)
            for b in range(B):
                sp.wait_ge(y_st[b], 16 * (NCH + 1))

        @block.tensor
        def _(pe):
            def turn(i, b):
                c = B * i + b
                pe.wait_ge(norm_ready, c + 1)
                for k in range(KT):
                    pe.wait_ge(u_ready, KT * c + k - 1 + U_FREE)
                    for t in range(TT):
                        mm = pe.transpose(psum[:, TR + k % 2, t * P:(t + 1) * P], norm[:, t, k * P:(k + 1) * P], ident[:, :])
                    mm.then_inc(tr_ready, 1)

            def project_in(i, b):
                c = B * i + b
                wait_count(pe, prod_ready, 4 * (c - 1) + PROD_FREE)
                for k in range(KT):
                    pe.wait_ge((ulo_even, ulo_odd)[k % 2], KT // 2 * c + k // 2 + 1)
                    for n in range(2):
                        mm = split_matmuls(nc, psum[:, BU + 2 * b + n, :], s5["b_hi"][:, k, n * P:(n + 1) * P],
                                           s5["b_lo"][:, k, n * P:(n + 1) * P], u_hi[b][:, k, :], u_lo[b][:, k, :], k == 0, k == KT - 1)
                mm.then_inc(bu_ready, 1)

            def project_out(i, b):
                c = B * i + b
                for t in range(TT):
                    pe.wait_ge(gated_ready, TT * c + t - 1 + GATED_FREE)
                    tok = slice(t * P, (t + 1) * P)
                    out = psum[:, CY + t % 2, :]
                    for n in range(2):
                        if t == 0:
                            pe.wait_ge(slo_ready, 2 * c + n + 1)
                        split_matmuls(nc, out, s_hi[:, n, tok], s_lo[:, n, tok], s5["c_hi"][:, n, :], s5["c_lo"][:, n, :], n == 0, False)
                    for k in range(KT):
                        mm = split_matmuls(nc, out[:, k * P:(k + 1) * P], u_hi[b][:, k, tok], u_lo[b][:, k, tok],
                                           s5["d_hi"][:, k, :], s5["d_lo"][:, k, :], False, k == KT - 1)
                    mm.then_inc(cy_ready, 1)

            def step(i, b, previous, following, second):
                project_in(i, b)
                if previous:
                    project_out(*previous)
                if following:
                    turn(*following)

            turn(0, 0)
            steps(pe, step)
            project_out(NCH - 1, 1)

        @block.scalar
        def _(act):
            act.sem_inc(u_ready, U_FREE)

            def take_root(i, b):
                c = B * i + b
                act.wait_ge(stat, MOMENT_STEPS * (c + 1))
                act.activation(root[:, :], var[:, :], ACT.Sqrt).then_inc(root_ready, 1)

            def split(i, b):
                c = B * i + b
                for k in range(KT):
                    act.wait_ge(tr_ready, KT * c + k + 1)
                    wait_count(act, (ulo_even, ulo_odd)[k % 2], KT // 2 * c + k // 2)
                    act.activation(u[k % 2][:, :], psum[:, TR + k % 2, :], ACT.Identity, scale=columns[:, V_GAIN_A, k, b:b + 1],
                                   bias=columns[:, V_SHIFT_A, k, b:b + 1]).then_inc(u_ready, 1)
                    act.wait_ge(u_ready, KT * c + k + 1 + U_FREE)
                    wait_count(act, cy_ready, TT * (c - 1))
                    act.activation(u_hi[b][:, k, :], u[k % 2][:, :], ACT.Copy).then_inc(uhi_ready, 1)

            def step(i, b, previous, following, second):
                c = B * i + b
                for n in range(2):
                    act.wait_ge(state_ready, 2 * c + n + 1)
                    wait_count(act, cy_ready, TT * c)
                    act.activation(s_hi[:, n, :], state[b][:, n, :], ACT.Copy).then_inc(shi_ready, 1)
                if following:
                    split(*following)
                if second:
                    take_root(*second)

            take_root(0, 0)
            split(0, 0)
            take_root(0, 1)
            steps(act, step)

        @block.vector
        def _(dve):
            dve.sem_inc(prod_ready, PROD_FREE)
            dve.sem_inc(gated_ready, GATED_FREE)
            for b in range(B):
                dve.memset(state[b][:, :, CH - 1:CH], 0.0).then_inc(start, 1)
            dve.wait_ge(start, B)

            def moments(i, b):
                c = B * i + b
                dve.wait_ge(x_ld[b], 16 * (i + 1))
                wait_count(dve, ln_chain, INVERSE_STEPS * c)
                ln_moments(dve, x[b], stats, mean2, var, diff, stat, MOMENT_STEPS * c)

            def normalise(i, b):
                c = B * i + b
                dve.wait_ge(root_ready, c + 1)
                ln_inverse(dve, root, mean2, var, inv, off, ln_chain, INVERSE_STEPS * c)
                dve.wait_ge(ln_chain, INVERSE_STEPS * (c + 1))
                wait_count(dve, tr_ready, KT * c)
                for t in range(TT):
                    nrm = dve.tensor_scalar(norm[:, t, :], x[b][:, t, :], inv[:, t:t + 1], off[:, t:t + 1], ALU.mult, ALU.add)
                nrm.then_inc(norm_ready, 1)

            def split(i, b):
                c = B * i + b
                for k in range(1, KT, 2):
                    dve.wait_ge(uhi_ready, KT * c + k + 1)
                    dve.tensor_tensor(u_lo[b][:, k, :], u[k % 2][:, :], u_hi[b][:, k, :].bitcast(F32), ALU.subtract).then_inc(ulo_odd, 1)

            def apply_gate(i, b, t):
                c = B * i + b
                dve.wait_ge(cy_ready, TT * c + t + 1)
                dve.wait_ge(y_ready, TT * c + t - 1 + Y_FREE)
                dve.tensor_tensor(gated[t % 2][:, :], psum[:, CY + t % 2, :], gate[b][:, :], ALU.mult).then_inc(gated_ready, 1)

            def step(i, b, previous, following, second):
                c = B * i + b
                if following:
                    normalise(*following)
                re, im = psum[:, BU + 2 * b, :], psum[:, BU + 2 * b + 1, :]
                dve.wait_ge(bu_ready, c + 1)
                wait_count(dve, state_ready, 2 * c)
                for n, (v, table) in enumerate(((re, cos), (im, sin), (im, cos), (re, sin))):
                    dve.tensor_tensor(prod[:, n, :], v, table[:, :], ALU.mult).then_inc(prod_ready, 1)
                if previous:
                    apply_gate(*previous, 0)
                for n in range(2):
                    dve.wait_ge(turned_ready, 2 * c + n + 1)
                    wait_count(dve, back_ready, 4 * c)
                    dve.tensor_tensor_scan(scan[:, n, :], decay[:, :], turned[:, n, :], state[b][:, n, CH - 1:CH],
                                           ALU.mult, ALU.add).then_inc(scan_ready, 1)
                if previous:
                    apply_gate(*previous, 1)
                dve.wait_ge(scan_ready, 2 * (c + 1))
                for n, (v, table) in enumerate(((0, cos), (1, sin), (1, cos), (0, sin))):
                    dve.tensor_tensor(prod[:, n, :], scan[:, v, :], table[:, :], ALU.mult).then_inc(back_ready, 1)
                if second:
                    moments(*second)
                if previous:
                    for t in range(2, TT):
                        apply_gate(*previous, t)
                if following:
                    split(*following)

            moments(0, 0)
            normalise(0, 0)
            moments(0, 1)
            split(0, 0)
            dve.wait_ge(gate_ld, 16 * B)
            steps(dve, step)
            for t in range(TT):
                apply_gate(NCH - 1, 1, t)

        @block.gpsimd
        def _(pool):
            pool.sem_inc(y_ready, Y_FREE)

            def split(i, b, k):
                c = B * i + b
                pool.wait_ge(uhi_ready, KT * c + k + 1)
                pool.tensor_tensor(u_lo[b][:, k, :], u[k % 2][:, :], u_hi[b][:, k, :].bitcast(F32), ALU.subtract).then_inc(ulo_even, 1)

            def add(i, b, t):
                c = B * i + b
                if t == 0:
                    pool.wait_ge(y_ld[b], 16 * (i + 1))
                pool.wait_ge(gated_ready, TT * c + t + 1 + GATED_FREE)
                pool.tensor_tensor(y[b][:, t, :], gated[t % 2][:, :], y[b][:, t, :], ALU.add).then_inc(y_ready, 1)

            def step(i, b, previous, following, second):
                c = B * i + b
                for n, op in enumerate((ALU.add, ALU.subtract)):
                    pool.wait_ge(prod_ready, 4 * c + 2 * n + 2 + PROD_FREE)
                    wait_count(pool, scan_ready, 2 * c)
                    pool.tensor_tensor(turned[:, n, :], prod[:, 2 * n, :], prod[:, 2 * n + 1, :], op).then_inc(turned_ready, 1)
                if previous:
                    add(*previous, 0)
                    add(*previous, 1)
                for n, op in enumerate((ALU.subtract, ALU.add)):
                    pool.wait_ge(back_ready, 4 * c + 2 * n + 2)
                    wait_count(pool, shi_ready, 2 * c)
                    pool.tensor_tensor(state[b][:, n, :], prod[:, 2 * n, :], prod[:, 2 * n + 1, :], op).then_inc(state_ready, 1)
                for n in range(2):
                    pool.wait_ge(shi_ready, 2 * c + n + 1)
                    pool.tensor_tensor(s_lo[:, n, :], state[b][:, n, :], s_hi[:, n, :].bitcast(F32), ALU.subtract).then_inc(slo_ready, 1)
                    if following:
                        split(*following, 2 * n)
                if previous:
                    for t in range(2, TT):
                        add(*previous, t)

            for k in range(0, KT, 2):
                split(0, 0, k)
            steps(pool, step)
            for t in range(TT):
                add(NCH - 1, 1, t)


def ffn_stage(nc, sb, sem, psum, a, ident, columns, stage, y_first, vec_dram, y_dram, z_dram):
    w1_hi, w1_lo = (sb(f"w1_{n}", [P, KT, FF], F32R) for n in ("hi", "lo"))
    w2_hi, w2_lo = (sb(f"w2_{n}", [P, FT, D], F32R) for n in ("hi", "lo"))
    y = [y_first, stage[1]]
    norm = sb("ffn_norm", [P, TT, D])
    gate = [sb(f"ffn_gate{b}", [P, D]) for b in range(B)]
    stats = sb("ffn_stats", [P, TT, 6])
    root, inv, off, mean2, var, diff = (sb(f"ffn_ln_{n}", [P, TT]) for n in ("root", "inv", "off", "mean2", "var", "diff"))
    u = [sb(f"ffn_u{n}", [P, CH]) for n in range(2)]
    u_hi = sb("ffn_u_hi", [P, KT, CH], F32R)
    u_lo = sb("ffn_u_lo", [P, KT, CH], F32R)
    b1_rows = sb("b1_rows", [FT, P])
    b1_col = sb("b1_col", [P, FT])
    b2_row = sb("b2_row", [1, D])
    b2_parts = sb("b2_parts", [P, D], F32R)
    ones_parts = sb("ones_parts", [P, P], F32R)
    g = [stage[2][:, n, :] for n in range(2)]
    NH = 2
    h_hi = [sb(f"h_hi{n}", [P, CH], F32R) for n in range(NH)]
    h_lo = [sb(f"h_lo{n}", [P, CH], F32R) for n in range(NH)]
    gated = [stage[2][:, 2 + n, :] for n in range(2)]

    w_ld, wq_ld = [sem(f"ffn_w_ld{n}") for n in range(2)], sem("ffn_wq_ld")
    y_ld = [sem(f"ffn_y_ld{b}") for b in range(B)]
    z_st = [sem(f"ffn_z_st{b}") for b in range(B)]
    small_ld, gate_ld, b1_tp, consts = (sem(f"ffn_{n}") for n in ("small_ld", "gate_ld", "b1_tp", "consts"))
    whi_ready, whi_pool, wlo_dve, wlo_pool = sem("ffn_whi"), sem("ffn_whi_pool"), sem("ffn_wlo_dve"), sem("ffn_wlo_pool")
    stat, root_ready, ln_chain, norm_ready = (sem(f"ffn_{n}") for n in ("stat", "root", "ln_chain", "norm"))
    tr_ready, uhi_ready, u_ready, ulo_ready = (sem(f"ffn_{n}") for n in ("tr", "uhi", "u", "ulo"))
    h_ready, g_ready, ghi_ready, glo_ready = (sem(f"ffn_{n}") for n in ("h", "g", "ghi", "glo"))
    down_ready, acc_ready, gated_ready, z_ready = (sem(f"ffn_{n}") for n in ("down", "acc", "gated", "z"))

    ACC, H, TR = 0, 4, 6
    NP = 4
    FP = FT // NP
    LN_TILE = 8
    HI_ACT = [(1, 0), (1, 1), (1, 3), (2, 0)]
    LO_DVE = [(1, 0), (1, 1), (2, 0)]
    POOL = [(1, 3), (2, 1), (1, 2), (2, 2), (2, 3)]
    HELD = [[(1, 0), (2, 0), (1, 2), (2, 2), (2, 3)], [(1, 1), (2, 1)], [(1, 3)]]
    LOADS = [(2, 0), (2, 1), (1, 2), (2, 2), (2, 3)]

    G_FREE, Z_FREE, DOWN_FREE, ACC_FREE = 2, 2, 1, TT

    def chunk(dram, i, b):
        return dram[b].rearrange("(i t p) d -> i p t d", p=P, t=TT)[bass.ds(i, 1)].rearrange("o p t d -> (o p) t d")

    def held(w, p):
        return next((n, pieces.index((w, p))) for n, pieces in enumerate(HELD) if (w, p) in pieces)

    def raw(w, p):
        return stage[held(w, p)[0]][:, :, :]

    def source(w, p):
        if w == 1:
            return a["L0_cond_W1"].rearrange("(k p) f -> p k f", p=P)[:, :, p * FP * P:(p + 1) * FP * P]
        return a["L0_cond_W2"].rearrange("(f p) d -> p f d", p=P)[:, p * FP:(p + 1) * FP, :]

    def part(w1, w2, w, p):
        return w1[:, :, p * FP * P:(p + 1) * FP * P] if w == 1 else w2[:, p * FP:(p + 1) * FP, :]

    def wait_loaded(engine, w, p):
        tile, before = held(w, p)
        if before:
            engine.wait_ge(w_ld[tile], 16 * before)

    def split_low(engine, w, p, signal):
        engine.tensor_tensor(part(w1_lo, w2_lo, w, p), raw(w, p), part(w1_hi, w2_hi, w, p).bitcast(F32), ALU.subtract).then_inc(signal, 1)

    def wait_split(engine, w, p):
        if (w, p) in LO_DVE:
            engine.wait_ge(wlo_dve, LO_DVE.index((w, p)) + 1)
        else:
            engine.wait_ge(wlo_pool, POOL.index((w, p)) + 1)

    def steps(engine, front, back, prepare):
        front(0, 0)
        prepare()
        with engine.Fori(0, NCH - 1) as i:
            back(i, 0, lambda: front(i, 1))
            back(i, 1, lambda: front(i + 1, 0))
        back(NCH - 1, 0, lambda: front(NCH - 1, 1))
        back(NCH - 1, 1, None)

    with nc.Block() as block:
        @block.sync
        def _(sp):
            sp.sem_inc(y_ld[0], 16)
            sp.dma_start(b1_rows[:, :], a["L0_cond_b1"].rearrange("(f p) -> f p", p=P)).then_inc(small_ld, 16)
            sp.dma_start(b2_row[:, :], a["L0_cond_b2"].rearrange("(o d) -> o d", o=1)).then_inc(small_ld, 16)
            for b in range(B):
                sp.dma_start(gate[b][:, :], vec_dram[V_GATE_F, b:b + 1, :].broadcast_to((P, D))).then_inc(gate_ld, 16)
            for w, p in LOADS:
                tile, before = held(w, p)
                wait_split(sp, *HELD[tile][before - 1])
                sp.dma_start(raw(w, p), source(w, p)).then_inc(w_ld[tile], 16)
                if (w, p) == (1, 2):
                    wait_split(sp, *HELD[1][-1])
                    sp.dma_start(y[1][:, :, :], chunk(y_dram, 0, 1)).then_inc(y_ld[1], 16)

            wait_split(sp, *HELD[0][-1])
            sp.dma_start(stage[0][:, :, :], wqkv_rows(a)[0]).then_inc(wq_ld, 16)

            def store(i, b):
                sp.wait_ge(z_ready, TT * (2 * i + b + 1) + Z_FREE)
                sp.dma_start(chunk(z_dram, i, b), y[b][:, :, :]).then_inc(z_st[b], 16)

            with sp.Fori(0, NCH - 1) as i:
                for b in range(B):
                    store(i, b)
                    sp.wait_ge(z_st[b], 16 * (i + 1))
                    sp.dma_start(y[b][:, :, :], chunk(y_dram, i + 1, b)).then_inc(y_ld[b], 16)
            for b in range(B):
                store(NCH - 1, b)
            for b in range(B):
                sp.wait_ge(z_st[b], 16 * NCH)
            sp.wait_ge(wq_ld, 16)

        @block.tensor
        def _(pe):
            pe.wait_ge(small_ld, 32)
            pe.transpose(psum[:, ACC, 0:FT], b1_rows[:, :], ident[0:FT, 0:FT]).then_inc(b1_tp, 1)

            def front(i, b):
                c = 2 * i + b
                pe.wait_ge(norm_ready, c + 1)
                for k in range(KT):
                    pe.wait_ge(u_ready, KT * c + k + 1)
                    for t in range(TT):
                        mm = pe.transpose(psum[:, TR + k % 2, t * P:(t + 1) * P], norm[:, t, k * P:(k + 1) * P], ident[:, :])
                    mm.then_inc(tr_ready, 1)

            def up(c, j):
                if j == 0:
                    pe.wait_ge(uhi_ready, KT * (c + 1))
                    pe.wait_ge(ulo_ready, KT * (c + 1) + 2)
                if j % FP == 0:
                    wait_split(pe, 1, j // FP)
                pe.wait_ge(g_ready, FT * c + j + 1)
                for k in range(KT):
                    f = slice(j * P, (j + 1) * P)
                    mm = split_matmuls(nc, psum[:, H + j % 2, :], w1_hi[:, k, f], w1_lo[:, k, f], u_hi[:, k, :], u_lo[:, k, :],
                                       k == 0, k == KT - 1)
                mm.then_inc(h_ready, 1)

            def down(c, j):
                if j % FP == 0:
                    wait_split(pe, 2, j // FP)
                pe.wait_ge(ghi_ready, FT * c + j + 1)
                pe.wait_ge(glo_ready, FT * c + j + 1 + G_FREE)
                for t in range(TT):
                    tok = slice(t * P, (t + 1) * P)
                    if j == 0:
                        pe.wait_ge(gated_ready, TT * c + t + 1)
                        pe.matmul(psum[:, ACC + t, :], ones_parts[:, :], b2_parts[:, :], start=True, stop=False)
                    mm = split_matmuls(nc, psum[:, ACC + t, :], h_hi[j % NH][:, tok], h_lo[j % NH][:, tok], w2_hi[:, j, :], w2_lo[:, j, :],
                                       False, j == FT - 1)
                    if j == FT - 1:
                        mm.then_inc(acc_ready, 1)
                if j < FT - 1:
                    mm.then_inc(down_ready, 1)

            def back(i, b, following):
                c = 2 * i + b
                for j in range(FT):
                    up(c, j)
                    if j == FT - 1 and following:
                        following()
                    if j >= 1:
                        down(c, j - 1)
                down(c, FT - 1)

            steps(pe, front, back, lambda: pe.wait_ge(consts, 7))

        @block.scalar
        def _(act):
            act.sem_inc(u_ready, 2)
            act.sem_inc(g_ready, 2)
            act.sem_inc(glo_ready, G_FREE)
            act.sem_inc(down_ready, DOWN_FREE)
            act.sem_inc(acc_ready, ACC_FREE)

            def split_high(w, p):
                wait_loaded(act, w, p)
                act.activation(part(w1_hi, w2_hi, w, p), raw(w, p), ACT.Copy).then_inc(whi_ready, 1)

            def front(i, b):
                c = 2 * i + b
                act.wait_ge(stat, MOMENT_STEPS * (c + 1))
                act.activation(root[:, :], var[:, :], ACT.Sqrt).then_inc(root_ready, 1)

            def split(i, b):
                c = 2 * i + b
                for k in range(KT):
                    act.wait_ge(tr_ready, KT * c + k + 1)
                    act.wait_ge(ulo_ready, KT * c + k + 1)
                    act.activation(u[k % 2][:, :], psum[:, TR + k % 2, :], ACT.Identity, scale=columns[:, V_GAIN_F, k, b:b + 1],
                                   bias=columns[:, V_SHIFT_F, k, b:b + 1]).then_inc(u_ready, 1)

            def gelu(c, j):
                act.wait_ge(h_ready, FT * c + j + 1)
                act.wait_ge(glo_ready, FT * c + j - 1 + G_FREE)
                act.activation(g[j % 2], psum[:, H + j % 2, :], ACT.Gelu_apprx_tanh, bias=b1_col[:, j:j + 1]).then_inc(g_ready, 1)
                act.wait_ge(g_ready, FT * c + j + 3)
                if j == 1:
                    act.wait_ge(acc_ready, TT * c + ACC_FREE)
                else:
                    act.wait_ge(down_ready, (FT - 1) * c + max(j - NH + 1, 0) + DOWN_FREE)
                act.activation(h_hi[j % NH][:, :], g[j % 2], ACT.Copy).then_inc(ghi_ready, 1)

            for w, p in HI_ACT[:2]:
                split_high(w, p)
            front(0, 0)
            split_high(*HI_ACT[2])
            split(0, 0)
            for w, p in HI_ACT[3:]:
                split_high(w, p)
            act.wait_ge(consts, 1)
            wait_split(act, *HELD[2][-1])

            def back(i, b, nxt):
                c = 2 * i + b
                for j in range(FT):
                    if j == LN_TILE + 2 and nxt:
                        front(*nxt)
                    gelu(c, j)
                if nxt:
                    split(*nxt)

            with act.Fori(0, NCH - 1) as i:
                back(i, 0, (i, 1))
                back(i, 1, (i + 1, 0))
            back(NCH - 1, 0, (NCH - 1, 1))
            back(NCH - 1, 1, None)

        @block.vector
        def _(dve):
            dve.sem_inc(gated_ready, TT)
            dve.sem_inc(z_ready, Z_FREE)

            def moments(i, b):
                c = 2 * i + b
                dve.wait_ge(y_ld[b], 16 * (i + 1))
                ln_moments(dve, y[b], stats, mean2, var, diff, stat, MOMENT_STEPS * c)

            def normalise(i, b):
                c = 2 * i + b
                dve.wait_ge(root_ready, c + 1)
                ln_inverse(dve, root, mean2, var, inv, off, ln_chain, INVERSE_STEPS * c)
                dve.wait_ge(ln_chain, INVERSE_STEPS * (c + 1))
                dve.wait_ge(tr_ready, KT * c)
                for t in range(TT):
                    nrm = dve.tensor_scalar(norm[:, t, :], y[b][:, t, :], inv[:, t:t + 1], off[:, t:t + 1], ALU.mult, ALU.add)
                nrm.then_inc(norm_ready, 1)

            def split(i, b):
                c = 2 * i + b
                for k in range(KT):
                    dve.wait_ge(u_ready, KT * c + k + 3)
                    dve.tensor_copy(u_hi[:, k, :], u[k % 2][:, :]).then_inc(uhi_ready, 1)

            def back(i, b, nxt):
                c = 2 * i + b
                for j in range(FT):
                    if j == LN_TILE and nxt:
                        moments(*nxt)
                    if j == LN_TILE + 2 and nxt:
                        normalise(*nxt)
                    dve.wait_ge(ghi_ready, FT * c + j + 1)
                    dve.tensor_tensor(h_lo[j % NH][:, :], g[j % 2], h_hi[j % NH][:, :].bitcast(F32), ALU.subtract).then_inc(glo_ready, 1)
                if nxt:
                    split(*nxt)
                for t in range(TT):
                    dve.wait_ge(acc_ready, TT * c + t + 1 + ACC_FREE)
                    dve.wait_ge(z_ready, TT * c + t - 1 + Z_FREE)
                    dve.tensor_tensor(gated[t % 2], psum[:, ACC + t, :], gate[b][:, :], ALU.mult).then_inc(gated_ready, 1)

            def split_weight(w, p):
                dve.wait_ge(whi_ready, HI_ACT.index((w, p)) + 1)
                split_low(dve, w, p, wlo_dve)

            moments(0, 0)
            normalise(0, 0)
            split_weight(*LO_DVE[0])
            split(0, 0)
            dve.wait_ge(b1_tp, 1)
            dve.tensor_copy(b1_col[:, :], psum[:, ACC, 0:FT]).then_inc(consts, 1)
            dve.memset(ones_parts[:, :].bitcast(F32), 0.0).then_inc(consts, 1)
            dve.memset(b2_parts[:, :].bitcast(F32), 0.0).then_inc(consts, 1)
            dve.wait_ge(consts, 3)
            for r in (0, 32):
                dve.memset(ones_parts[r:r + 1, :].bitcast(F32), 1.0).then_inc(consts, 1)
            dve.tensor_copy(b2_parts[0:1, :], b2_row[:, :]).then_inc(consts, 1)
            dve.wait_ge(consts, 6)
            dve.tensor_tensor(b2_parts[32:33, :], b2_row[:, :], b2_parts[0:1, :].bitcast(F32), ALU.subtract).then_inc(consts, 1)
            for w, p in LO_DVE[1:]:
                split_weight(w, p)
            dve.wait_ge(gate_ld, 16 * B)
            with dve.Fori(0, NCH - 1) as i:
                back(i, 0, (i, 1))
                back(i, 1, (i + 1, 0))
            back(NCH - 1, 0, (NCH - 1, 1))
            back(NCH - 1, 1, None)

        @block.gpsimd
        def _(pool):
            pool.sem_inc(ulo_ready, 2)

            def split(i, b):
                c = 2 * i + b
                for k in range(KT):
                    pool.wait_ge(uhi_ready, KT * c + k + 1)
                    pool.tensor_tensor(u_lo[:, k, :], u[k % 2][:, :], u_hi[:, k, :].bitcast(F32), ALU.subtract).then_inc(ulo_ready, 1)

            def back(i, b, nxt):
                c = 2 * i + b
                if nxt:
                    split(*nxt)
                for t in range(TT):
                    pool.wait_ge(gated_ready, TT * c + t + 1 + TT)
                    pool.tensor_tensor(y[b][:, t, :], gated[t % 2], y[b][:, t, :], ALU.add).then_inc(z_ready, 1)

            pool.wait_ge(whi_ready, HI_ACT.index(POOL[0]) + 1)
            split_low(pool, *POOL[0], wlo_pool)
            split(0, 0)
            for n, (w, p) in enumerate(POOL[1:]):
                wait_loaded(pool, w, p)
                pool.tensor_copy(part(w1_hi, w2_hi, w, p), raw(w, p)).then_inc(whi_pool, 1)
                pool.wait_ge(whi_pool, n + 1)
                split_low(pool, w, p, wlo_pool)
            with pool.Fori(0, NCH - 1) as i:
                back(i, 0, (i, 1))
                back(i, 1, (i + 1, 0))
            back(NCH - 1, 0, (NCH - 1, 1))
            back(NCH - 1, 1, None)


def negate_maxima(dve, tiles, turning, before, ready):
    dve.tensor_reduce(tiles["maxima"][:, 0:HG * TT], tiles["part_max"][:, :, :], AX.X, ALU.max).then_inc(turning, 1)
    dve.wait_ge(turning, before + 1)
    dve.transpose(tiles["max_rows"][:, :], tiles["maxima"][:, :]).then_inc(turning, 1)
    dve.wait_ge(turning, before + 2)
    dve.tensor_scalar(tiles["neg_rows"][:, :], tiles["max_rows"][:, :], -1.0, None, ALU.mult).then_inc(ready, 1)


def load_max_rows(sp, queries, neg_rows, signal):
    row = queries[3 * HD:3 * HD + 1, :, :].bitcast(F32).rearrange("o h (t r i) -> o (h t) r i", r=4, i=32)
    for r in range(4):
        sp.dma_start(row[:, :, r, :], neg_rows[32 * r:32 * r + HG * TT, :].bitcast(F32)).then_inc(signal, 16)


def qkv_stage(nc, sb, sem, psum, a, ident, columns, wq, first, z_dram, q_dram, k_dram, v_dram):
    NC = B * NCH
    SEARCH_FROM = NCH + 1
    SEARCHES = -(-HG * TT * NCH // (NC - SEARCH_FROM))
    PER_TILE = -(-SEARCHES // (2 * KT))
    wt_hi, wt_lo = (sb(f"wqkv_{n}", [P, KT, 3 * D], F32R) for n in ("hi", "lo"))
    w_raw = [wq] + [sb(f"wqkv_raw{n}", [P, KT, D]) for n in (1, 2)]
    z = [sb(f"qkv_z{n}", [P, TT, D]) for n in range(2)]
    norm = sb("qkv_norm", [P, TT, D])
    stats = sb("qkv_stats", [P, TT, 6])
    root, inv, off, mean2, var, diff = (sb(f"qkv_ln_{n}", [P, TT]) for n in ("root", "inv", "off", "mean2", "var", "diff"))
    u = [sb(f"qkv_u{n}", [P, CH]) for n in range(2)]
    u_hi = [sb(f"qkv_u_hi{n}", [P, KT, CH], F32R) for n in range(2)]
    u_lo = [sb(f"qkv_u_lo{n}", [P, KT, CH], F32R) for n in range(2)]
    NO = 4
    o_hi = [sb(f"qk_hi{n}", [P, CH], F32R) for n in range(NO)]
    o_lo = [sb(f"qk_lo{n}", [P, CH], F32R) for n in range(NO)]
    v_out = [sb(f"v_out{n}", [P, D]) for n in range(2)]
    biases = sb("bqkv_rows", [33, 3 * D])
    b_nat, b_sorted = biases[32:33, :], biases[0:1, :]
    b_col = sb("bqkv_col", [P, 2 * KT])
    bv_parts = sb("bv_parts", [P, D], F32R)
    bqkv_ones = sb("bqkv_ones", [P, P], F32R)

    w_ld, small_ld = [sem(f"qkv_w_ld{j}") for j in (1, 2)], sem("qkv_small_ld")
    z_ld = [sem(f"qkv_z_ld{n}") for n in range(2)]
    o_st = [sem(f"qk_st{n}") for n in range(NO)]
    v_st = [sem(f"v_st{n}") for n in range(2)]
    b_tp, consts = sem("qkv_b_tp"), sem("qkv_consts")
    wt_tp, whi_ready, wlo_ready = sem("qkv_wt"), sem("qkv_whi"), sem("qkv_wlo")
    stat, root_ready, ln_chain, norm_ready = (sem(f"qkv_{n}") for n in ("stat", "root", "ln_chain", "norm"))
    tr_ready, uhi_ready, u_ready, ulo_ready = (sem(f"qkv_{n}") for n in ("tr", "uhi", "u", "ulo"))
    o_ready, ohi_ready, olo_ready = sem("qk_ready"), sem("qk_hi_ready"), sem("qk_lo_ready")
    v_ready, v_copied = sem("v_ready"), sem("v_copied")

    TR, QK, V = 0, 2, 5
    MX = (TR, TR + 1, 7)
    first_ld, row_ones, clear, max_ready, max_read = (sem(f"first_{n}") for n in ("ld", "ones", "clear", "max_ready", "max_read"))
    turning, row_ready = sem("first_turning"), sem("first_row")
    NM = 2 * KT

    def chunk(dram, c):
        return dram.rearrange("b l d -> (b l) d")[bass.ds(c * CH, CH)].rearrange("(t p) d -> p t d", p=P)

    U_FREE, O_FREE, V_FREE = 2, 3, 2

    def steps(engine, step):
        with engine.Fori(0, NCH // 2) as n:
            step(2 * n, 0, 1, None)
            step(2 * n + 1, 1, 0, None)
        for c in range(NCH, NC):
            step(c, c % 2, (c + 1) % 2 if c < NC - 1 else None, SEARCHES * (c - SEARCH_FROM) if c >= SEARCH_FROM else None)

    def product(j):
        return j // (HG * TT), j // HG % TT, j % HG

    with nc.Block() as block:
        @block.sync
        def _(sp):
            for done, free in [(o, 32) for o in o_st] + [(v, 16) for v in v_st]:
                sp.sem_inc(done, free)
            sp.dma_start(b_nat[:, :], a["L1_cond_bqkv"].rearrange("(o c) -> o c", o=1)).then_inc(small_ld, 16)
            sp.dma_start(z[0][:, :, :], chunk(z_dram, 0)).then_inc(z_ld[0], 16)
            for n in (1, 2):
                sp.dma_start(w_raw[n][:, :, :], wqkv_rows(a)[n]).then_inc(w_ld[n - 1], 16)
            sp.dma_start(z[1][:, :, :], chunk(z_dram, 1)).then_inc(z_ld[1], 16)

            def step(c, n, nxt, search):
                if isinstance(c, int) and c == NCH:
                    for slot in range(NO):
                        sp.wait_ge(o_st[slot], 32 * ((NM // NO) * NCH + 1))
                    for row, (qp, kp) in enumerate(((0, 0), (0, 1), (1, 0))):
                        rows = slice(row * HD, (row + 1) * HD)
                        for tile, dram, part, tokens in ((first["keys"], k_dram, kp, L), (first["queries"], q_dram, qp, CH)):
                            src = dram.rearrange("e (g h d) t -> e g d h t", h=HG, d=HD)[part, 0, :, :, 0:tokens]
                            sp.dma_start(tile[rows, :, :].bitcast(F32), src).then_inc(first_ld, 16)
                if nxt is not None and not (isinstance(c, int) and c == NC - 2):
                    sp.wait_ge(norm_ready, c + 1)
                    sp.dma_start(z[n][:, :, :], chunk(z_dram, c + 2)).then_inc(z_ld[n], 16)
                for m in range(NM):
                    sp.wait_ge(olo_ready, NM * c + m + 1 + O_FREE)
                    dram = (q_dram, k_dram)[m // KT]
                    for part, tile in enumerate((o_hi[m % NO], o_lo[m % NO])):
                        sp.dma_start(dram[part, (m % KT) * P:(m % KT + 1) * P, bass.ds(c * CH, CH)],
                                     tile[:, :].bitcast(F32)).then_inc(o_st[m % NO], 16)
                for t in range(TT):
                    sp.wait_ge(v_copied, TT * c + t + 1 + V_FREE)
                    sp.dma_start(v_dram[bass.ds(c * CH + t * P, P), :], v_out[t % 2][:, :]).then_inc(v_st[t % 2], 16)

            steps(sp, step)
            sp.wait_ge(row_ready, 1)
            load_max_rows(sp, first["queries"], first["neg_rows"], first_ld)
            sp.wait_ge(first_ld, 16 * (6 + 4))
            for n in range(NO):
                sp.wait_ge(o_st[n], 32 * ((NM // NO) * B * NCH + 1))
            for n in range(2):
                sp.wait_ge(v_st[n], 16 * ((TT // 2) * B * NCH + 1))

        @block.tensor
        def _(pe):
            for n in range(3 * KT):
                j, k = divmod(n, KT)
                if j > 0:
                    pe.wait_ge(w_ld[j - 1], 16)
                if n >= 6:
                    pe.wait_ge(wlo_ready, n - 5)
                for m in range(KT):
                    mm = pe.transpose(psum[:, n % 6, m * P:(m + 1) * P], w_raw[j][:, m, k * P:(k + 1) * P], ident[:, :])
                mm.then_inc(wt_tp, 1)
            pe.wait_ge(consts, 7)
            for m in range(NM):
                mm = pe.transpose(psum[:, 7, m:m + 1], b_sorted[:, m * P:(m + 1) * P], ident[0:1, 0:1])
            mm.then_inc(b_tp, 1)
            pe.wait_ge(wlo_ready, 3 * KT)
            pe.wait_ge(consts, 9)

            def turn(c):
                pe.wait_ge(norm_ready, c + 1)
                for k in range(KT):
                    pe.wait_ge(u_ready, KT * c + k - 1 + U_FREE)
                    for t in range(TT):
                        mm = pe.transpose(psum[:, TR + k % 2, t * P:(t + 1) * P], norm[:, t, k * P:(k + 1) * P], ident[:, :])
                    mm.then_inc(tr_ready, 1)

            def step(c, n, nxt, search):
                todo = [] if search is None else list(range(search, min(search + SEARCHES, HG * TT * NCH)))
                if search == 0:
                    pe.wait_ge(first_ld, 16 * 6)

                def look():
                    if todo:
                        j = todo.pop(0)
                        kc, qt, h = product(j)
                        if j > 2:
                            pe.wait_ge(max_read, j - 2)
                        nc.tensor.matmul(psum[:, MX[j % 3], :], first["queries"][0:3 * HD, h, qt * P:(qt + 1) * P],
                                         first["keys"][0:3 * HD, h, kc * CH:(kc + 1) * CH], start=True, stop=True).then_inc(max_ready, 1)

                for m in range(NM):
                    pe.wait_ge(olo_ready, NM * c + m - 2 + O_FREE)
                    cols = slice(m * P, (m + 1) * P)
                    for k in range(KT):
                        if m == 0:
                            pe.wait_ge(ulo_ready, KT * c + k + 1 + U_FREE)
                        mm = split_matmuls(nc, psum[:, QK + m % 3, :], wt_hi[:, k, cols], wt_lo[:, k, cols],
                                           u_hi[n][:, k, :], u_lo[n][:, k, :], k == 0, k == KT - 1)
                        if k < PER_TILE:
                            look()
                    mm.then_inc(o_ready, 1)
                if nxt is not None:
                    if search is not None:
                        pe.wait_ge(max_read, search + SEARCHES)
                    turn(c + 1)
                for t in range(TT):
                    pe.wait_ge(v_copied, TT * c + t - 1 + V_FREE)
                    tok = slice(t * P, (t + 1) * P)
                    nc.tensor.matmul(psum[:, V + t % 2, :], bqkv_ones[:, :], bv_parts[:, :], start=True, stop=False)
                    for k in range(KT):
                        mm = split_matmuls(nc, psum[:, V + t % 2, :], u_hi[n][:, k, tok], u_lo[n][:, k, tok],
                                           wt_hi[:, k, 2 * D:3 * D], wt_lo[:, k, 2 * D:3 * D], False, k == KT - 1)
                    mm.then_inc(v_ready, 1)

            turn(0)
            steps(pe, step)

        @block.scalar
        def _(act):
            act.sem_inc(u_ready, U_FREE)
            act.sem_inc(v_copied, V_FREE)

            def take_root(c):
                act.wait_ge(stat, MOMENT_STEPS * (c + 1))
                act.activation(root[:, :], var[:, :], ACT.Sqrt).then_inc(root_ready, 1)

            def scale(c):
                for k in range(KT):
                    act.wait_ge(tr_ready, KT * c + k + 1)
                    act.wait_ge(ulo_ready, KT * c + k - 1 + U_FREE)
                    gain, shift = (columns[:, v, k, bass.ds(c // NCH, 1)] for v in (V_GAIN_1, V_SHIFT_1))
                    act.activation(u[k % 2][:, :], psum[:, TR + k % 2, :], ACT.Identity, scale=gain, bias=shift).then_inc(u_ready, 1)

            def step(c, n, nxt, search):
                for m in range(NM):
                    if m == NM // 2 and nxt is not None:
                        take_root(c + 1)
                    act.wait_ge(o_ready, NM * c + m + 1)
                    act.wait_ge(o_st[m % NO], 32 * ((NM // NO) * c + m // NO + 1))
                    act.activation(o_hi[m % NO][:, :], psum[:, QK + m % 3, :], ACT.Identity, bias=b_col[:, m:m + 1]).then_inc(ohi_ready, 1)
                if nxt is not None:
                    scale(c + 1)
                for t in range(TT):
                    act.wait_ge(v_ready, TT * c + t + 1)
                    act.wait_ge(v_st[t % 2], 16 * ((TT // 2) * c + t // 2 + 1))
                    act.activation(v_out[t % 2][:, :], psum[:, V + t % 2, :], ACT.Copy).then_inc(v_copied, 1)

            for n in range(3 * KT):
                j, k = divmod(n, KT)
                if n == KT:
                    take_root(0)
                act.wait_ge(wt_tp, n + 1)
                act.activation(wt_hi[:, k, j * D:(j + 1) * D], psum[:, n % 6, :], ACT.Copy).then_inc(whi_ready, 1)
            act.wait_ge(consts, 10)
            scale(0)
            steps(act, step)

        @block.vector
        def _(dve):
            dve.memset(bqkv_ones[:, :].bitcast(F32), 0.0).then_inc(consts, 1)
            dve.memset(bv_parts[:, :].bitcast(F32), 0.0).then_inc(consts, 1)
            dve.wait_ge(consts, 2)
            for r in (0, 32):
                dve.memset(bqkv_ones[r:r + 1, :].bitcast(F32), 1.0).then_inc(consts, 1)
            dve.wait_ge(small_ld, 16)
            for j in range(3):
                dve.tensor_copy(b_sorted[:, j * D:(j + 1) * D], b_nat[:, :].rearrange("o (c j) -> o j c", j=3)[:, j, :]).then_inc(consts, 1)
            dve.wait_ge(consts, 7)
            dve.tensor_copy(bv_parts[0:1, :], b_sorted[:, 2 * D:3 * D]).then_inc(consts, 1)
            dve.wait_ge(consts, 8)
            dve.tensor_tensor(bv_parts[32:33, :], b_sorted[:, 2 * D:3 * D], bv_parts[0:1, :].bitcast(F32), ALU.subtract).then_inc(consts, 1)

            def moments(c, n):
                dve.wait_ge(z_ld[n], 16 * (c // 2 + 1))
                ln_moments(dve, z[n], stats, mean2, var, diff, stat, MOMENT_STEPS * c)

            def normalise(c, n):
                dve.wait_ge(root_ready, c + 1)
                ln_inverse(dve, root, mean2, var, inv, off, ln_chain, INVERSE_STEPS * c)
                dve.wait_ge(ln_chain, INVERSE_STEPS * (c + 1))
                wait_count(dve, tr_ready, KT * c)
                for t in range(TT):
                    nrm = dve.tensor_scalar(norm[:, t, :], z[n][:, t, :], inv[:, t:t + 1], off[:, t:t + 1], ALU.mult, ALU.add)
                nrm.then_inc(norm_ready, 1)

            def split(c, n):
                for k in range(KT):
                    dve.wait_ge(u_ready, KT * c + k + 1 + U_FREE)
                    dve.tensor_copy(u_hi[n][:, k, :], u[k % 2][:, :]).then_inc(uhi_ready, 1)

            def step(c, n, nxt, search):
                todo = [] if search is None else list(range(search, min(search + SEARCHES, HG * TT * NCH)))

                def find(number):
                    for _ in range(min(number, len(todo))):
                        j = todo.pop(0)
                        kc, qt, h = product(j)
                        at = h * TT + qt
                        dve.wait_ge(max_ready, j + 1)
                        dve.tensor_reduce(first["part_max"][:, at, kc:kc + 1], psum[:, MX[j % 3], :], AX.X, ALU.max).then_inc(max_read, 1)

                for m in range(NM):
                    if nxt is not None and m == 2:
                        moments(c + 1, nxt)
                    if nxt is not None and m == 5:
                        normalise(c + 1, nxt)
                    find(PER_TILE)
                    dve.wait_ge(ohi_ready, NM * c + m + 1)
                    dve.scalar_tensor_tensor(out=o_lo[m % NO][:, :], in0=psum[:, QK + m % 3, :], scalar=b_col[:, m:m + 1],
                                             in1=o_hi[m % NO][:, :].bitcast(F32), op0=ALU.add, op1=ALU.subtract).then_inc(olo_ready, 1)
                if nxt is not None:
                    split(c + 1, nxt)

            dve.sem_inc(olo_ready, O_FREE)
            dve.memset(first["maxima"][:, :], 0.0).then_inc(clear, 1)
            for n in range(3 * KT):
                j, k = divmod(n, KT)
                if n == KT:
                    moments(0, 0)
                    normalise(0, 0)
                dve.wait_ge(whi_ready, n + 1)
                dve.tensor_tensor(wt_lo[:, k, j * D:(j + 1) * D], psum[:, n % 6, :], wt_hi[:, k, j * D:(j + 1) * D].bitcast(F32),
                                  ALU.subtract).then_inc(wlo_ready, 1)
            dve.wait_ge(b_tp, 1)
            dve.tensor_copy(b_col[:, :], psum[:, 7, 0:NM]).then_inc(consts, 1)
            split(0, 0)
            dve.wait_ge(consts, 10)
            steps(dve, step)
            dve.wait_ge(clear, 1)
            dve.wait_ge(max_read, HG * TT * NCH)
            negate_maxima(dve, first, turning, 0, row_ready)

        @block.gpsimd
        def _(pool):
            pool.sem_inc(ulo_ready, U_FREE)
            pool.memset(first["keys"][3 * HD:3 * HD + 1, :, :].bitcast(F32), 1.0).then_inc(row_ones, 1)
            pool.wait_ge(row_ones, 1)

            def split(c, n):
                for k in range(KT):
                    pool.wait_ge(uhi_ready, KT * c + k + 1)
                    pool.tensor_tensor(u_lo[n][:, k, :], u[k % 2][:, :], u_hi[n][:, k, :].bitcast(F32), ALU.subtract).then_inc(ulo_ready, 1)

            def step(c, n, nxt, search):
                if nxt is not None:
                    split(c + 1, nxt)

            split(0, 0)
            steps(pool, step)


def attention_stage(nc, sb, sem, psum, a, wp, first, q_dram, k_dram, v_dram, att_dram):
    R = 3 * HD
    NKT = L // P
    NKC = L // CH
    PB = 2
    NB = PB * B
    PER_GROUP = B * NCH // NB
    ITERS = NG * PER_GROUP
    PAIRS = NKT // 2
    NPROB = 8
    MAXES = HG * TT * NKC
    SHARES = [4] + [5] * 12 + [0] * 3
    AV_LAG, SUM_LAG = 2, 5
    Q_LD, ROW_LD = 3 * 16, 4 * 16

    keys = [first["keys"]] + [sb(f"keys{b}", [P, HG, L], F32R) for b in range(1, B)]
    queries = [first["queries"]] + [sb(f"queries{n}", [P, HG, CH], F32R) for n in range(1, NB)]
    values = [sb(f"values{b}", [P, NKT, P]) for b in range(B)]
    ones = sb("att_ones", [P, HD])
    probs = [sb(f"probs{n}", [P, HG, CH]) for n in range(NPROB)]
    pair = [sb(f"pair{n}", [P, HG, CH]) for n in range(2)]
    part_max, neg_rows = first["part_max"], first["neg_rows"]
    o_sum, den, att = sb("o_sum", [P, CH]), sb("den", [P, CH]), sb("att", [P, CH])

    k_ld = [[sem(f"k_ld{b}{half}") for half in range(2)] for b in range(B)]
    v_ld = [sem(f"v_ld{b}") for b in range(B)]
    q_ld = [sem(f"q_ld{n}") for n in range(NB)]
    att_st, consts = sem("att_st"), sem("att_consts")
    ones_ld, wp_ld = sem("ones_ld"), sem("wp_ld")
    sc_ready, exp_ready = sem("scores_ready"), sem("exp_ready")
    av_ready, pair_ready, sums_ready = sem("av_ready"), sem("pair_ready"), sem("sums_ready")
    max_ready, max_read, turning, neg_ready = (sem(n) for n in ("max_ready", "max_read", "max_turning", "neg_ready"))
    o_copied, den_copied, inverted, att_ready = (sem(n) for n in ("o_copied", "den_copied", "den_inverted", "att_ready"))

    SC, MX, OUT, DEN = 0, 3, 6, 7
    UNITS = HG * NKT

    def place(w):
        return w % NB // PB, w // NB * PB + w % PB

    def blocks(engine, block):
        block(0, 0, True, False)
        with engine.Fori(0, ITERS - 1) as it:
            for n in range(1, NB):
                block(it, n, False, False)
            block(it + 1, 0, False, False)
        for n in range(1, NB):
            block(ITERS - 1, n, False, n == NB - 1)

    with nc.Block() as block:
        @block.sync
        def _(sp):
            def load_keys(g, b, half):
                src = k_dram.rearrange("e (g h d) t -> e g d h t", h=HG, d=HD)
                at, n_tok = half * (L // 2), L // 2
                for n, part in enumerate((0, 1, 0)):
                    sp.dma_start(keys[b][n * HD:(n + 1) * HD, :, at:at + n_tok].bitcast(F32),
                                 src[part, bass.ds(g, 1), :, :, b * L + at:b * L + at + n_tok].rearrange("o d h t -> (o d) h t")
                                 ).then_inc(k_ld[b][half], 16)

            def load_values(g, b):
                sp.dma_start(values[b][:, :, :],
                             v_dram[b * L:(b + 1) * L, bass.ds(g * P, P)].rearrange("(n p) c -> p n c", p=P)).then_inc(v_ld[b], 16)

            def load_queries(g, chunk, n):
                src = q_dram.rearrange("e (g h d) t -> e g d h t", h=HG, d=HD)
                at = n // PB * L + chunk * CH
                for row, part in enumerate((0, 0, 1)):
                    sp.dma_start(queries[n][row * HD:(row + 1) * HD, :, :].bitcast(F32),
                                 src[part, bass.ds(g, 1), :, :, at:at + CH].rearrange("o d h t -> (o d) h t")).then_inc(q_ld[n], 16)

            def load_max_row(count, n):
                sp.wait_ge(neg_ready, count + 1)
                load_max_rows(sp, queries[n], neg_rows, q_ld[n])

            def store(count, g, b, chunk):
                sp.wait_ge(att_ready, count + 2)
                sp.dma_start(att_dram[bass.ds(g * P, P), b * L + chunk * CH:b * L + (chunk + 1) * CH], att[:, :]).then_inc(att_st, 16)

            sp.sem_inc(att_st, 16)
            for half in range(2):
                sp.sem_inc(k_ld[0][half], 48)
            sp.sem_inc(q_ld[0], Q_LD + ROW_LD)
            for n in range(1, PB):
                load_queries(0, n, n)
            load_values(0, 0)
            for b in range(1, B):
                sp.dma_start(keys[b][R:R + 1, :, :].bitcast(F32), keys[0][R:R + 1, :, :].bitcast(F32)).then_inc(ones_ld, 16)
            for half in range(2):
                load_keys(0, 1, half)
            load_values(0, 1)
            for n in range(PB, NB):
                load_queries(0, n % PB, n)
            sp.dma_start(wp[:, :, :], a["L1_cond_Wp"].rearrange("(m p) k -> p m k", p=P)).then_inc(wp_ld, 16)

            def group(g, first, last):
                in_group = B * NCH
                for w in range(in_group):
                    n, count = w % NB, in_group * g + w
                    b, chunk = place(w)
                    ends = chunk == NCH - 1 and not last
                    if ends:
                        sp.wait_ge(sc_ready, UNITS * count + UNITS // 2)
                        load_keys(g + 1, b, 0)
                    if not (last and w == in_group - 1):
                        load_max_row(count + 1, (n + 1) % NB)
                    sp.wait_ge(sc_ready, UNITS * (count + 1))
                    if ends:
                        load_keys(g + 1, b, 1)
                    if w + NB < in_group:
                        load_queries(g, place(w + NB)[1], n)
                    elif not last:
                        load_queries(g + 1, place(w + NB - in_group)[1], n)
                    if ends:
                        sp.wait_ge(av_ready, NKT * (count + 1))
                        load_values(g + 1, b)
                    if w > 0:
                        store(count - 1, g, *place(w - 1))
                    elif not first:
                        store(count - 1, g - 1, B - 1, NCH - 1)

            group(0, True, False)
            with sp.Fori(1, NG - 1) as g:
                group(g, False, False)
            group(NG - 1, False, True)
            store(B * NCH * NG - 1, NG - 1, B - 1, NCH - 1)
            sp.wait_ge(att_st, 16 * (B * NCH * NG + 1))
            sp.wait_ge(wp_ld, 16)

        @block.tensor
        def _(pe):
            def search(it, n, j):
                kc, qt, h = j // (HG * TT), j // HG % TT, j % HG
                if j == 0:
                    pe.wait_ge(q_ld[n], (Q_LD + ROW_LD) * it + Q_LD)
                if j in (0, MAXES // 2):
                    pe.wait_ge(k_ld[n // PB][2 * j // MAXES], 48 * (it // PER_GROUP + 1))
                pe.wait_ge(max_read, MAXES * (NB * it + n) + max(j - 2, 0))
                nc.tensor.matmul(psum[:, MX + j % 3, :], queries[n][0:R, h, qt * P:(qt + 1) * P],
                                 keys[n // PB][0:R, h, kc * CH:(kc + 1) * CH], start=True, stop=True).then_inc(max_ready, 1)

            def score(it, n, kt, h):
                if kt == 0 and h == 0:
                    pe.wait_ge(q_ld[n], (Q_LD + ROW_LD) * (it + 1))
                unit = UNITS * n + HG * kt + h
                if unit >= 3:
                    pe.wait_ge(exp_ready, NB * UNITS * it + unit - 2)
                elif not (n == 0 and isinstance(it, int)):
                    pe.wait_ge(exp_ready, NB * UNITS * it)
                nc.tensor.matmul(psum[:, SC + unit % 3, :], keys[n // PB][0:R + 1, h, kt * P:(kt + 1) * P], queries[n][0:R + 1, h, :],
                                 start=True, stop=True).then_inc(sc_ready, 1)

            def weigh(it, n, kt):
                tile = NKT * (NB * it + n) + kt
                pe.wait_ge(exp_ready, HG * (tile + 1))
                if kt == 0:
                    pe.wait_ge(o_copied, NB * it + n + 1)
                    pe.wait_ge(v_ld[n // PB], 16 * (it // PER_GROUP + 1))
                for h in range(HG):
                    mm = nc.tensor.matmul(psum[h * HD:(h + 1) * HD, OUT, :], values[n // PB][:, kt, h * HD:(h + 1) * HD], probs[kt % NPROB][:, h, :],
                                          start=(kt == 0), stop=(kt == NKT - 1))
                mm.then_inc(av_ready, 1)

            def total(it, n, p):
                pe.wait_ge(pair_ready, PAIRS * (NB * it + n) + p + 1)
                if p == 0:
                    pe.wait_ge(den_copied, NB * it + n + 1)
                for h in range(HG):
                    mm = nc.tensor.matmul(psum[h * HD:(h + 1) * HD, DEN, :], ones[:, :], pair[p % 2][:, h, :],
                                          start=(p == 0), stop=(p == PAIRS - 1))
                mm.then_inc(sums_ready, 1)

            def lagged(it, n, kt, lag):
                if kt >= lag:
                    return it, n, kt - lag
                return (it, n - 1, kt + NKT - lag) if n > 0 else (it - 1, NB - 1, kt + NKT - lag)

            def pair_of(it, n, kt):
                return it, n, kt // 2

            def one(it, n, first, last):
                following = (it, n + 1) if n < NB - 1 else (it + 1, 0)
                j = iter(() if last else range(MAXES))
                for kt in range(NKT):
                    share = [next(j, None) for _ in range(SHARES[kt])]

                    def searches():
                        if share and (at := share.pop(0)) is not None:
                            search(*following, at)

                    if first and kt == AV_LAG:
                        pe.wait_ge(consts, 1)
                        pe.wait_ge(ones_ld, 16 * (B - 1))
                    score(it, n, kt, 0)
                    searches()
                    score(it, n, kt, 1)
                    searches()
                    if kt >= AV_LAG or not first:
                        weigh(*lagged(it, n, kt, AV_LAG))
                    searches()
                    score(it, n, kt, 2)
                    searches()
                    score(it, n, kt, 3)
                    searches()
                    if (kt - SUM_LAG) % 2 == 0 and (kt >= SUM_LAG or not first):
                        total(*pair_of(*lagged(it, n, kt, SUM_LAG)))

            blocks(pe, one)
            for kt in range(NKT, NKT + AV_LAG):
                weigh(ITERS - 1, NB - 1, kt - AV_LAG)
            for kt in range(NKT + 1, NKT + SUM_LAG, 2):
                total(ITERS - 1, NB - 1, (kt - SUM_LAG) // 2)

        @block.scalar
        def _(act):
            act.sem_inc(o_copied, 1)
            act.sem_inc(den_copied, 1)

            def copy_out(count):
                act.wait_ge(av_ready, NKT * (count + 1))
                act.wait_ge(att_ready, count + 1)
                act.activation(o_sum[:, :], psum[:, OUT, :], ACT.Copy).then_inc(o_copied, 1)

            def copy_sums(count):
                act.wait_ge(sums_ready, PAIRS * (count + 1))
                act.activation(den[:, :], psum[:, DEN, :], ACT.Copy).then_inc(den_copied, 1)

            def one(it, n, first, last):
                count = NB * it + n
                for kt in range(NKT):
                    tile = NKT * count + kt
                    if kt >= NPROB or not first:
                        act.wait_ge(av_ready, tile - NPROB + 1)
                        act.wait_ge(pair_ready, PAIRS * count + (kt - NPROB) // 2 + 1)
                    for h in range(HG):
                        act.wait_ge(sc_ready, HG * tile + h + 1)
                        unit = UNITS * n + HG * kt + h
                        act.activation(probs[kt % NPROB][:, h, :], psum[:, SC + unit % 3, :], ACT.Exp).then_inc(exp_ready, 1)
                    if not first:
                        if kt == AV_LAG - 1:
                            copy_out(count - 1)
                        if kt == SUM_LAG - 1:
                            copy_sums(count - 1)

            blocks(act, one)
            copy_out(NB * ITERS - 1)
            copy_sums(NB * ITERS - 1)

        @block.vector
        def _(dve):
            dve.sem_inc(att_ready, 1)
            dve.sem_inc(max_read, MAXES)
            dve.sem_inc(neg_ready, 1)
            dve.memset(ones[:, :], 1.0).then_inc(consts, 1)

            def find(count, j):
                kc, qt, h = j // (HG * TT), j // HG % TT, j % HG
                dve.wait_ge(max_ready, MAXES * (count - 1) + j + 1)
                at = h * TT + qt
                dve.tensor_reduce(part_max[:, at, kc:kc + 1], psum[:, MX + j % 3, :], AX.X, ALU.max).then_inc(max_read, 1)

            def finish(count):
                dve.wait_ge(max_read, MAXES * (count + 1))
                negate_maxima(dve, first, turning, 2 * (count - 1), neg_ready)

            def normalise(count):
                dve.wait_ge(den_copied, count + 2)
                dve.reciprocal(den[:, :], den[:, :]).then_inc(inverted, 1)
                dve.wait_ge(inverted, count + 1)
                dve.wait_ge(o_copied, count + 2)
                dve.wait_ge(att_st, 16 * (count + 1))
                dve.scalar_tensor_tensor(out=att[:, :], in0=o_sum[:, :], scalar=float(D) ** -0.5, in1=den[:, :],
                                         op0=ALU.mult, op1=ALU.mult).then_inc(att_ready, 1)

            def one(it, n, start, last):
                count = NB * it + n
                if not last:
                    for j in range(MAXES):
                        find(count + 1, j)
                    dve.wait_ge(q_ld[n], (Q_LD + ROW_LD) * (it + 1))
                    finish(count + 1)
                if not start:
                    normalise(count - 1)

            blocks(dve, one)
            normalise(NB * ITERS - 1)

        @block.gpsimd
        def _(pool):
            def one(it, n, first, last):
                count = NB * it + n
                for p in range(PAIRS):
                    number = PAIRS * count + p
                    pool.wait_ge(exp_ready, 2 * HG * (number + 1))
                    if p >= 2 or not first:
                        pool.wait_ge(sums_ready, number - 1)
                    pool.tensor_tensor(pair[p % 2][:, :, :], probs[2 * p % NPROB][:, :, :], probs[(2 * p + 1) % NPROB][:, :, :],
                                       ALU.add).then_inc(pair_ready, 1)

            blocks(pool, one)


def project_stage(nc, sb, sem, psum, a, ident, wp, vec_dram, att_dram, z_dram, out):
    wt_hi, wt_lo = (sb(f"wp_{n}", [P, KT, D], F32R) for n in ("hi", "lo"))
    bp_row = sb("bp_row", [1, D])
    bp_parts = sb("bp_parts", [P, D], F32R)
    bp_ones = sb("bp_ones", [P, P], F32R)
    gain = [sb(f"gain{b}", [P, D]) for b in range(B)]
    shift = [sb(f"shift{b}", [P, D]) for b in range(B)]
    att = [sb(f"p_att{b}", [P, KT, CH]) for b in range(B)]
    att_hi, att_lo = ([sb(f"p_att_{n}{b}", [P, KT, CH], F32R) for b in range(B)] for n in ("hi", "lo"))
    z = [sb(f"p_z{b}", [P, TT, D]) for b in range(B)]
    h = [sb(f"p_h{b}", [P, TT, D]) for b in range(B)]
    shifted = [sb(f"p_shifted{b}", [P, TT, D]) for b in range(B)]
    norm = [sb(f"p_norm{b}", [P, TT, D]) for b in range(B)]
    result = [sb(f"p_result{b}", [P, TT, D]) for b in range(B)]
    stats = sb("p_stats", [P, TT, 6])
    root, mean2, var, diff, inv, off = (sb(f"p_{n}", [P, TT]) for n in ("root", "mean2", "var", "diff", "inv", "off"))

    row_ld, vec_ld = sem("p_row_ld"), sem("p_vec_ld")
    att_ld, z_ld, out_st = ([sem(f"p_{n}{b}") for b in range(B)] for n in ("att_ld", "z_ld", "out_st"))
    last_st = [sem(f"p_last_st{t}") for t in range(TT)]
    consts, wt_tp, whi_ready, wlo_ready = (sem(f"p_{n}") for n in ("consts", "wt_tp", "whi", "wlo"))
    ahi_ready, alo_ready, sum_ready, h_ready = (sem(f"p_{n}") for n in ("ahi", "alo", "sum", "h"))
    stat, root_ready, ln_chain = (sem(f"p_{n}") for n in ("stat", "root", "ln_chain"))
    shifted_ready, norm_ready, scaled_ready, result_ready = (sem(f"p_{n}") for n in ("shifted", "norm", "scaled", "result"))

    H_FREE = B * TT

    def chunk(dram, i, b):
        return dram[b].rearrange("(i t p) d -> i p t d", p=P, t=TT)[bass.ds(i, 1)].rearrange("o p t d -> (o p) t d")

    def steps(engine, step):
        step(0, 0, None, (0, 1))
        with engine.Fori(0, NCH - 1) as i:
            step(i, 1, (i, 0), (i + 1, 0))
            step(i + 1, 0, (i, 1), (i + 1, 1))
        step(NCH - 1, 1, (NCH - 1, 0), None)

    with nc.Block() as block:
        @block.sync
        def _(sp):
            def load(i, b):
                sp.dma_start(att[b][:, :, :], att_dram[:, bass.ds(b * L + i * CH, CH)].rearrange("(k p) t -> p k t", p=P)).then_inc(att_ld[b], 16)
                sp.dma_start(z[b][:, :, :], chunk(z_dram, i, b)).then_inc(z_ld[b], 16)

            def store(i, b):
                sp.wait_ge(result_ready, TT * (B * i + b + 1))
                sp.dma_start(chunk(out, i, b), result[b][:, :, :]).then_inc(out_st[b], 16)

            sp.dma_start(bp_row[:, :], a["L1_cond_bp"].rearrange("(o d) -> o d", o=1)).then_inc(row_ld, 16)
            for b in range(B):
                load(0, b)
            for b in range(B):
                sp.dma_start(gain[b][:, :], vec_dram[V_GAIN_1, b:b + 1, :].broadcast_to((P, D))).then_inc(vec_ld, 16)
                sp.dma_start(shift[b][:, :], vec_dram[V_SHIFT_1, b:b + 1, :].broadcast_to((P, D))).then_inc(vec_ld, 16)

            def step(i, b, previous, loads=True):
                if loads:
                    sp.wait_ge(h_ready, TT * (B * i + b + 1) + H_FREE)
                    load(i + 1, b)
                if previous:
                    store(*previous)

            step(0, 0, None)
            with sp.Fori(0, NCH - 2) as i:
                step(i, 1, (i, 0))
                step(i + 1, 0, (i, 1))
            step(NCH - 2, 1, (NCH - 2, 0))
            step(NCH - 1, 0, (NCH - 2, 1), False)
            step(NCH - 1, 1, (NCH - 1, 0), False)
            for t in range(TT):
                sp.wait_ge(result_ready, TT * (B * NCH - 1) + t + 1)
                sp.dma_start(out[B - 1, L - (TT - t) * P:L - (TT - t - 1) * P, :], result[B - 1][:, t, :]).then_inc(last_st[t], 16)
            for b in range(B):
                sp.wait_ge(out_st[b], 16 * (NCH + 1 - b))
            for t in range(TT):
                sp.wait_ge(last_st[t], 16)

        @block.tensor
        def _(pe):
            for k in range(KT):
                for m in range(KT):
                    mm = pe.transpose(psum[:, TT + k, m * P:(m + 1) * P], wp[:, m, k * P:(k + 1) * P], ident[:, :])
                mm.then_inc(wt_tp, 1)
            pe.wait_ge(consts, 6)
            pe.wait_ge(wlo_ready, KT)

            def step(i, b, previous, following):
                c = B * i + b
                pe.wait_ge(alo_ready, KT * (c + 1))
                pe.wait_ge(h_ready, TT * (c - 1) + H_FREE)
                for t in range(TT):
                    tok, out = slice(t * P, (t + 1) * P), psum[:, TT * b + t, :]
                    nc.tensor.matmul(out, bp_ones[:, :], bp_parts[:, :], start=True, stop=False)
                    for k in range(KT):
                        mm = split_matmuls(nc, out, att_hi[b][:, k, tok], att_lo[b][:, k, tok], wt_hi[:, k, :], wt_lo[:, k, :], False, k == KT - 1)
                    mm.then_inc(sum_ready, 1)

            steps(pe, step)

        @block.scalar
        def _(act):
            def split(i, b):
                c = B * i + b
                act.wait_ge(att_ld[b], 16 * (i + 1))
                wait_count(act, sum_ready, TT * (c - 1))
                for k in range(KT):
                    act.activation(att_hi[b][:, k, :], att[b][:, k, :], ACT.Copy).then_inc(ahi_ready, 1)

            def step(i, b, previous, following):
                c = B * i + b
                if following:
                    split(*following)
                act.wait_ge(stat, MOMENT_STEPS * (c + 1))
                act.activation(root[:, :], var[:, :], ACT.Sqrt).then_inc(root_ready, 1)
                act.wait_ge(ln_chain, INVERSE_STEPS * (c + 1))
                for t in range(TT):
                    act.activation(norm[b][:, t, :], h[b][:, t, :], ACT.Identity, scale=inv[:, t:t + 1], bias=off[:, t:t + 1]).then_inc(norm_ready, 1)

            for k in range(KT):
                act.wait_ge(wt_tp, k + 1)
                act.activation(wt_hi[:, k, :], psum[:, TT + k, :], ACT.Copy).then_inc(whi_ready, 1)
            split(0, 0)
            steps(act, step)

        @block.vector
        def _(dve):
            dve.sem_inc(h_ready, H_FREE)
            for b in range(B):
                dve.sem_inc(out_st[b], 16)
            dve.memset(bp_ones[:, :].bitcast(F32), 0.0).then_inc(consts, 1)
            dve.memset(bp_parts[:, :].bitcast(F32), 0.0).then_inc(consts, 1)
            dve.wait_ge(consts, 2)
            for r in (0, 32):
                dve.memset(bp_ones[r:r + 1, :].bitcast(F32), 1.0).then_inc(consts, 1)
            dve.wait_ge(row_ld, 16)
            dve.tensor_copy(bp_parts[0:1, :], bp_row[:, :]).then_inc(consts, 1)
            dve.wait_ge(consts, 5)
            dve.tensor_tensor(bp_parts[32:33, :], bp_row[:, :], bp_parts[0:1, :].bitcast(F32), ALU.subtract).then_inc(consts, 1)
            for k in range(KT):
                dve.wait_ge(whi_ready, k + 1)
                dve.tensor_tensor(wt_lo[:, k, :], psum[:, TT + k, :], wt_hi[:, k, :].bitcast(F32), ALU.subtract).then_inc(wlo_ready, 1)

            def scale(i, b):
                c = B * i + b
                for t in range(TT):
                    dve.wait_ge(norm_ready, TT * c + t + 1)
                    dve.tensor_tensor(norm[b][:, t, :], norm[b][:, t, :], gain[b][:, :], ALU.mult).then_inc(scaled_ready, 1)

            def finish(i, b):
                c = B * i + b
                dve.wait_ge(out_st[b], 16 * (i + 1))
                for t in range(TT):
                    dve.wait_ge(scaled_ready, TT * c + t + 1)
                    dve.wait_ge(shifted_ready, TT * c + t + 1)
                    dve.tensor_tensor(result[b][:, t, :], norm[b][:, t, :], shifted[b][:, t, :], ALU.add).then_inc(result_ready, 1)

            def step(i, b, previous, following):
                c = B * i + b
                dve.wait_ge(z_ld[b], 16 * (i + 1))
                for t in range(TT):
                    dve.wait_ge(sum_ready, TT * c + t + 1)
                    dve.tensor_tensor(h[b][:, t, :], psum[:, TT * b + t, :], z[b][:, t, :], ALU.add).then_inc(h_ready, 1)
                dve.wait_ge(h_ready, TT * (c + 1) + H_FREE)
                ln_moments(dve, h[b], stats, mean2, var, diff, stat, MOMENT_STEPS * c)
                if previous:
                    scale(*previous)
                dve.wait_ge(root_ready, c + 1)
                ln_inverse(dve, root, mean2, var, inv, off, ln_chain, INVERSE_STEPS * c)
                if previous:
                    finish(*previous)

            dve.wait_ge(vec_ld, 32 * B)
            steps(dve, step)
            scale(NCH - 1, 1)
            finish(NCH - 1, 1)

        @block.gpsimd
        def _(pool):
            def split(i, b):
                c = B * i + b
                for k in range(KT):
                    pool.wait_ge(ahi_ready, KT * c + k + 1)
                    pool.tensor_tensor(att_lo[b][:, k, :], att[b][:, k, :], att_hi[b][:, k, :].bitcast(F32), ALU.subtract).then_inc(alo_ready, 1)

            def step(i, b, previous, following):
                c = B * i + b
                if following:
                    split(*following)
                for t in range(TT):
                    pool.wait_ge(h_ready, TT * c + t + 1 + H_FREE)
                    pool.tensor_tensor(shifted[b][:, t, :], h[b][:, t, :], shift[b][:, :], ALU.add).then_inc(shifted_ready, 1)

            split(0, 0)
            pool.wait_ge(vec_ld, 32 * B)
            steps(pool, step)


def cond_seq_kernel(nc, a, out):
    with ExitStack() as whole:
        used = []

        def sem(name):
            used.append(nc.alloc_semaphore(name))
            return used[-1]

        def scope(stack):
            def sb(name, shape, dtype=F32):
                return stack.enter_context(nc.sbuf_tensor(name, list(shape), dtype))
            return sb

        psum = whole.enter_context(nc.psum_tensor("psum", [P, 8, CH], F32))
        sb = scope(whole)
        ident = sb("ident", [P, P])
        columns = sb("columns", [P, NVC, KT, B])
        raw_weight = sb("raw_weight", [P, KT, D])

        def scratch(name, shape, dtype=F32):
            return nc.dram_tensor(name, list(shape), dtype).ap()

        vec_dram = scratch("vec_rows", [NV, B, D])
        y_dram, z_dram = scratch("y_rows", [B, L, D]), scratch("z_rows", [B, L, D])
        q_dram, k_dram = scratch("q_parts", [2, D, B * L]), scratch("k_parts", [2, D, B * L])
        v_dram, att_dram = scratch("v_rows", [B * L, D]), scratch("att_columns", [D, B * L])

        with ExitStack() as weights:
            w1_stage = [raw_weight] + [scope(weights)(f"w1_stage{n}", [P, KT, D]) for n in (1, 2)]
            y_first = scope(weights)("y_first", [P, TT, D])
            with ExitStack() as state_space:
                own = scope(state_space)
                s5 = {n: own(f"s5_{n}", [P, CH]) for n in ("cos", "sin", "decay")}
                for part in ("hi", "lo"):
                    s5[f"b_{part}"] = own(f"s5_b_{part}", [P, KT, 2 * P], F32R)
                    s5[f"c_{part}"] = own(f"s5_c_{part}", [P, 2, D], F32R)
                    s5[f"d_{part}"] = own(f"s5_d_{part}", [P, KT, P], F32R)
                x = [own(f"x{b}", [P, TT, D]) for b in range(B)]
                with ExitStack() as stage:
                    prep_stage(nc, scope(stage), sem, psum, a, ident, columns, s5, x, w1_stage[1:], vec_dram)
                with ExitStack() as stage:
                    s5_stage(nc, scope(stage), sem, psum, a, ident, columns, s5, x, w1_stage, y_first, vec_dram, y_dram)
            with ExitStack() as stage:
                ffn_stage(nc, scope(stage), sem, psum, a, ident, columns, w1_stage, y_first, vec_dram, y_dram, z_dram)
        nc.clear_and_free_semaphores(used)
        nc.all_engine_barrier()
        with ExitStack() as block_0:
            own = scope(block_0)
            first = {"keys": own("keys0", [P, HG, L], F32R), "queries": own("queries0", [P, HG, CH], F32R),
                     "part_max": own("part_max", [P, HG * TT, NCH]), "maxima": own("maxima", [P, 32]),
                     "max_rows": own("max_rows", [P, 32]), "neg_rows": own("neg_rows", [P, 32], F32R)}
            with ExitStack() as stage:
                qkv_stage(nc, scope(stage), sem, psum, a, ident, columns, raw_weight, first, z_dram, q_dram, k_dram, v_dram)
            with ExitStack() as stage:
                attention_stage(nc, scope(stage), sem, psum, a, raw_weight, first, q_dram, k_dram, v_dram, att_dram)
        with ExitStack() as stage:
            project_stage(nc, scope(stage), sem, psum, a, ident, raw_weight, vec_dram, att_dram, z_dram, out)


_INS = ["x", "cond_1024"] + [f"L0_cond_{n}" for n in (
    "Wm", "bm", "Lam_re", "Lam_im", "B_re", "B_im", "C_re", "C_im", "D_diag", "log_step", "Wc", "bc", "W1", "b1", "W2", "b2")] + [
    f"L1_cond_{n}" for n in ("ln_g", "ln_b", "Wg", "bg", "Wb", "bb", "Wqkv", "bqkv", "Wp", "bp")]


def kernel(**inputs):
    import numpy as _np
    import concourse.bacc as _bacc
    from concourse import mybir as _mybir
    from concourse.bass_utils import run_bass_kernel_spmd as _run

    nc = _bacc.Bacc("TRN2", target_bir_lowering=False, num_devices=1)
    arrays, args = {}, {}
    for name in _INS:
        v = _np.ascontiguousarray(inputs[name])
        arrays[f"in_{name}_dram"] = v
        args[name] = nc.dram_tensor(f"in_{name}_dram", v.shape, _mybir.dt.from_np(v.dtype), kind="ExternalInput").ap()
    out = nc.dram_tensor("out_dram", (B, L, D), F32, kind="ExternalOutput").ap()
    cond_seq_kernel(nc, args, out)
    r = _run(nc, [arrays], core_ids=[0])
    return r.results[0]["out_dram"]
```
